# Optimizing a Trainium2 kernel written in Bass

```python
import numpy as np
import jax
import jax.numpy as jnp

def _softmax(x, axis=-1):
    return jax.nn.softmax(x, axis=axis)

def _gelu(x):
    return jax.nn.gelu(x, approximate=True)

def _silu(x):
    return jax.nn.silu(x)

def _sigmoid(x):
    return jax.nn.sigmoid(x)

def _layernorm(x, axis=-1, eps=1e-05):
    m = jnp.mean(x, axis=axis, keepdims=True)
    v = jnp.var(x, axis=axis, keepdims=True)
    return (x - m) / jnp.sqrt(v + eps)

def _scatter_add(tgt, idx, src, axis=0):
    return tgt.at[idx].add(src)

def _segment_sum(src, seg, n):
    return jax.ops.segment_sum(src, seg, n)
kernel_name = 'mk_conv_seq_d2_conv_nhwc384_r4_b78b17'

def setup_inputs(seed: int=0):
    np.random.seed(seed)
    _w = jnp.asarray

    def _rec_inputs():
        import jax
        import jax.numpy as jnp
        _gk = jax.random.key(seed)
        x = -0.0001476 + 0.9999 * jax.random.normal(jax.random.fold_in(_gk, 1), (32, 56, 56, 96), jnp.float32)
        return x
    x = _rec_inputs()

    def _L0_conv_setup():
        import jax, jax.numpy as jnp
        import numpy as np
        DIM = 96
        HEADS = 12
        HDIM = DIM // HEADS
        FEAT = (56, 56)
        WS = (7, 7)
        SS = (3, 3)
        L = WS[0] * WS[1]
        MLP_HID = 4 * DIM
        META_HID = 96
        EPS = 1e-05

        def _rel_coords_log():
            ch, cw = np.meshgrid(np.arange(WS[0]), np.arange(WS[1]), indexing='ij')
            coords = np.stack([ch, cw]).reshape(2, -1)
            rel = (coords[:, :, None] - coords[:, None, :]).transpose(1, 2, 0).reshape(-1, 2).astype(np.float32)
            return jnp.asarray(np.sign(rel) * np.log1p(np.abs(rel)))

        def _attn_mask():
            H, W = FEAT
            img = np.zeros((H, W))
            cnt = 0
            for hs in (slice(0, -WS[0]), slice(-WS[0], -SS[0]), slice(-SS[0], None)):
                for ws_ in (slice(0, -WS[1]), slice(-WS[1], -SS[1]), slice(-SS[1], None)):
                    img[hs, ws_] = cnt
                    cnt += 1
            mw = img.reshape(H // WS[0], WS[0], W // WS[1], WS[1]).transpose(0, 2, 1, 3).reshape(-1, L)
            am = mw[:, None, :] - mw[:, :, None]
            return jnp.asarray(np.where(am != 0, -100.0, 0.0).astype(np.float32))
        REL_LOG = _rel_coords_log()
        ATTN_MASK = _attn_mask()

        def _ln(x, g, b):
            mu = x.mean(-1, keepdims=True)
            var = ((x - mu) ** 2).mean(-1, keepdims=True)
            return (x - mu) * jax.lax.rsqrt(var + EPS) * g + b
        key = jax.random.key(seed)
        ks = jax.random.split(key, 16)
        s = 0.02
        return {'x': jax.random.normal(ks[0], (32, FEAT[0], FEAT[1], DIM), jnp.float32), 'qkv_w': jax.random.normal(ks[1], (DIM, 3 * DIM), jnp.float32) * s, 'qkv_b': jnp.zeros((3 * DIM,), jnp.float32), 'proj_w': jax.random.normal(ks[2], (DIM, DIM), jnp.float32) * s, 'proj_b': jnp.zeros((DIM,), jnp.float32), 'tau': jnp.ones((HEADS,), jnp.float32), 'meta_w1': jax.random.normal(ks[3], (2, META_HID), jnp.float32) * s, 'meta_b1': jnp.zeros((META_HID,), jnp.float32), 'meta_w2': jax.random.normal(ks[4], (META_HID, HEADS), jnp.float32) * s, 'meta_b2': jnp.zeros((HEADS,), jnp.float32), 'norm1_g': jnp.ones((DIM,), jnp.float32), 'norm1_b': jnp.zeros((DIM,), jnp.float32), 'fc1_w': jax.random.normal(ks[5], (DIM, MLP_HID), jnp.float32) * s, 'fc1_b': jnp.zeros((MLP_HID,), jnp.float32), 'fc2_w': jax.random.normal(ks[6], (MLP_HID, DIM), jnp.float32) * s, 'fc2_b': jnp.zeros((DIM,), jnp.float32), 'norm2_g': jnp.ones((DIM,), jnp.float32), 'norm2_b': jnp.zeros((DIM,), jnp.float32)}
    _L0_conv_all = _L0_conv_setup()
    _L0_conv_in = {k: v for k, v in _L0_conv_all.items() if k in ('qkv_w', 'qkv_b', 'proj_w', 'proj_b', 'tau', 'meta_w1', 'meta_b1', 'meta_w2', 'meta_b2', 'norm1_g', 'norm1_b', 'fc1_w', 'fc1_b', 'fc2_w', 'fc2_b', 'norm2_g', 'norm2_b')}
    del _L0_conv_all

    def _L1_conv_setup():
        import jax, jax.numpy as jnp
        import numpy as np
        DIM = 96
        DIM_OUT = 96
        HEADS = 6
        HEAD_DIM = DIM_OUT // HEADS
        WS = 8
        HIDDEN = int(DIM_OUT * 4.0)
        EPS = 1e-06

        def layernorm(x, gamma, beta):
            mu = jnp.mean(x, axis=-1, keepdims=True)
            var = jnp.var(x, axis=-1, keepdims=True)
            return (x - mu) * jax.lax.rsqrt(var + EPS) * gamma + beta

        def window_partition(x, ws):
            B, H, W, C = x.shape
            pad_h = (ws - H % ws) % ws
            pad_w = (ws - W % ws) % ws
            x = jnp.pad(x, ((0, 0), (0, pad_h), (0, pad_w), (0, 0)))
            Hp, Wp = (H + pad_h, W + pad_w)
            x = x.reshape(B, Hp // ws, ws, Wp // ws, ws, C)
            x = x.transpose(0, 1, 3, 2, 4, 5).reshape(-1, ws, ws, C)
            return (x, Hp, Wp)

        def window_unpartition(windows, ws, Hp, Wp, H, W):
            C = windows.shape[-1]
            x = windows.reshape(-1, Hp // ws, Wp // ws, ws, ws, C)
            x = x.transpose(0, 1, 3, 2, 4, 5).reshape(-1, Hp, Wp, C)
            return x[:, :H, :W, :]

        def attention(xw, w_qkv, b_qkv, w_proj, b_proj):
            Bw, h, w, _ = xw.shape
            N = h * w
            qkv = jnp.einsum('bhwc,cd->bhwd', xw, w_qkv) + b_qkv
            qkv = qkv.reshape(Bw, N, 3, HEADS, HEAD_DIM)
            q, k, v = (qkv[:, :, 0], qkv[:, :, 1], qkv[:, :, 2])
            q = q * (1.0 / jnp.sqrt(jnp.float32(HEAD_DIM)))
            attn = jnp.einsum('bnhd,bmhd->bhnm', q, k)
            attn = jax.nn.softmax(attn, axis=-1)
            out = jnp.einsum('bhnm,bmhd->bnhd', attn, v).reshape(Bw, h, w, DIM_OUT)
            return jnp.einsum('bhwc,cd->bhwd', out, w_proj) + b_proj
        key = jax.random.key(seed)
        ks = jax.random.split(key, 8)
        s = 0.02
        return {'x': jax.random.normal(ks[0], (16, 56, 56, DIM), dtype=jnp.float32), 'g1': jnp.ones((DIM,), jnp.float32), 'b1': jnp.zeros((DIM,), jnp.float32), 'w_qkv': jax.random.normal(ks[1], (DIM, 3 * DIM_OUT), jnp.float32) * s, 'b_qkv': jnp.zeros((3 * DIM_OUT,), jnp.float32), 'w_proj': jax.random.normal(ks[2], (DIM_OUT, DIM_OUT), jnp.float32) * s, 'b_proj': jnp.zeros((DIM_OUT,), jnp.float32), 'g2': jnp.ones((DIM_OUT,), jnp.float32), 'b2': jnp.zeros((DIM_OUT,), jnp.float32), 'w_fc1': jax.random.normal(ks[3], (DIM_OUT, HIDDEN), jnp.float32) * s, 'b_fc1': jnp.zeros((HIDDEN,), jnp.float32), 'w_fc2': jax.random.normal(ks[4], (HIDDEN, DIM_OUT), jnp.float32) * s, 'b_fc2': jnp.zeros((DIM_OUT,), jnp.float32)}
    _L1_conv_all = _L1_conv_setup()
    _L1_conv_in = {k: v for k, v in _L1_conv_all.items() if k in ('g1', 'b1', 'w_qkv', 'b_qkv', 'w_proj', 'b_proj', 'g2', 'b2', 'w_fc1', 'b_fc1', 'w_fc2', 'b_fc2')}
    del _L1_conv_all
    return {'x': x, 'L0_conv_qkv_w': _L0_conv_in['qkv_w'], 'L0_conv_qkv_b': _L0_conv_in['qkv_b'], 'L0_conv_proj_w': _L0_conv_in['proj_w'], 'L0_conv_proj_b': _L0_conv_in['proj_b'], 'L0_conv_tau': _L0_conv_in['tau'], 'L0_conv_meta_w1': _L0_conv_in['meta_w1'], 'L0_conv_meta_b1': _L0_conv_in['meta_b1'], 'L0_conv_meta_w2': _L0_conv_in['meta_w2'], 'L0_conv_meta_b2': _L0_conv_in['meta_b2'], 'L0_conv_norm1_g': _L0_conv_in['norm1_g'], 'L0_conv_norm1_b': _L0_conv_in['norm1_b'], 'L0_conv_fc1_w': _L0_conv_in['fc1_w'], 'L0_conv_fc1_b': _L0_conv_in['fc1_b'], 'L0_conv_fc2_w': _L0_conv_in['fc2_w'], 'L0_conv_fc2_b': _L0_conv_in['fc2_b'], 'L0_conv_norm2_g': _L0_conv_in['norm2_g'], 'L0_conv_norm2_b': _L0_conv_in['norm2_b'], 'L1_conv_g1': _L1_conv_in['g1'], 'L1_conv_b1': _L1_conv_in['b1'], 'L1_conv_w_qkv': _L1_conv_in['w_qkv'], 'L1_conv_b_qkv': _L1_conv_in['b_qkv'], 'L1_conv_w_proj': _L1_conv_in['w_proj'], 'L1_conv_b_proj': _L1_conv_in['b_proj'], 'L1_conv_g2': _L1_conv_in['g2'], 'L1_conv_b2': _L1_conv_in['b2'], 'L1_conv_w_fc1': _L1_conv_in['w_fc1'], 'L1_conv_b_fc1': _L1_conv_in['b_fc1'], 'L1_conv_w_fc2': _L1_conv_in['w_fc2'], 'L1_conv_b_fc2': _L1_conv_in['b_fc2']}

def reference(x, L0_conv_qkv_w, L0_conv_qkv_b, L0_conv_proj_w, L0_conv_proj_b, L0_conv_tau, L0_conv_meta_w1, L0_conv_meta_b1, L0_conv_meta_w2, L0_conv_meta_b2, L0_conv_norm1_g, L0_conv_norm1_b, L0_conv_fc1_w, L0_conv_fc1_b, L0_conv_fc2_w, L0_conv_fc2_b, L0_conv_norm2_g, L0_conv_norm2_b, L1_conv_g1, L1_conv_b1, L1_conv_w_qkv, L1_conv_b_qkv, L1_conv_w_proj, L1_conv_b_proj, L1_conv_g2, L1_conv_b2, L1_conv_w_fc1, L1_conv_b_fc1, L1_conv_w_fc2, L1_conv_b_fc2):
    import jax
    import jax.numpy as jnp

    def _L0_conv_ref(x, qkv_w, qkv_b, proj_w, proj_b, tau, meta_w1, meta_b1, meta_w2, meta_b2, norm1_g, norm1_b, fc1_w, fc1_b, fc2_w, fc2_b, norm2_g, norm2_b):
        import jax, jax.numpy as jnp
        import numpy as np
        DIM = 96
        HEADS = 12
        HDIM = DIM // HEADS
        FEAT = (56, 56)
        WS = (7, 7)
        SS = (3, 3)
        L = WS[0] * WS[1]
        MLP_HID = 4 * DIM
        META_HID = 96
        EPS = 1e-05

        def _rel_coords_log():
            ch, cw = np.meshgrid(np.arange(WS[0]), np.arange(WS[1]), indexing='ij')
            coords = np.stack([ch, cw]).reshape(2, -1)
            rel = (coords[:, :, None] - coords[:, None, :]).transpose(1, 2, 0).reshape(-1, 2).astype(np.float32)
            return jnp.asarray(np.sign(rel) * np.log1p(np.abs(rel)))

        def _attn_mask():
            H, W = FEAT
            img = np.zeros((H, W))
            cnt = 0
            for hs in (slice(0, -WS[0]), slice(-WS[0], -SS[0]), slice(-SS[0], None)):
                for ws_ in (slice(0, -WS[1]), slice(-WS[1], -SS[1]), slice(-SS[1], None)):
                    img[hs, ws_] = cnt
                    cnt += 1
            mw = img.reshape(H // WS[0], WS[0], W // WS[1], WS[1]).transpose(0, 2, 1, 3).reshape(-1, L)
            am = mw[:, None, :] - mw[:, :, None]
            return jnp.asarray(np.where(am != 0, -100.0, 0.0).astype(np.float32))
        REL_LOG = _rel_coords_log()
        ATTN_MASK = _attn_mask()

        def _ln(x, g, b):
            mu = x.mean(-1, keepdims=True)
            var = ((x - mu) ** 2).mean(-1, keepdims=True)
            return (x - mu) * jax.lax.rsqrt(var + EPS) * g + b
        B, H, W, C = x.shape
        shortcut = x
        xs = jnp.roll(x, (-SS[0], -SS[1]), axis=(1, 2))
        xw = xs.reshape(B, H // WS[0], WS[0], W // WS[1], WS[1], C)
        xw = xw.transpose(0, 1, 3, 2, 4, 5).reshape(-1, L, C)
        qkv = (xw @ qkv_w + qkv_b).reshape(-1, L, 3, HEADS, HDIM).transpose(2, 0, 3, 1, 4)
        q, k, v = (qkv[0], qkv[1], qkv[2])
        qn = jnp.linalg.norm(q, axis=-1, keepdims=True)
        kn = jnp.linalg.norm(k, axis=-1, keepdims=True)
        denom = qn * jnp.swapaxes(kn, -2, -1)
        attn = jnp.einsum('whqd,whkd->whqk', q, k) / jnp.clip(denom, 1e-06)
        attn = attn / jnp.clip(tau, 0.01)[None, :, None, None]
        bias = jax.nn.relu(REL_LOG @ meta_w1 + meta_b1) @ meta_w2 + meta_b2
        bias = bias.T.reshape(HEADS, L, L)
        attn = attn + bias[None]
        nW = ATTN_MASK.shape[0]
        attn = attn.reshape(B, nW, HEADS, L, L) + ATTN_MASK[None, :, None]
        attn = jax.nn.softmax(attn.reshape(-1, HEADS, L, L), axis=-1)
        out = jnp.einsum('whqk,whkd->whqd', attn, v)
        out = out.transpose(0, 2, 1, 3).reshape(-1, L, C)
        out = out @ proj_w + proj_b
        out = out.reshape(B, H // WS[0], W // WS[1], WS[0], WS[1], C)
        out = out.transpose(0, 1, 3, 2, 4, 5).reshape(B, H, W, C)
        out = jnp.roll(out, (SS[0], SS[1]), axis=(1, 2))
        x = shortcut + _ln(out, norm1_g, norm1_b)
        h = jax.nn.gelu(x @ fc1_w + fc1_b, approximate=False) @ fc2_w + fc2_b
        x = x + _ln(h, norm2_g, norm2_b)
        return x

    def _L1_conv_ref(x, g1, b1, w_qkv, b_qkv, w_proj, b_proj, g2, b2, w_fc1, b_fc1, w_fc2, b_fc2):
        import jax, jax.numpy as jnp
        import numpy as np
        DIM = 96
        DIM_OUT = 96
        HEADS = 6
        HEAD_DIM = DIM_OUT // HEADS
        WS = 8
        HIDDEN = int(DIM_OUT * 4.0)
        EPS = 1e-06

        def layernorm(x, gamma, beta):
            mu = jnp.mean(x, axis=-1, keepdims=True)
            var = jnp.var(x, axis=-1, keepdims=True)
            return (x - mu) * jax.lax.rsqrt(var + EPS) * gamma + beta

        def window_partition(x, ws):
            B, H, W, C = x.shape
            pad_h = (ws - H % ws) % ws
            pad_w = (ws - W % ws) % ws
            x = jnp.pad(x, ((0, 0), (0, pad_h), (0, pad_w), (0, 0)))
            Hp, Wp = (H + pad_h, W + pad_w)
            x = x.reshape(B, Hp // ws, ws, Wp // ws, ws, C)
            x = x.transpose(0, 1, 3, 2, 4, 5).reshape(-1, ws, ws, C)
            return (x, Hp, Wp)

        def window_unpartition(windows, ws, Hp, Wp, H, W):
            C = windows.shape[-1]
            x = windows.reshape(-1, Hp // ws, Wp // ws, ws, ws, C)
            x = x.transpose(0, 1, 3, 2, 4, 5).reshape(-1, Hp, Wp, C)
            return x[:, :H, :W, :]

        def attention(xw, w_qkv, b_qkv, w_proj, b_proj):
            Bw, h, w, _ = xw.shape
            N = h * w
            qkv = jnp.einsum('bhwc,cd->bhwd', xw, w_qkv) + b_qkv
            qkv = qkv.reshape(Bw, N, 3, HEADS, HEAD_DIM)
            q, k, v = (qkv[:, :, 0], qkv[:, :, 1], qkv[:, :, 2])
            q = q * (1.0 / jnp.sqrt(jnp.float32(HEAD_DIM)))
            attn = jnp.einsum('bnhd,bmhd->bhnm', q, k)
            attn = jax.nn.softmax(attn, axis=-1)
            out = jnp.einsum('bhnm,bmhd->bnhd', attn, v).reshape(Bw, h, w, DIM_OUT)
            return jnp.einsum('bhwc,cd->bhwd', out, w_proj) + b_proj
        B, H, W, _ = x.shape
        shortcut = x
        xn = layernorm(x, g1, b1)
        windows, Hp, Wp = window_partition(xn, WS)
        attn_out = attention(windows, w_qkv, b_qkv, w_proj, b_proj)
        attn_out = window_unpartition(attn_out, WS, Hp, Wp, H, W)
        x = shortcut + attn_out
        h = layernorm(x, g2, b2)
        h = jax.nn.gelu(jnp.einsum('bhwc,cd->bhwd', h, w_fc1) + b_fc1, approximate=False)
        h = jnp.einsum('bhwc,cd->bhwd', h, w_fc2) + b_fc2
        return x + h

    def _gn(v, G=32, eps=1e-05):
        B_, H_, W_, C_ = v.shape
        g = v.reshape(B_, H_, W_, G, C_ // G)
        m = jnp.mean(g, axis=(1, 2, 4), keepdims=True)
        s = jnp.var(g, axis=(1, 2, 4), keepdims=True)
        return ((g - m) / jnp.sqrt(s + eps)).reshape(v.shape)

    def _ln_c(v, eps=1e-06):
        m = jnp.mean(v, axis=-1, keepdims=True)
        s = jnp.var(v, axis=-1, keepdims=True)
        return (v - m) / jnp.sqrt(s + eps)

    def _ln_t(v, eps=1e-05):
        m = jnp.mean(v, axis=-1, keepdims=True)
        s = jnp.var(v, axis=-1, keepdims=True)
        return (v - m) / jnp.sqrt(s + eps)

    def _to_tokens(v):
        B_, H_, W_, C_ = v.shape
        return v.reshape(B_, H_ * W_, C_)

    def _from_tokens(t, like):
        return t.reshape(like.shape)
    x = _L0_conv_ref(x, L0_conv_qkv_w, L0_conv_qkv_b, L0_conv_proj_w, L0_conv_proj_b, L0_conv_tau, L0_conv_meta_w1, L0_conv_meta_b1, L0_conv_meta_w2, L0_conv_meta_b2, L0_conv_norm1_g, L0_conv_norm1_b, L0_conv_fc1_w, L0_conv_fc1_b, L0_conv_fc2_w, L0_conv_fc2_b, L0_conv_norm2_g, L0_conv_norm2_b)
    x = _L1_conv_ref(x, L1_conv_g1, L1_conv_b1, L1_conv_w_qkv, L1_conv_b_qkv, L1_conv_w_proj, L1_conv_b_proj, L1_conv_g2, L1_conv_b2, L1_conv_w_fc1, L1_conv_b_fc1, L1_conv_w_fc2, L1_conv_b_fc2)
    return x

_drawn_inputs = setup_inputs


def setup_inputs(seed=0):
    import zlib

    import numpy as np

    out = dict(_drawn_inputs(seed))
    spreads = {'L0_conv_qkv_b': (0.0, 0.1),
     'L0_conv_proj_b': (0.0, 0.1),
     'L0_conv_tau': (1.0, 0.6),
     'L0_conv_meta_b1': (0.0, 2.0),
     'L0_conv_meta_b2': (0.0, 2.0),
     'L0_conv_norm1_g': (1.0, 0.2),
     'L0_conv_norm1_b': (0.0, 0.1),
     'L0_conv_fc1_b': (0.0, 0.1),
     'L0_conv_fc2_b': (0.0, 0.1),
     'L0_conv_norm2_g': (1.0, 0.2),
     'L0_conv_norm2_b': (0.0, 0.1),
     'L1_conv_g1': (1.0, 0.6),
     'L1_conv_b1': (0.0, 0.8),
     'L1_conv_b_qkv': (0.0, 0.737),
     'L1_conv_b_proj': (0.0, 0.1),
     'L1_conv_g2': (1.0, 0.6),
     'L1_conv_b2': (0.0, 2.0),
     'L1_conv_b_fc1': (0.0, 0.578),
     'L1_conv_b_fc2': (0.0, 0.1)}
    factors = {'L0_conv_meta_w1': 64.0, 'L0_conv_meta_w2': 52.084, 'L1_conv_w_qkv': 2.814}
    for name, (base, spread) in spreads.items():
        noise = np.random.default_rng([zlib.crc32(name.encode()), seed]).standard_normal(out[name].shape)
        drawn = base * np.exp(spread * noise) if base else spread * noise
        out[name] = jnp.asarray(drawn.astype(out[name].dtype))
    for name, factor in factors.items():
        out[name] = (out[name] * factor).astype(out[name].dtype)
    return out
```

```python
from contextlib import ExitStack

import numpy as np
import concourse.bass as bass
from concourse import mybir

F32 = mybir.dt.float32
ALU = mybir.AluOpType
ACT = mybir.ActivationFunctionType
AX = mybir.AxisListType

IMAGES, SIDE, DIM, HIDDEN = 32, 56, 96, 384
PAIRS = 4
WINDOWS = 2 * PAIRS
HALF = 64
CHUNKS = HIDDEN // 128
BANDS = 3
BANK = 512
EXP_SET = "natural_log_exp_and_others"


class Swin:
    name, win, heads, shift, eps = "swin", 7, 12, 3, 1e-5
    groups = IMAGES * (SIDE // 7) * (SIDE // 7) // WINDOWS
    cosine = True
    score_banks = 2
    score_parts = [(0, 0, 4, 0, 0), (1, 0, 2, 0, 196), (1, 2, 2, 1, 0), (2, 0, 4, 1, 98)]


class Plain:
    name, win, heads, shift, eps = "plain", 8, 6, 0, 1e-6
    groups = IMAGES * (SIDE // 8) * (SIDE // 8) // WINDOWS
    cosine = False
    score_banks = 1
    score_parts = [(0, 0, 2, 0, 0), (1, 0, 2, 0, 128), (2, 0, 2, 0, 256)]


STEPS = {
    "setup_zeroed": "buffers cleared", "setup_loaded": "weights in SBUF", "setup_vector": "vector engine's set-up steps",
    "setup_products": "tensor engine's set-up steps", "setup_scalar": "scalar engine's set-up steps",
    "setup_hidden": "a part of the bias network's hidden layer is in PSUM",
    "x_loaded_even": "windows of an even group are in x_in", "x_loaded_odd": "windows of an odd group are in x_in",
    "x2_stored_even": "an even group's result is in DRAM", "x2_stored_odd": "an odd group's result is in DRAM",
    "stats": "partial moments of x_in", "moments": "mean and variance of x_in", "var_eps": "variance + epsilon",
    "rstd": "its power -1/2", "x_norm": "normalised input", "x_res": "input + constant row",
    "x_turned": "input is feature-major in psT", "xT": "... and in SBUF",
    "q_made": "queries in dense bank 0", "k_made": "keys in dense bank 1",
    "q_read": "dense bank 0 read", "k_read": "dense bank 1 read",
    "qk_sq": "squares of queries and keys", "norms_made": "squared norms in the dense banks",
    "sq_norm": "squared norms with their floor in SBUF", "log_norm": "their logarithm", "inv_norm": "1 / norm",
    "q_band": "queries, one copy to a band, other bands zero", "k_hat": "keys ready to be spread over heads",
    "k_heads": "keys spread over heads, for one pair", "v_made": "values in dense bank 0", "v_heads": "... and in SBUF",
    "scored0": "scores in their first bank", "scored1": "scores in their second bank",
    "score_read0": "first score bank read", "score_read1": "second score bank read",
    "top": "greatest score of each query and head", "shifted": "scores less their top",
    "prob": "exponentials", "total": "their sums", "inv_total": "1 / sum, for two pairs",
    "prob_turned": "exponentials turned in psP", "probT": "... and in SBUF",
    "mixed_made": "exponentials times values in psO", "mixed": "two pairs divided by their sums, in SBUF",
    "mixed_turned": "attention output feature-major in psT", "mixedT": "... and in SBUF",
    "proj_made": "projection in dense bank 0", "proj_read": "... and read",
    "y_sq": "squares of the projection", "y_var": "variance", "y_eps": "+ epsilon", "y_rstd": "power -1/2",
    "x1": "first residual", "x1_res": "x1 + constant row", "stats2": "partial moments of x1",
    "moments2": "mean and variance of x1", "var_eps2": "+ epsilon", "rstd2": "power -1/2", "x1_norm": "normalised x1",
    "x1_turned": "MLP input feature-major in psT", "x1T": "... and in SBUF",
    "fc1_made": "a chunk of the hidden layer in a dense bank", "hid": "GELU of a chunk in SBUF",
    "fc2_made": "MLP output in dense bank 1", "fc2_read": "... and read",
    "z_sq": "squares of the MLP output", "z_var": "variance", "z_eps": "+ epsilon", "z_rstd": "power -1/2",
    "z_ln": "normalised MLP output", "x2": "the block's result",
}


def bcast(ap, axis, count):
    dims = [list(d) for d in ap.ap]
    dims.insert(axis, [0, count])
    return bass.AP(ap.tensor, ap.offset, dims)


def count_for(group, index, per_group, groups):
    if isinstance(group, int):
        if group < 0:
            return 0
        if group >= groups:
            group, index = groups - 1, per_group - 1
    return group * per_group + (index + 1)


def before(group, slot, lag):
    while slot < lag:
        group, slot = group - 1, slot + PAIRS
    return group, slot - lag


def exists(group, groups):
    return not isinstance(group, int) or 0 <= group < groups


def run_groups(engine, groups, body):
    for g in range(-2, 4):
        body(g, g % 2)
    with engine.Fori(2, groups // 2 - 1) as m:
        body(2 * m, 0)
        body(2 * m + 1, 1)
    for g in range(groups - 2, groups + 2):
        body(g, g % 2)


def block_program(nc, cfg, src, dst, par, const, psum):
    win, heads, groups = cfg.win, cfg.heads, cfg.groups
    WIN = win * win
    NT = WINDOWS * WIN
    NTP = NT + 16
    D = DIM // heads
    J = 32 // D
    HP = heads // 2
    SC = heads * WIN
    cosine = cfg.cosine
    SB = cfg.score_banks
    SBC = SC // SB
    PAIR_COLS = 2 * WIN

    ctx = ExitStack()
    with ctx:
        def sb(name, shape):
            return ctx.enter_context(nc.sbuf_tensor(f"{cfg.name}_{name}", shape, F32))

        did = {name: ctx.enter_context(nc.semaphore(f"{cfg.name}_{name}")) for name in STEPS}
        if not cosine:
            did.update(q_read=did["q_band"], k_read=did["k_hat"], score_read0=did["shifted"],
                       proj_read=did["x1"], fc2_read=did["x2"])

        def upto(group, index=0, per=1):
            return count_for(group, index, per, groups)

        psS = psum["scores"]
        psP = psum["probs"]
        psT = psum["turn"]
        psM = psum["dense"]
        psO = psum["mixed"]

        ident = sb("ident", [128, 128])
        w_qkv = sb("w_qkv", [128, 3 * DIM])
        b_qk = sb("b_qk", [DIM, 2])
        w_proj = sb("w_proj", [DIM + 1, DIM])
        w_fc1 = sb("w_fc1", [DIM, HIDDEN])
        b_fc1 = sb("b_fc1", [128, CHUNKS])
        w_fc2 = sb("w_fc2", [128, CHUNKS, DIM])
        row_fc2 = sb("row_fc2", [128, DIM])
        head_mask = sb("head_mask", [DIM, J])
        mean_row = sb("mean_row", [128, 8])
        res_row1 = sb("res_row1", [128, DIM])
        scr = sb("scr", [128, 128])
        half_power = sb("half_power", [128, PAIRS])
        epsilon = sb("epsilon", [128, PAIRS])
        if cosine:
            same_head = sb("same_head", [DIM, DIM])
            gain1 = sb("gain1", [128, DIM])
            gain2 = sb("gain2", [128, DIM])
            res_row2 = sb("res_row2", [128, DIM])
            bias_tab = sb("bias_tab", [128, 2, 2, SC])
            pick = sb("pick", [heads, DIM])
            tau = sb("tau", [heads, 1])
        else:
            norm_par = sb("norm_par", [DIM, 4])
            b_v = sb("b_v", [DIM, 1])

        x_in = sb("x_in", [128, 2, PAIRS, DIM])
        x_res = sb("x_res", [128, 2, PAIRS, DIM])
        xT = sb("xT", [128, NTP])
        q_band = sb("q_band", [128, 2, BANDS, NTP])
        k_hat = sb("k_hat", [DIM, NT])
        k_heads = sb("k_heads", [128, 2, WINDOWS, J * WIN])
        v_heads = sb("v_heads", [128, 2, PAIRS, HP, 2, 2, D])
        score = sb("score", [128, 2, SC])
        top = sb("top", [128, 2, heads])
        prob = sb("prob", [128, 2, heads, HALF])
        probT = sb("probT", [128, 2, HP * 128])
        total = sb("total", [128, PAIRS, heads])
        inv_total = sb("inv_total", [128, PAIRS, heads])
        mixed = sb("mixed", [128, PAIRS, DIM])
        mixedT = sb("mixedT", [DIM + 1, NTP])
        x1 = sb("x1", [128, PAIRS, DIM])
        x1_res = sb("x1_res", [128, 2, PAIRS, DIM])
        x1T = sb("x1T", [DIM, NT])
        hid = sb("hid", [128, CHUNKS, NTP])
        x2 = sb("x2", [128, 2, PAIRS, DIM])
        if cosine:
            qk = sb("qk", [DIM, 2, NT])
            qk_sq = sb("qk_sq", [DIM, 2, NT])
            sq_norm = sb("sq_norm", [DIM, 2, NT])
            y_sq = sb("y_sq", [128, PAIRS, DIM])
            y_var = sb("y_var", [128, PAIRS])
            y_eps = sb("y_eps", [128, PAIRS])
            y_rstd = sb("y_rstd", [128, PAIRS])
            y_ln = sb("y_ln", [128, PAIRS, DIM])
            z = sb("z", [128, PAIRS, DIM])
            z_sq = sb("z_sq", [128, PAIRS, DIM])
            z_var = sb("z_var", [128, PAIRS])
            z_eps = sb("z_eps", [128, PAIRS])
            z_rstd = sb("z_rstd", [128, PAIRS])
            z_ln = sb("z_ln", [128, PAIRS, DIM])
        else:
            stats = sb("stats", [128, PAIRS, 6])
            moments = sb("moments", [128, PAIRS, 2])
            var_eps = sb("var_eps", [128, PAIRS])
            rstd = sb("rstd", [128, PAIRS])
            x_norm = sb("x_norm", [128, PAIRS, DIM])
            stats2 = sb("stats2", [128, PAIRS, 6])
            moments2 = sb("moments2", [128, PAIRS, 2])
            var_eps2 = sb("var_eps2", [128, PAIRS])
            rstd2 = sb("rstd2", [128, PAIRS])
            x1_norm = sb("x1_norm", [128, PAIRS, DIM])

        def windows_of(ap, width):
            return ap.rearrange("p (w t) -> p w t", t=HALF)[:, :, 0:width]

        setup = ExitStack()
        with setup:
            if cosine:
                hidden = setup.enter_context(nc.sbuf_tensor("meta_hidden", [DIM, 2, WIN * WIN], F32))
                rel = setup.enter_context(nc.sbuf_tensor("meta_rel", [2, 2, WIN * WIN], F32))
                meta_w1 = setup.enter_context(nc.sbuf_tensor("meta_w1", [2, DIM], F32))
                meta_b1 = setup.enter_context(nc.sbuf_tensor("meta_b1", [DIM, 1], F32))
                meta_w2 = setup.enter_context(nc.sbuf_tensor("meta_w2", [DIM, heads], F32))
                meta_b2 = setup.enter_context(nc.sbuf_tensor("meta_b2", [128, heads], F32))
                mask = setup.enter_context(nc.sbuf_tensor("mask", [128, 2, 2, WIN], F32))
                b_v = setup.enter_context(nc.sbuf_tensor("b_v", [DIM, 1], F32))
            b_proj = setup.enter_context(nc.sbuf_tensor(f"{cfg.name}_b_proj", [128, DIM], F32))
            s_zero = did["setup_zeroed"]
            s_par = did["setup_loaded"]
            s_vec = did["setup_vector"]
            s_mul = did["setup_products"]
            s_act = did["setup_scalar"]
            loads = []

            def column(a):
                return a.rearrange("(c o) -> c o", o=1)

            def every_row(a, n):
                return a.rearrange("(o c) -> o c", o=1).broadcast_to([128, n])

            loads += [(ident[:, :], const["ident"]), (w_fc1[:, :], par["fc1_w"]),
                      (w_fc2[:, :, :], par["fc2_w"].rearrange("(c p) n -> p c n", p=128)),
                      (w_qkv[0:DIM, :], par["qkv_w"]), (w_proj[0:DIM, :], par["proj_w"]),
                      (b_qk[:, :], par["qkv_b"][0:2 * DIM].rearrange("(t c) -> c t", t=2)),
                      (b_v[:, :], column(par["qkv_b"][2 * DIM:3 * DIM])),
                      (b_fc1[:, :], par["fc1_b"].rearrange("(c p) -> p c", p=128)),
                      (row_fc2[:, :], every_row(par["fc2_b"], DIM)),
                      (head_mask[:, :], const[f"{cfg.name}_head_mask"])]
            if cosine:
                loads += [(same_head[:, :], const["same_head"]), (pick[:, :], const["pick"]),
                          (tau[:, :], column(par["tau"])),
                          (gain1[:, :], every_row(par["norm1_g"], DIM)),
                          (res_row1[:, :], every_row(par["norm1_b"], DIM)),
                          (gain2[:, :], every_row(par["norm2_g"], DIM)),
                          (res_row2[:, :], every_row(par["norm2_b"], DIM)),
                          (b_proj[DIM:DIM + 1, :], par["proj_b"].rearrange("(o c) -> o c", o=1)),
                          (rel[:, :, :], const["rel"]), (meta_w1[:, :], par["meta_w1"]),
                          (meta_b1[:, :], column(par["meta_b1"])), (meta_w2[:, :], par["meta_w2"]),
                          (meta_b2[:, :], every_row(par["meta_b2"], heads)),
                          (mask[:, :, :, :], const["mask"])]
            else:
                loads += [(norm_par[:, n:n + 1], column(par[k])) for n, k in enumerate(["g1", "b1", "g2", "b2"])]
                loads += [(b_proj[:, :], every_row(par["proj_b"], DIM))]

            with nc.Block() as block:
                @block.sync
                def _(sp):
                    sp.wait_ge(s_zero, 1)
                    for to, frm in loads:
                        sp.dma_start(to, frm, allow_slow_non_contiguous=True).then_inc(s_par, 16)

                @block.gpsimd
                def _(pool):
                    nc.gpsimd.memset(w_qkv[:, :], 0.0).then_inc(s_zero, 1)
                    for buf in (xT, hid, q_band, k_heads, v_heads, prob, probT, x_in, mixedT):
                        nc.gpsimd.memset(buf[:], 0.0)
                    if cosine:
                        nc.gpsimd.memset(bias_tab[:], 0.0)
                    nc.gpsimd.memset(epsilon[:], cfg.eps)
                    nc.gpsimd.memset(half_power[:], -0.5).then_inc(s_zero, 1)

                @block.vector
                def _(dve):
                    steps = [0]

                    def step(ins):
                        steps[0] += 1
                        ins.then_inc(s_vec, 1)
                        dve.wait_ge(s_vec, steps[0])

                    def centre(w, rows, slot):
                        step(nc.vector.reduce_sum(mean_row[0:rows, slot:slot + 1], w, axis=AX.X))
                        step(nc.vector.tensor_scalar(mean_row[0:rows, slot:slot + 1],
                                                     mean_row[0:rows, slot:slot + 1], 1.0 / DIM, None, ALU.mult))
                        step(nc.vector.tensor_scalar(w, w, mean_row[0:rows, slot:slot + 1], None, ALU.subtract))

                    dve.wait_ge(s_par, 16 * len(loads))
                    dve.wait_ge(s_zero, 2)
                    if cosine:
                        step(nc.vector.memset(mixedT[DIM:DIM + 1, :], 1.0))
                        dve.wait_ge(s_mul, 1)
                        step(nc.vector.tensor_tensor(w_proj[DIM:DIM + 1, :], psT[DIM:DIM + 1, 0:DIM],
                                                     b_proj[DIM:DIM + 1, :], ALU.add))
                        centre(w_proj[:, :], DIM + 1, 0)
                        for c in range(CHUNKS):
                            centre(w_fc2[:, c, :], 128, 1 + c)
                        centre(row_fc2[:, :], 128, 4)
                        dve.wait_ge(s_mul, 2)
                        step(nc.vector.tensor_scalar(scr[0:DIM, 0:1], psM[0:DIM, 0, 0:1], 0.01, None, ALU.max))
                        step(nc.vector.reciprocal(scr[0:DIM, 0:1], scr[0:DIM, 0:1]))
                        step(nc.vector.tensor_scalar(head_mask[:, :], head_mask[:, :], scr[0:DIM, 0:1], None, ALU.mult))
                        for order in range(2):
                            dve.wait_ge(s_mul, 2 + 2 * order + 2)
                            for part, (k0, k1) in enumerate([(0, 42), (42, WIN)]):
                                for r in (0, HALF):
                                    rows = slice(r, r + WIN)
                                    out = bias_tab[rows, order, 0, :].rearrange("p (h k) -> p h k", k=WIN)[:, :, k0:k1]
                                    got = psS[rows, part, 0:(k1 - k0) * heads].rearrange("p (k h) -> p h k", h=heads)
                                    step(nc.vector.tensor_tensor(out, got, bcast(meta_b2[rows, :], 2, k1 - k0), ALU.add))
                            for edge in (1, 0):
                                out = bias_tab[:, order, edge, :].rearrange("p (h k) -> p h k", k=WIN)
                                base = bias_tab[:, order, 0, :].rearrange("p (h k) -> p h k", k=WIN)
                                step(nc.vector.tensor_tensor(out, base, bcast(mask[:, order, edge, :], 1, heads), ALU.add))
                    else:
                        dve.wait_ge(s_mul, 1)
                        step(nc.vector.tensor_tensor(b_qk[:, :], b_qk[:, :], psT[0:DIM, 0:2], ALU.add))
                        step(nc.vector.tensor_scalar(b_qk[:, 0:1], b_qk[:, 0:1], D ** -0.5, None, ALU.mult))
                        step(nc.vector.tensor_tensor(b_v[:, :], b_v[:, :], psT[0:DIM, 2:3], ALU.add))
                        step(nc.vector.tensor_tensor(b_fc1[:, :], b_fc1[:, :], psT[:, 3:3 + CHUNKS], ALU.add))
                        step(nc.vector.tensor_scalar(w_qkv[0:DIM, :], w_qkv[0:DIM, :], norm_par[:, 0:1], None, ALU.mult))
                        step(nc.vector.tensor_scalar(w_qkv[0:DIM, 0:DIM], w_qkv[0:DIM, 0:DIM], D ** -0.5, None, ALU.mult))
                        step(nc.vector.tensor_scalar(w_fc1[:, :], w_fc1[:, :], norm_par[:, 2:3], None, ALU.mult))
                        step(nc.vector.tensor_copy(scr[0:DIM, 0:128], bcast(b_v[:, 0:1], 1, 128)[:, :, 0]))
                        dve.wait_ge(s_mul, 2)
                        step(nc.vector.tensor_tensor(res_row1[:, :], psM[:, 0, 0:DIM], b_proj[:, :], ALU.add))

                @block.tensor
                def _(pe):
                    pe.wait_ge(s_par, 16 * len(loads))
                    if cosine:
                        nc.tensor.matmul(psT[DIM:DIM + 1, 0:DIM], b_v[:, :], w_proj[0:DIM, :],
                                         start=True, stop=True).then_inc(s_mul, 1)
                        nc.tensor.matmul(psM[0:DIM, 0, 0:1], pick[:, :], tau[:, :],
                                         start=True, stop=True).then_inc(s_mul, 1)
                        for order in range(2):
                            cols = WIN * WIN
                            starts = list(range(0, cols, 480))
                            for n, a in enumerate(starts):
                                b = min(a + 480, cols)
                                if n or order:
                                    pe.wait_ge(s_act, n + order * len(starts))
                                last = nc.tensor.matmul(psM[0:DIM, 1, 0:b - a], meta_w1[:, :], rel[:, order, a:b],
                                                        start=True, stop=True)
                                last.then_inc(did["setup_hidden"], 1)
                            pe.wait_ge(s_act, (order + 1) * len(starts))
                            if order:
                                pe.wait_ge(s_vec, 1 + 1 + 3 * 5 + 3 + 6)
                            for half in (0, HALF):
                                for k in range(WIN):
                                    part, col = (0, k) if k < 42 else (1, k - 42)
                                    keyed = hidden[:, order, :].rearrange("c (q k) -> c q k", k=WIN)[:, :, k]
                                    last = nc.tensor.matmul(psS[half:half + WIN, part, col * heads:(col + 1) * heads],
                                                            keyed, meta_w2[:, :], start=True, stop=True)
                                last.then_inc(s_mul, 1)
                    else:
                        pe.wait_ge(s_zero, 1)
                        for n in range(3):
                            nc.tensor.matmul(psT[0:DIM, n:n + 1], w_qkv[0:DIM, n * DIM:(n + 1) * DIM], norm_par[:, 1:2],
                                             start=True, stop=True)
                        for c in range(CHUNKS):
                            last = nc.tensor.matmul(psT[:, 3 + c:4 + c], w_fc1[:, c * 128:(c + 1) * 128],
                                                    norm_par[:, 3:4], start=True, stop=True)
                        last.then_inc(s_mul, 1)
                        pe.wait_ge(s_vec, 8)
                        nc.tensor.matmul(psM[:, 0, 0:DIM], scr[0:DIM, 0:128], w_proj[0:DIM, :],
                                         start=True, stop=True).then_inc(s_mul, 1)

                if cosine:
                    @block.scalar
                    def _(act):
                        act.wait_ge(s_par, 16 * len(loads))
                        done = 0
                        for order in range(2):
                            cols = WIN * WIN
                            for a in range(0, cols, 480):
                                b = min(a + 480, cols)
                                done += 1
                                act.wait_ge(did["setup_hidden"], done)
                                nc.scalar.activation(hidden[:, order, a:b], psM[0:DIM, 1, 0:b - a], ACT.Relu,
                                                     bias=meta_b1[:, :]).then_inc(s_act, 1)

        def dma_total(parity, upto):
            per = 16 * (WINDOWS + 1 if cosine else PAIRS)
            if not cosine:
                return upto * per
            if parity == 0:
                return upto * per
            return upto * per + (upto // 4) * 16 * 19

        def swin_windows(image, wy, tile, move):
            rows = bass.ds(image * SIDE + cfg.shift + win * wy, win) if wy < 7 else None
            for p in range(PAIRS):
                for half in range(2):
                    at = half * HALF
                    col = cfg.shift + win * (2 * p + half)
                    spans = [(col, 0, win)] if col + win <= SIDE else [(col, 0, SIDE - col), (0, SIDE - col, win)]
                    if wy < 7:
                        for c0, a, b in spans:
                            move(tile[at + a * win:at + b * win, p, :],
                                 rows, slice(c0, c0 + b - a), "y x c -> x y c")
                    else:
                        low = cfg.shift + win * 7
                        for r0, ya, yb in [(low, 0, SIDE - low), (0, SIDE - low, win)]:
                            if len(spans) == 1:
                                move(tile[at + ya * win:at + yb * win, p, :],
                                     bass.ds(image * SIDE + r0, yb - ya), slice(col, col + win), "y x c -> y x c")
                            else:
                                for y in range(ya, yb):
                                    for c0, a, b in spans:
                                        move(tile[at + y * win + a:at + y * win + b, p, :],
                                             bass.ds(image * SIDE + r0 + y - ya, 1), slice(c0, c0 + b - a),
                                             "y x c -> (y x) c")

        with nc.Block() as block:
            s_load = [did["x_loaded_even"], did["x_loaded_odd"]]
            s_store = [did["x2_stored_even"], did["x2_stored_odd"]]

            @block.sync
            def _(sp):
                src_rows = src.rearrange("b h w c -> (b h) w c")
                dst_rows = dst.rearrange("b h w c -> (b h) w c")

                def may_load(n):
                    sp.wait_ge(did["x_res"], upto(n - 2))
                    sp.wait_ge(did["x_turned" if cosine else "x_norm"], upto(n - 2))

                if cosine:
                    def load(image, wy):
                        may_load(image * 8 + wy)
                        swin_windows(image, wy, x_in[:, wy % 2], lambda tile, rows, cols, order:
                                     sp.dma_start(tile, src_rows[rows, cols, :].rearrange(order))
                                     .then_inc(s_load[wy % 2], 16))

                    def store(image, wy):
                        sp.wait_ge(did["x2"], upto(image * 8 + wy))
                        swin_windows(image, wy, x2[:, wy % 2], lambda tile, rows, cols, order:
                                     sp.dma_start(dst_rows[rows, cols, :].rearrange(order), tile)
                                     .then_inc(s_store[wy % 2], 16))

                    for wy in range(8):
                        load(0, wy)
                        if wy >= 4:
                            store(0, wy - 4)
                    with sp.Fori(1, IMAGES) as image:
                        for wy in range(8):
                            load(image, wy)
                            if wy >= 4:
                                store(image, wy - 4)
                            else:
                                store(image - 1, wy + 4)
                    for wy in range(4, 8):
                        store(IMAGES - 1, wy)
                else:
                    def place(n, p):
                        pair = n * PAIRS + p
                        return bass.ds((pair // 7) * 2 * win, 2 * win), bass.ds((pair % 7) * win, win)

                    def load(n, parity):
                        may_load(n)
                        for p in range(PAIRS):
                            rows, cols = place(n, p)
                            sp.dma_start(x_in[:, parity, p, :], src_rows[rows, cols, :]).then_inc(s_load[parity], 16)

                    def store(n, parity):
                        sp.wait_ge(did["x2"], upto(n))
                        for p in range(PAIRS):
                            rows, cols = place(n, p)
                            sp.dma_start(dst_rows[rows, cols, :], x2[:, parity, p, :]).then_inc(s_store[parity], 16)

                    for n in range(4):
                        load(n, n % 2)
                    with sp.Fori(2, groups // 2) as m:
                        for k in range(2):
                            load(2 * m + k, k)
                            store(2 * m + k - 4, k)
                    for n in range(groups - 4, groups):
                        store(n, n % 2)
                for parity in range(2):
                    sp.wait_ge(s_store[parity], dma_total(parity, groups // 2))

            def moved(g, parity):
                return 0 if isinstance(g, int) and g < 0 else dma_total(parity, g // 2 + 1)

            @block.tensor
            def _(pe):
                def body(g, parity):
                    front, back, mlp = g + 1, g - 1, g - 2
                    other = 1 - parity
                    for slot in range(PAIRS):
                        if exists(g, groups):
                            pe.wait_ge(did["q_band"], upto(g))
                            pe.wait_ge(did["k_heads"], upto(g, slot, PAIRS))
                            ug, us = before(g, slot, 1 if SB == 2 else 2)
                            for bank in range(SB):
                                pe.wait_ge(did[f"score_read{bank}"], upto(ug, us, PAIRS))
                                for band, j0, nj, at_bank, col in cfg.score_parts:
                                    if at_bank != bank:
                                        continue
                                    for half in range(2):
                                        w = 2 * slot + half
                                        last = nc.tensor.matmul(
                                            psS[half * HALF:half * HALF + HALF, bank if SB == 2 else slot % 2,
                                                col:col + nj * WIN],
                                            q_band[:, parity, band, w * WIN:w * WIN + HALF],
                                            k_heads[:, parity, w, j0 * WIN:(j0 + nj) * WIN], start=True, stop=True)
                                last.then_inc(did[f"scored{bank}"], 1)
                        if slot == 0:
                            if exists(front, groups):
                                if cosine:
                                    pe.wait_ge(s_load[other], moved(front, other))
                                else:
                                    pe.wait_ge(did["x_norm"], upto(front))
                                pe.wait_ge(did["mixedT"], upto(g - 2))
                                pe.wait_ge(did["x1T"], upto(g - 3))
                                for p in range(PAIRS):
                                    rows = x_in[:, other, p, :] if cosine else x_norm[:, p, :]
                                    last = nc.tensor.transpose(psT[0:DIM, p * 128:(p + 1) * 128], rows, ident[:, :])
                                last.then_inc(did["x_turned"], 1)
                            if exists(mlp, groups):
                                pe.wait_ge(did["x1" if cosine else "x1_norm"], upto(mlp))
                                pe.wait_ge(did["xT"], upto(front))
                                pe.wait_ge(did["mixedT"], upto(mlp))
                                for p in range(PAIRS):
                                    rows = x1[:, p, :] if cosine else x1_norm[:, p, :]
                                    last = nc.tensor.transpose(psT[0:DIM, p * 128:(p + 1) * 128], rows, ident[:, :])
                                last.then_inc(did["x1_turned"], 1)
                            if exists(front, groups):
                                pe.wait_ge(did["xT"], upto(front))
                                pe.wait_ge(did["proj_read"], upto(mlp))
                                pe.wait_ge(did["v_heads"], upto(g))
                                nc.tensor.matmul(psM[0:DIM, 0, 0:NT], w_qkv[0:DIM, 0:DIM], xT[0:DIM, 0:NT],
                                                 start=True, stop=True).then_inc(did["q_made"], 1)
                                pe.wait_ge(did["fc2_read"], upto(g - 3))
                                pe.wait_ge(did["sq_norm" if cosine else "k_hat"], upto(g))
                                nc.tensor.matmul(psM[0:DIM, 1, 0:NT], w_qkv[0:DIM, DIM:2 * DIM], xT[0:DIM, 0:NT],
                                                 start=True, stop=True).then_inc(did["k_made"], 1)
                            if exists(mlp, groups):
                                pe.wait_ge(did["x1T"], upto(mlp))
                                pe.wait_ge(did["q_read"], upto(front))
                                pe.wait_ge(did["proj_read"], upto(mlp))
                                for c in range(CHUNKS):
                                    if c == 1:
                                        pe.wait_ge(did["k_read"], upto(front))
                                        pe.wait_ge(did["fc2_read"], upto(g - 3))
                                    if c == 2:
                                        pe.wait_ge(did["hid"], upto(mlp, 0, CHUNKS))
                                    nc.tensor.matmul(psM[:, c % 2, 0:NT], w_fc1[:, c * 128:(c + 1) * 128], x1T[:, :],
                                                     start=True, stop=True).then_inc(did["fc1_made"], 1)
                        if slot == 1:
                            if exists(front, groups):
                                if cosine:
                                    pe.wait_ge(did["qk_sq"], upto(front))
                                    pe.wait_ge(did["q_read"], upto(front))
                                    pe.wait_ge(did["k_read"], upto(front))
                                    for n in range(2):
                                        pe.wait_ge(did["hid"], upto(mlp, 2 if n == 0 else 1, CHUNKS))
                                        last = nc.tensor.matmul(psM[0:DIM, n, 0:NT], same_head[:, :], qk_sq[:, n, :],
                                                                start=True, stop=True)
                                    last.then_inc(did["norms_made"], 1)
                                pe.wait_ge(did["sq_norm" if cosine else "q_read"], upto(front))
                                pe.wait_ge(did["hid"], upto(mlp, 2, CHUNKS))
                                for w in range(WINDOWS):
                                    for odd in range(2):
                                        cols = w_qkv[:, 2 * DIM:3 * DIM].rearrange("c (h o d) -> c h o d", o=2, d=D)[:, :, odd, :]
                                        out = psM[odd * HALF:(odd + 1) * HALF, 0, 0:WINDOWS * HP * D]\
                                            .rearrange("r (p h v d) -> r p h v d", p=PAIRS, h=HP, v=2)[:, w // 2, :, w % 2, :]
                                        last = nc.tensor.matmul(out, xT[:, w * WIN:w * WIN + HALF], cols,
                                                                start=True, stop=True)
                                last.then_inc(did["v_made"], 1)
                            if exists(mlp, groups):
                                pe.wait_ge(did["hid"], upto(mlp, 2, CHUNKS))
                                pe.wait_ge(did["sq_norm" if cosine else "k_read"], upto(front))
                                for p in range(PAIRS):
                                    for c in range(CHUNKS):
                                        for half in range(2):
                                            first = (2 * p + half) * WIN
                                            last = nc.tensor.matmul(
                                                psM[half * HALF:(half + 1) * HALF, 1, p * DIM:(p + 1) * DIM],
                                                hid[:, c, first:first + HALF],
                                                w_fc2[:, c, :], start=(c == 0), stop=(c == CHUNKS - 1))
                                last.then_inc(did["fc2_made"], 1)
                        if slot == 2 and exists(back, groups):
                            pe.wait_ge(did["mixed"], upto(back, 1, 2))
                            pe.wait_ge(did["x1T"], upto(mlp))
                            pe.wait_ge(did["xT"], upto(front))
                            for p in range(PAIRS):
                                last = nc.tensor.transpose(psT[0:DIM, p * 128:(p + 1) * 128], mixed[:, p, :], ident[:, :])
                            last.then_inc(did["mixed_turned"], 1)
                            pe.wait_ge(did["mixedT"], upto(back))
                            pe.wait_ge(did["v_heads"], upto(front))
                            pe.wait_ge(did["hid"], upto(mlp, 2, CHUNKS))
                            rows = DIM + 1 if cosine else DIM
                            for p in range(PAIRS):
                                for half in range(2):
                                    first = (2 * p + half) * WIN
                                    last = nc.tensor.matmul(psM[half * HALF:(half + 1) * HALF, 0, p * DIM:(p + 1) * DIM],
                                                            mixedT[0:rows, first:first + HALF],
                                                            w_proj[0:rows, :], start=True, stop=True)
                            last.then_inc(did["proj_made"], 1)
                        ag, as_ = before(g, slot, 2)
                        if exists(ag, groups):
                            pe.wait_ge(did["v_heads"], upto(ag))
                            pe.wait_ge(did["probT"], upto(ag, as_, PAIRS))
                            if as_ % 2 == 0:
                                mg, ms = before(ag, as_, 2)
                                pe.wait_ge(did["mixed"], upto(mg, ms // 2, 2))
                            apar = parity if slot >= 2 else other
                            for hp in range(HP):
                                last = nc.tensor.matmul(
                                    psO[:, (as_ % 2) * 2 * DIM:(as_ % 2 + 1) * 2 * DIM]
                                    .rearrange("r (h n) -> r h n", h=HP)[:, hp, :],
                                    probT[:, as_ % 2, hp * 128:(hp + 1) * 128],
                                    v_heads[:, apar, as_, hp].rearrange("r v o d -> r (v o d)"), start=True, stop=True)
                            last.then_inc(did["mixed_made"], 1)
                        tg, ts = before(g, slot, 1)
                        if exists(tg, groups):
                            pe.wait_ge(did["prob"], upto(tg, ts, PAIRS))
                            rg, rs = before(tg, ts, 1 if HP > 3 else 2)
                            pe.wait_ge(did["probT"], upto(rg, rs, PAIRS))
                            for hp in range(HP):
                                bank = hp // 3 if HP > 3 else ts % 2
                                last = nc.tensor.transpose(psP[:, bank, hp % 3 * 128:hp % 3 * 128 + 128],
                                                           prob[:, ts % 2, 2 * hp:2 * hp + 2, :].rearrange("p h k -> p (h k)"),
                                                           ident[:, :])
                            last.then_inc(did["prob_turned"], 1)

                run_groups(pe, groups, body)

            @block.scalar
            def _(act):
                def body(g, parity):
                    front, back, mlp = g + 1, g - 1, g - 2
                    other = 1 - parity
                    for slot in range(PAIRS):
                        eg, es = before(g, slot, 1)
                        if exists(eg, groups):
                            act.wait_ge(did["shifted"], upto(eg, es, PAIRS))
                            fg, fs = before(eg, es, 2)
                            act.wait_ge(did["prob_turned"], upto(fg, fs, PAIRS))
                            act.wait_ge(did["total"], upto(fg, fs, PAIRS))
                            nc.scalar.activation(prob[:, es % 2, :, 0:WIN],
                                                 score[:, es % 2, :].rearrange("p (h k) -> p h k", k=WIN),
                                                 ACT.Exp).then_inc(did["prob"], 1)
                        tg, ts = before(g, slot, 2)
                        if exists(tg, groups):
                            act.wait_ge(did["prob_turned"], upto(tg, ts, PAIRS))
                            fg, fs = before(tg, ts, 2)
                            act.wait_ge(did["mixed_made"], upto(fg, fs, PAIRS))
                            if HP > 3:
                                frm = psP[:, :, 0:384]
                                to = probT[:, ts % 2, :].rearrange("p (b q) -> p b q", b=2)
                            else:
                                frm = psP[:, ts % 2, 0:384]
                                to = probT[:, ts % 2, :]
                            nc.scalar.activation(to, frm, ACT.Copy).then_inc(did["probT"], 1)
                        if slot == 0:
                            if exists(front, groups):
                                act.wait_ge(did["x_turned"], upto(front))
                                act.wait_ge(did["v_made"], upto(g))
                                nc.scalar.activation(xT[0:DIM, 0:NT].rearrange("p (w t) -> p w t", t=WIN),
                                                     windows_of(psT[0:DIM, :], WIN), ACT.Copy).then_inc(did["xT"], 1)
                            if exists(mlp, groups):
                                act.wait_ge(did["x1_turned"], upto(mlp))
                                act.wait_ge(did["fc1_made"], upto(g - 3, 2, CHUNKS))
                                nc.scalar.activation(x1T[:, :].rearrange("p (w t) -> p w t", t=WIN),
                                                     windows_of(psT[0:DIM, :], WIN), ACT.Copy).then_inc(did["x1T"], 1)
                            if not cosine and exists(front, groups):
                                act.wait_ge(did["k_made"], upto(front))
                                act.wait_ge(did["k_heads"], upto(g, PAIRS - 1, PAIRS))
                                nc.scalar.activation(k_hat[:, :], psM[0:DIM, 1, 0:NT], ACT.Identity,
                                                     bias=b_qk[:, 1:2]).then_inc(did["k_hat"], 1)
                            if exists(mlp, groups):
                                for c in range(CHUNKS):
                                    act.wait_ge(did["fc1_made"], upto(mlp, c, CHUNKS))
                                    if c == 0:
                                        act.wait_ge(did["fc2_made"], upto(g - 3))
                                    nc.scalar.activation(hid[:, c, 0:NT], psM[:, c % 2, 0:NT], ACT.Gelu,
                                                         bias=b_fc1[:, c:c + 1]).then_inc(did["hid"], 1)
                                if cosine:
                                    act.preload_act_table_set(EXP_SET)
                        if slot == 1:
                            if exists(front, groups):
                                if cosine:
                                    act.wait_ge(did["k_read"], upto(front))
                                    act.wait_ge(did["norms_made"], upto(g))
                                    nc.scalar.activation(qk_sq[:, :, :], qk[:, :, :], ACT.Square).then_inc(did["qk_sq"], 1)
                                    act.wait_ge(did["sq_norm"], upto(front))
                                    nc.scalar.activation(sq_norm[:, :, :], sq_norm[:, :, :], ACT.Ln).then_inc(did["log_norm"], 1)
                                    act.wait_ge(did["log_norm"], upto(front))
                                    nc.scalar.activation(sq_norm[:, :, :], sq_norm[:, :, :], ACT.Exp,
                                                         scale=-0.5).then_inc(did["inv_norm"], 1)
                                act.wait_ge(did["v_made"], upto(front))
                                act.wait_ge(did["mixed_made"], upto(g - 1, PAIRS - 1, PAIRS))
                                for odd in range(2):
                                    rows = slice(odd * HALF, (odd + 1) * HALF)
                                    last = nc.scalar.activation(
                                        v_heads[rows, other].rearrange("r p h v o d -> r (p h v) o d")[:, :, odd, :],
                                        psM[rows, 0, 0:WINDOWS * HP * D].rearrange("r (n d) -> r n d", d=D), ACT.Copy)
                                last.then_inc(did["v_heads"], 1)
                        if slot == 2:
                            if exists(back, groups):
                                act.wait_ge(did["mixed_turned"], upto(back))
                                act.wait_ge(did["proj_made"], upto(mlp))
                                nc.scalar.activation(mixedT[0:DIM, 0:NT].rearrange("p (w t) -> p w t", t=WIN),
                                                     windows_of(psT[0:DIM, :], WIN), ACT.Copy).then_inc(did["mixedT"], 1)
                            if cosine and exists(mlp, groups):
                                act.wait_ge(did["fc2_read"], upto(mlp))
                                act.wait_ge(did["z_var"], upto(g - 3))
                                nc.scalar.activation(z_sq[:, :, :], z[:, :, :], ACT.Square,
                                                     scale=DIM ** -0.5).then_inc(did["z_sq"], 1)
                        if slot == 3 and cosine and exists(back, groups):
                            act.wait_ge(did["proj_made"], upto(back))
                            act.wait_ge(did["y_var"], upto(mlp))
                            nc.scalar.activation(y_sq[:, :, :].rearrange("p n c -> p (n c)"), psM[:, 0, 0:PAIRS * DIM],
                                                 ACT.Square, scale=DIM ** -0.5).then_inc(did["y_sq"], 1)

                run_groups(act, groups, body)

            @block.vector
            def _(dve):
                def body(g, parity):
                    front, back, mlp = g + 1, g - 1, g - 2
                    other = 1 - parity
                    for slot in range(PAIRS):
                        if slot == 3 and not cosine and exists(back, groups):
                            dve.wait_ge(did["stats2"], upto(back))
                        if exists(g, groups):
                            half = slot % 2
                            hg, hs = before(g, slot, 2)
                            dve.wait_ge(did["prob"], upto(hg, hs, PAIRS))
                            heads_view = score[:, half, :].rearrange("p (h k) -> p h k", k=WIN)
                            if cosine:
                                for bank in range(SB):
                                    dve.wait_ge(did[f"scored{bank}"], upto(g, slot, PAIRS))
                                    cols = slice(bank * SBC, (bank + 1) * SBC)
                                    kind = bias_tab[:, bass.ds((g % 8) // 7, 1), slot // 3, cols]
                                    nc.vector.tensor_tensor(score[:, half, cols], psS[:, bank, 0:SBC],
                                                            kind.rearrange("p o n -> p (o n)"), ALU.add)\
                                        .then_inc(did[f"score_read{bank}"], 1)
                                dve.wait_ge(did["score_read1"], upto(g, slot, PAIRS))
                                nc.vector.tensor_reduce(top[:, half, :], heads_view, AX.X, ALU.max).then_inc(did["top"], 1)
                            else:
                                dve.wait_ge(did["scored0"], upto(g, slot, PAIRS))
                                from_psum = psS[:, half, 0:SC].rearrange("p (h k) -> p h k", k=WIN)
                                nc.vector.tensor_reduce(top[:, half, :], from_psum, AX.X, ALU.max).then_inc(did["top"], 1)
                                dve.wait_ge(did["top"], upto(g, slot, PAIRS))
                                nc.vector.tensor_tensor(heads_view, from_psum, bcast(top[:, half, :], 2, WIN),
                                                        ALU.subtract).then_inc(did["shifted"], 1)
                        if slot == 3 and not cosine and exists(back, groups):
                            for p in range(PAIRS):
                                last = nc.vector.bn_aggr(moments2[:, p, :], stats2[:, p, :])
                            last.then_inc(did["moments2"], 1)
                        tg, ts = before(g, slot, 1)
                        if exists(tg, groups):
                            dve.wait_ge(did["prob"], upto(tg, ts, PAIRS))
                            nc.vector.tensor_reduce(total[:, ts, :], prob[:, ts % 2, :, 0:WIN], AX.X, ALU.add)\
                                .then_inc(did["total"], 1)
                        if slot == 0 and exists(front, groups):
                            if cosine:
                                dve.wait_ge(did["q_band"], upto(g))
                                dve.wait_ge(did["qk_sq"], upto(g))
                                for n, name in enumerate(("q", "k")):
                                    dve.wait_ge(did[f"{name}_made"], upto(front))
                                    last = nc.vector.tensor_scalar(qk[:, n, :], psM[0:DIM, n, 0:NT], b_qk[:, n:n + 1],
                                                                   None, ALU.add).then_inc(did[f"{name}_read"], 1)
                            else:
                                dve.wait_ge(did["q_made"], upto(front))
                                dve.wait_ge(did["scored0"], upto(g - 1, PAIRS - 1, PAIRS))
                                for band in range(BANDS):
                                    rows = slice(32 * band, 32 * band + 32)
                                    last = nc.vector.tensor_scalar(q_band[rows, other, band, 0:NT], psM[rows, 0, 0:NT],
                                                                   b_qk[rows, 0:1], None, ALU.add)
                                last.then_inc(did["q_band"], 1)
                        if slot == 1:
                            if cosine and exists(front, groups):
                                dve.wait_ge(did["norms_made"], upto(front))
                                dve.wait_ge(did["q_band"], upto(g))
                                nc.vector.tensor_scalar(sq_norm[:, :, :], psM[0:DIM, :, 0:NT], 1e-6, None,
                                                        ALU.max).then_inc(did["sq_norm"], 1)
                            if exists(mlp, groups):
                                dve.wait_ge(did["fc2_made"], upto(mlp))
                                out_of = psM[:, 1, 0:PAIRS * DIM].rearrange("p (n c) -> p n c", c=DIM)
                                if cosine:
                                    dve.wait_ge(did["z_ln"], upto(g - 3))
                                    dve.wait_ge(did["z_sq"], upto(g - 3))
                                    nc.vector.tensor_tensor(z[:, :, :], out_of, bcast(row_fc2[:, :], 1, PAIRS),
                                                            ALU.add).then_inc(did["fc2_read"], 1)
                                else:
                                    dve.wait_ge(did["x1_res"], upto(mlp))
                                    dve.wait_ge(s_store[parity], moved(mlp - 2, parity))
                                    nc.vector.tensor_tensor(x2[:, parity], out_of, x1_res[:, parity],
                                                            ALU.add).then_inc(did["x2"], 1)
                        if slot == 2:
                            if cosine and exists(front, groups):
                                dve.wait_ge(did["inv_norm"], upto(front))
                                dve.wait_ge(did["scored1"], upto(g - 1, PAIRS - 1, PAIRS))
                                dve.wait_ge(did["k_heads"], upto(g, PAIRS - 1, PAIRS))
                                nc.vector.tensor_tensor(k_hat[:, :], qk[:, 1, :], sq_norm[:, 1, :], ALU.mult)\
                                    .then_inc(did["k_hat"], 1)
                                for band in range(BANDS):
                                    rows = slice(32 * band, 32 * band + 32)
                                    last = nc.vector.tensor_tensor(q_band[rows, other, band, 0:NT], qk[rows, 0, :],
                                                                   sq_norm[rows, 0, :], ALU.mult)
                                last.then_inc(did["q_band"], 1)
                            if cosine and exists(mlp, groups):
                                dve.wait_ge(did["z_sq"], upto(mlp))
                                dve.wait_ge(did["z_eps"], upto(g - 3))
                                nc.vector.tensor_reduce(z_var[:, :], z_sq[:, :, :], AX.X, ALU.add).then_inc(did["z_var"], 1)
                            if not cosine and exists(g + 2, groups):
                                dve.wait_ge(s_load[parity], moved(g + 2, parity))
                                dve.wait_ge(did["x_norm"], upto(g + 1))
                                dve.wait_ge(did["var_eps"], upto(g + 1))
                                for p in range(PAIRS):
                                    last = nc.vector.bn_stats(stats[:, p, :], x_in[:, parity, p, :])
                                last.then_inc(did["stats"], 1)
                                dve.wait_ge(did["stats"], upto(g + 2))
                            if not cosine and exists(back, groups):
                                dve.wait_ge(did["proj_made"], upto(back))
                                dve.wait_ge(did["x_res"], upto(back))
                                dve.wait_ge(did["x1_norm"], upto(mlp))
                                dve.wait_ge(did["x1_res"], upto(mlp))
                                nc.vector.tensor_tensor(x1[:, :, :], psM[:, 0, 0:PAIRS * DIM]
                                                        .rearrange("p (n c) -> p n c", c=DIM), x_res[:, other],
                                                        ALU.add).then_inc(did["x1"], 1)
                            if not cosine and exists(g + 2, groups):
                                for p in range(PAIRS):
                                    last = nc.vector.bn_aggr(moments[:, p, :], stats[:, p, :])
                                last.then_inc(did["moments"], 1)
                            if not cosine and exists(back, groups):
                                dve.wait_ge(did["var_eps2"], upto(mlp))
                                dve.wait_ge(did["x1"], upto(back))
                                for p in range(PAIRS):
                                    last = nc.vector.bn_stats(stats2[:, p, :], x1[:, p, :])
                                last.then_inc(did["stats2"], 1)
                        if slot == 3:
                            if cosine and exists(mlp, groups):
                                dve.wait_ge(did["z_rstd"], upto(mlp))
                                dve.wait_ge(did["x2"], upto(g - 3))
                                for p in range(PAIRS):
                                    last = nc.vector.scalar_tensor_tensor(z_ln[:, p, :], z[:, p, :], z_rstd[:, p:p + 1],
                                                                          gain2[:, :], ALU.mult, ALU.mult)
                                last.then_inc(did["z_ln"], 1)
                            if cosine and exists(back, groups):
                                dve.wait_ge(did["y_sq"], upto(back))
                                dve.wait_ge(did["y_eps"], upto(mlp))
                                nc.vector.tensor_reduce(y_var[:, :], y_sq[:, :, :], AX.X, ALU.add).then_inc(did["y_var"], 1)
                                dve.wait_ge(did["y_rstd"], upto(back))
                                dve.wait_ge(did["x1"], upto(mlp))
                                for p in range(PAIRS):
                                    last = nc.vector.scalar_tensor_tensor(y_ln[:, p, :], psM[:, 0, p * DIM:(p + 1) * DIM],
                                                                          y_rstd[:, p:p + 1], gain1[:, :], ALU.mult, ALU.mult)
                                last.then_inc(did["proj_read"], 1)
                            if not cosine and exists(g + 2, groups):
                                dve.wait_ge(did["rstd"], upto(g + 2))
                                dve.wait_ge(did["x_turned"], upto(g + 1))
                                for p in range(PAIRS):
                                    last = nc.vector.tensor_scalar(x_norm[:, p, :], x_in[:, parity, p, :], moments[:, p, 0:1],
                                                                   rstd[:, p:p + 1], ALU.subtract, ALU.mult)
                                last.then_inc(did["x_norm"], 1)
                            if not cosine and exists(back, groups):
                                dve.wait_ge(did["rstd2"], upto(back))
                                dve.wait_ge(did["x1_turned"], upto(mlp))
                                for p in range(PAIRS):
                                    last = nc.vector.tensor_scalar(x1_norm[:, p, :], x1[:, p, :], moments2[:, p, 0:1],
                                                                   rstd2[:, p:p + 1], ALU.subtract, ALU.mult)
                                last.then_inc(did["x1_norm"], 1)
                        mg, ms = before(g, slot, 2)
                        if ms % 2 == 1 and exists(mg, groups):
                            dve.wait_ge(did["total"], upto(mg, ms, PAIRS))
                            dve.wait_ge(did["mixed"], upto(mg - 1, ms // 2, 2))
                            nc.vector.reciprocal(inv_total[:, ms - 1:ms + 1, :], total[:, ms - 1:ms + 1, :])\
                                .then_inc(did["inv_total"], 1)
                            dve.wait_ge(did["inv_total"], upto(mg, ms // 2, 2))
                            dve.wait_ge(did["mixed_made"], upto(mg, ms, PAIRS))
                            dve.wait_ge(did["mixed_turned"], upto(mg - 1))
                            for half in range(2):
                                rows = slice(half * HALF, (half + 1) * HALF)
                                made = psO[rows, 0:4 * DIM].rearrange("r (n v o d) -> r n v o d", v=2, o=2, d=D)[:, :, half]
                                inv = inv_total[rows, ms - 1:ms + 1, :].rearrange("r p (h o) -> r (p h) o", o=2)
                                out = mixed[rows, ms - 1:ms + 1, :].rearrange("r p (h o d) -> r (p h) o d", o=2, d=D)
                                last = nc.vector.tensor_tensor(out, made, bcast(inv, 3, D), ALU.mult)
                            last.then_inc(did["mixed"], 1)

                run_groups(dve, groups, body)

            @block.gpsimd
            def _(pool):
                def add_eps_power(name_in, v_in, group, eps_buf, name_eps, out, name_out, free):
                    pool.wait_ge(did[name_in], upto(group))
                    pool.wait_ge(did[name_out], upto(group - 1))
                    nc.gpsimd.tensor_tensor(eps_buf, v_in, epsilon[:, :], ALU.add).then_inc(did[name_eps], 1)
                    pool.wait_ge(did[name_eps], upto(group))
                    pool.wait_ge(did[free], upto(group - 1))
                    nc.gpsimd.tensor_tensor(out, eps_buf, half_power[:, :], ALU.pow).then_inc(did[name_out], 1)

                def body(g, parity):
                    front, back, mlp = g + 1, g - 1, g - 2
                    other = 1 - parity
                    for slot in range(PAIRS):
                        if slot == 0 and exists(g, groups):
                            pool.wait_ge(s_load[parity], moved(g, parity))
                            pool.wait_ge(did["x1"], upto(g - 2))
                            nc.gpsimd.tensor_tensor(x_res[:, parity], x_in[:, parity], bcast(res_row1[:, :], 1, PAIRS),
                                                    ALU.add).then_inc(did["x_res"], 1)
                        if cosine and exists(g, groups):
                            half = slot % 2
                            pool.wait_ge(did["top"], upto(g, slot, PAIRS))
                            view = score[:, half, :].rearrange("p (h k) -> p h k", k=WIN)
                            nc.gpsimd.tensor_tensor(view, view, bcast(top[:, half, :], 2, WIN), ALU.subtract)\
                                .then_inc(did["shifted"], 1)
                        if slot >= 2 and exists(front, groups):
                            if slot == 2:
                                pool.wait_ge(did["k_hat"], upto(front))
                                pool.wait_ge(did[f"scored{SB - 1}"], upto(g - 1, PAIRS - 1, PAIRS))
                            for p in ((0, 1) if slot == 2 else (2, 3)):
                                for half in range(2):
                                    w = 2 * p + half
                                    last = nc.gpsimd.tensor_tensor(
                                        k_heads[0:DIM, other, w, :].rearrange("c (j k) -> c j k", j=J),
                                        bcast(k_hat[:, w * WIN:(w + 1) * WIN], 1, J),
                                        bcast(head_mask[:, :], 2, WIN), ALU.mult)
                                last.then_inc(did["k_heads"], 1)
                        if cosine:
                            if slot == 2 and exists(mlp, groups):
                                add_eps_power("z_var", z_var[:, :], mlp, z_eps[:, :], "z_eps", z_rstd[:, :],
                                              "z_rstd", "z_ln")
                            if slot == 3 and exists(mlp, groups):
                                pool.wait_ge(did["z_ln"], upto(mlp))
                                pool.wait_ge(did["x1_res"], upto(mlp))
                                pool.wait_ge(s_store[parity], moved(mlp - 2, parity))
                                nc.gpsimd.tensor_tensor(x2[:, parity], z_ln[:, :, :], x1_res[:, parity], ALU.add)\
                                    .then_inc(did["x2"], 1)
                            if slot == 3 and exists(back, groups):
                                add_eps_power("y_var", y_var[:, :], back, y_eps[:, :], "y_eps", y_rstd[:, :],
                                              "y_rstd", "proj_read")
                                pool.wait_ge(did["proj_read"], upto(back))
                                pool.wait_ge(did["x1_turned"], upto(mlp))
                                pool.wait_ge(did["x1_res"], upto(mlp))
                                pool.wait_ge(did["x_res"], upto(back))
                                nc.gpsimd.tensor_tensor(x1[:, :, :], y_ln[:, :, :], x_res[:, other], ALU.add)\
                                    .then_inc(did["x1"], 1)
                                pool.wait_ge(did["x1"], upto(back))
                                pool.wait_ge(did["x2"], upto(g - 3))
                                nc.gpsimd.tensor_tensor(x1_res[:, other], x1[:, :, :], bcast(res_row2[:, :], 1, PAIRS),
                                                        ALU.add).then_inc(did["x1_res"], 1)
                        else:
                            if slot == 2 and exists(g + 2, groups):
                                add_eps_power("moments", moments[:, :, 1], g + 2, var_eps[:, :], "var_eps", rstd[:, :],
                                              "rstd", "x_norm")
                            if slot == 3 and exists(back, groups):
                                add_eps_power("moments2", moments2[:, :, 1], back, var_eps2[:, :], "var_eps2",
                                              rstd2[:, :], "rstd2", "x1_norm")
                            if slot == 3 and exists(back, groups):
                                pool.wait_ge(did["x1"], upto(back))
                                pool.wait_ge(did["x2"], upto(g - 3))
                                nc.gpsimd.tensor_tensor(x1_res[:, other], x1[:, :, :], bcast(row_fc2[:, :], 1, PAIRS),
                                                        ALU.add).then_inc(did["x1_res"], 1)

                run_groups(pool, groups, body)


def two_blocks(nc, x, out, params, const):
    scratch = nc.dram_tensor("between_blocks", [IMAGES, SIDE, SIDE, DIM], F32, kind="Internal").ap()
    with ExitStack() as ctx:
        def pb(name, shape):
            return ctx.enter_context(nc.psum_tensor(name, shape, F32))

        psum = {"scores": pb("ps_scores", [128, 2, BANK]), "probs": pb("ps_probs", [128, 2, BANK]),
                "turn": pb("ps_turn", [128, BANK]), "dense": pb("ps_dense", [128, 2, BANK]),
                "mixed": pb("ps_mixed", [128, BANK])}
        block_program(nc, Swin, x, scratch, params["L0"], const, psum)
        block_program(nc, Plain, scratch, out, params["L1"], const, psum)


def shape_constants():
    def token(order, n):
        return (n % 7, n // 7) if order == 0 else (n // 7, n % 7)

    c = {"ident": np.eye(128, dtype=np.float32)}
    f = np.arange(DIM)
    c["same_head"] = (f[:, None] // 8 == f[None, :] // 8).astype(np.float32)
    c["pick"] = (np.arange(12)[:, None] == f[None, :] // 8).astype(np.float32)
    c["swin_head_mask"] = (f[:, None] % 32 // 8 == np.arange(4)[None, :]).astype(np.float32)
    c["plain_head_mask"] = (f[:, None] % 32 // 16 == np.arange(2)[None, :]).astype(np.float32)
    rel = np.zeros((2, 2, 49, 49), np.float32)
    mask = np.zeros((128, 2, 2, 49), np.float32)
    region = np.zeros((SIDE, SIDE))
    n = 0
    for hs in (slice(0, -7), slice(-7, -3), slice(-3, None)):
        for ws in (slice(0, -7), slice(-7, -3), slice(-3, None)):
            region[hs, ws] = n
            n += 1
    for order in range(2):
        at = np.array([token(order, n) for n in range(49)])
        d = (at[:, None, :] - at[None, :, :]).astype(np.float32)
        rel[:, order] = np.moveaxis(np.sign(d) * np.log1p(np.abs(d)), 2, 0)
        wy = 7 if order else 0
        for edge in range(2):
            for half in range(2):
                wx = 6 * edge + half
                r = region[wy * 7 + at[:, 0], wx * 7 + at[:, 1]]
                mask[half * HALF:half * HALF + 49, order, edge] = np.where(r[:, None] != r[None, :], -100.0, 0.0)
    c["rel"] = rel.reshape(2, 2, 49 * 49)
    c["mask"] = mask
    return c


_L0 = ["qkv_w", "qkv_b", "proj_w", "proj_b", "tau", "meta_w1", "meta_b1", "meta_w2", "meta_b2", "norm1_g", "norm1_b",
       "fc1_w", "fc1_b", "fc2_w", "fc2_b", "norm2_g", "norm2_b"]
_L1 = {"g1": "g1", "b1": "b1", "w_qkv": "qkv_w", "b_qkv": "qkv_b", "w_proj": "proj_w", "b_proj": "proj_b", "g2": "g2",
       "b2": "b2", "w_fc1": "fc1_w", "b_fc1": "fc1_b", "w_fc2": "fc2_w", "b_fc2": "fc2_b"}


def kernel(**inputs):
    import numpy as _np
    import concourse.bacc as _bacc
    from concourse import mybir as _mybir
    from concourse.bass_utils import run_bass_kernel_spmd as _run

    nc = _bacc.Bacc("TRN2", target_bir_lowering=False, num_devices=1)
    arrays = {}

    def give(name, a):
        a = _np.ascontiguousarray(a)
        arrays[f"in_{name}"] = a
        return nc.dram_tensor(f"in_{name}", a.shape, _mybir.dt.from_np(a.dtype), kind="ExternalInput").ap()

    x = give("x", inputs["x"])
    params = {"L0": {k: give(f"L0_{k}", inputs[f"L0_conv_{k}"]) for k in _L0},
              "L1": {v: give(f"L1_{k}", inputs[f"L1_conv_{k}"]) for k, v in _L1.items()}}
    const = {k: give(f"const_{k}", v) for k, v in shape_constants().items()}
    out = nc.dram_tensor("out_0_dram", (IMAGES, SIDE, SIDE, DIM), _mybir.dt.float32, kind="ExternalOutput").ap()
    two_blocks(nc, x, out, params, const)
    r = _run(nc, [arrays], core_ids=[0])
    return r.results[0]["out_0_dram"]
```

```python
from contextlib import ExitStack

import numpy as np
import concourse.bass as bass
from concourse import mybir

F32 = mybir.dt.float32
ALU = mybir.AluOpType
ACT = mybir.ActivationFunctionType
AX = mybir.AxisListType

IMAGES, SIDE, DIM, HIDDEN = 32, 56, 96, 384
PAIRS = 4
WINDOWS = 2 * PAIRS
HALF = 64
CHUNKS = HIDDEN // 128
BANDS = 3
BANK = 512
EXP_SET = "natural_log_exp_and_others"
GELU_SET = "gelu_and_others"


class Swin:
    name, win, heads, shift, eps = "swin", 7, 12, 3, 1e-5
    groups = IMAGES * (SIDE // 7) * (SIDE // 7) // WINDOWS
    cosine = True
    score_banks = 2
    score_parts = [(0, 0, 4, 0, 0), (1, 0, 2, 0, 196), (1, 2, 2, 1, 0), (2, 0, 4, 1, 98)]


class Plain:
    name, win, heads, shift, eps = "plain", 8, 6, 0, 1e-6
    groups = IMAGES * (SIDE // 8) * (SIDE // 8) // WINDOWS
    cosine = False
    score_banks = 1
    score_parts = [(0, 0, 2, 0, 0), (1, 0, 2, 0, 128), (2, 0, 2, 0, 256)]


STEPS = {
    "setup_zeroed": "buffers cleared", "setup_loaded": "weights in SBUF", "setup_vector": "vector engine's set-up steps",
    "setup_products": "tensor engine's set-up steps", "setup_scalar": "scalar engine's set-up steps",
    "setup_hidden": "a part of the bias network's hidden layer is in PSUM",
    "x_loaded_even": "windows of an even group are in x_in", "x_loaded_odd": "windows of an odd group are in x_in",
    "x2_stored_even": "an even group's result is in DRAM", "x2_stored_odd": "an odd group's result is in DRAM",
    "stats": "partial moments of x_in", "moments": "mean and variance of x_in", "var_eps": "variance + epsilon",
    "rstd": "its power -1/2", "x_norm": "normalised input", "x_res": "input + constant row",
    "x_turned": "input is feature-major in psT", "xT": "... and in SBUF",
    "q_made": "queries in dense bank 0", "k_made": "keys in dense bank 1",
    "q_read": "dense bank 0 read", "k_read": "dense bank 1 read",
    "qk_sq": "squares of queries and keys", "norms_made": "squared norms in the dense banks",
    "sq_norm": "squared norms with their floor in SBUF", "log_norm": "their logarithm", "inv_norm": "1 / norm",
    "q_band": "queries, one copy to a band, other bands zero", "k_hat": "keys ready to be spread over heads",
    "k_heads": "keys spread over heads, for one pair", "v_made": "values in dense bank 0", "v_heads": "... and in SBUF",
    "scored0": "scores in their first bank", "scored1": "scores in their second bank",
    "score_read0": "first score bank read", "score_read1": "second score bank read",
    "top": "greatest score of each query and head", "shifted": "scores less their top",
    "prob": "exponentials", "total": "their sums", "inv_total": "1 / sum, for two pairs",
    "prob_turned": "exponentials turned in psP", "probT": "... and in SBUF",
    "mixed_made": "exponentials times values in psO", "mixed": "two pairs divided by their sums, in SBUF",
    "mixed_turned": "attention output feature-major in psT", "mixedT": "... and in SBUF",
    "proj_made": "projection in dense bank 0", "proj_read": "... and read",
    "y_ln": "normalised projection", "y_var": "variance", "y_eps": "+ epsilon", "y_rstd": "power -1/2",
    "x1": "first residual", "x1_res": "x1 + constant row", "stats2": "partial moments of x1",
    "moments2": "mean and variance of x1", "var_eps2": "+ epsilon", "rstd2": "power -1/2", "x1_norm": "normalised x1",
    "x1_turned": "MLP input feature-major in psT", "x1T": "... and in SBUF",
    "fc1_made": "a chunk of the hidden layer in a dense bank", "hid": "GELU of a chunk in SBUF",
    "fc2_made": "MLP output in dense bank 1", "fc2_read": "... and read",
    "z_sq": "squares of the MLP output", "z_var": "variance", "z_eps": "+ epsilon", "z_rstd": "power -1/2",
    "z_ln": "normalised MLP output", "x2": "the block's result",
}


def bcast(ap, axis, count):
    dims = [list(d) for d in ap.ap]
    dims.insert(axis, [0, count])
    return bass.AP(ap.tensor, ap.offset, dims)


def count_for(group, index, per_group, groups):
    if isinstance(group, int):
        if group < 0:
            return 0
        if group >= groups:
            group, index = groups - 1, per_group - 1
    return group * per_group + (index + 1)


def before(group, slot, lag):
    while slot < lag:
        group, slot = group - 1, slot + PAIRS
    return group, slot - lag


def exists(group, groups):
    return not isinstance(group, int) or 0 <= group < groups


def run_groups(engine, groups, body):
    for g in range(-3, 8):
        body(g, g % 4)
    with engine.Fori(2, groups // 4 - 1) as m:
        for r in range(4):
            body(4 * m + r, r)
    for g in range(groups - 4, groups + 5):
        body(g, g % 4)


def block_program(nc, cfg, src, dst, par, const, psum):
    win, heads, groups = cfg.win, cfg.heads, cfg.groups
    WIN = win * win
    NT = WINDOWS * WIN
    NTP = NT + 16
    D = DIM // heads
    J = 32 // D
    HP = heads // 2
    SC = heads * WIN
    cosine = cfg.cosine
    SB = cfg.score_banks
    SBC = SC // SB
    PAIR_COLS = 2 * WIN

    ctx = ExitStack()
    with ctx:
        def sb(name, shape):
            return ctx.enter_context(nc.sbuf_tensor(f"{cfg.name}_{name}", shape, F32))

        did = {name: ctx.enter_context(nc.semaphore(f"{cfg.name}_{name}")) for name in STEPS}
        if not cosine:
            did.update(q_read=did["q_band"], k_read=did["k_hat"], score_read0=did["shifted"],
                       proj_read=did["x1"], fc2_read=did["x2"])

        def upto(group, index=0, per=1):
            return count_for(group, index, per, groups)

        psS = psum["scores"]
        psP = psum["probs"]
        psT = psum["turn"]
        psM = psum["dense"]
        psO = psum["mixed"]

        ident = sb("ident", [128, 128])
        w_qkv = sb("w_qkv", [128, 3 * DIM])
        b_qk = sb("b_qk", [DIM, 2])
        w_proj = sb("w_proj", [DIM + 1, DIM])
        w_fc1 = sb("w_fc1", [DIM, HIDDEN])
        b_fc1 = sb("b_fc1", [128, CHUNKS])
        w_fc2 = sb("w_fc2", [128, CHUNKS, DIM])
        row_fc2 = sb("row_fc2", [128, DIM])
        head_mask = sb("head_mask", [DIM, J])
        mean_row = sb("mean_row", [128, 8])
        res_row1 = sb("res_row1", [128, DIM])
        scr = sb("scr", [128, 128])
        half_power = sb("half_power", [128, PAIRS])
        epsilon = sb("epsilon", [128, PAIRS])
        if cosine:
            same_head = sb("same_head", [DIM, DIM])
            gain1 = sb("gain1", [128, DIM])
            gain2 = sb("gain2", [128, DIM])
            res_row2 = sb("res_row2", [128, DIM])
            bias_tab = sb("bias_tab", [128, 2, 2, SC])
            pick = sb("pick", [heads, DIM])
            tau = sb("tau", [heads, 1])
        else:
            norm_par = sb("norm_par", [DIM, 4])
            b_v = sb("b_v", [DIM, 1])

        x_in = sb("x_in", [128, 2, PAIRS, DIM])
        x_res = sb("x_res", [128, 4, PAIRS, DIM])
        xT = sb("xT", [128, 2, NTP])
        q_band = sb("q_band", [128, 2, BANDS, NTP])
        k_hat = sb("k_hat", [DIM, NT])
        k_heads = sb("k_heads", [128, 2, WINDOWS, J * WIN])
        v_heads = sb("v_heads", [128, 2, PAIRS, HP, 2, 2, D])
        score = sb("score", [128, 2, SC])
        top = sb("top", [128, 2, heads])
        prob = sb("prob", [128, 2, heads, HALF])
        probT = sb("probT", [128, 2, HP * 128])
        total = sb("total", [128, PAIRS, heads])
        inv_total = sb("inv_total", [128, PAIRS, heads])
        mixed = sb("mixed", [128, PAIRS, DIM])
        mixedT = sb("mixedT", [DIM + 1, NTP])
        x1 = sb("x1", [128, PAIRS, DIM])
        x1_res = sb("x1_res", [128, 4, PAIRS, DIM])
        x1T = sb("x1T", [DIM, NT])
        hid = sb("hid", [128, CHUNKS, NTP])
        x2 = sb("x2", [128, 2, PAIRS, DIM])
        if cosine:
            qk = sb("qk", [DIM, 2, NT])
            qk_sq = sb("qk_sq", [DIM, 2, NT])
            sq_norm = sb("sq_norm", [DIM, 2, NT])
            y = sb("y", [128, PAIRS, DIM])
            y_sq = sb("y_sq", [128, PAIRS, DIM])
            y_var = sb("y_var", [128, PAIRS])
            y_eps = sb("y_eps", [128, PAIRS])
            y_rstd = sb("y_rstd", [128, PAIRS])
            y_ln = sb("y_ln", [128, PAIRS, DIM])
            z = sb("z", [128, PAIRS, DIM])
            z_sq = sb("z_sq", [128, PAIRS, DIM])
            z_var = sb("z_var", [128, PAIRS])
            z_eps = sb("z_eps", [128, PAIRS])
            z_rstd = sb("z_rstd", [128, PAIRS])
            z_ln = sb("z_ln", [128, PAIRS, DIM])
        else:
            stats = sb("stats", [128, PAIRS, 6])
            moments = sb("moments", [128, PAIRS, 2])
            var_eps = sb("var_eps", [128, PAIRS])
            rstd = sb("rstd", [128, PAIRS])
            x_norm = sb("x_norm", [128, PAIRS, DIM])
            stats2 = sb("stats2", [128, PAIRS, 6])
            moments2 = sb("moments2", [128, PAIRS, 2])
            var_eps2 = sb("var_eps2", [128, PAIRS])
            rstd2 = sb("rstd2", [128, PAIRS])
            x1_norm = sb("x1_norm", [128, PAIRS, DIM])

        def windows_of(ap, width):
            return ap.rearrange("p (w t) -> p w t", t=HALF)[:, :, 0:width]

        setup = ExitStack()
        with setup:
            if cosine:
                hidden = setup.enter_context(nc.sbuf_tensor("meta_hidden", [DIM, 2, WIN * WIN], F32))
                rel = setup.enter_context(nc.sbuf_tensor("meta_rel", [2, 2, WIN * WIN], F32))
                meta_w1 = setup.enter_context(nc.sbuf_tensor("meta_w1", [2, DIM], F32))
                meta_b1 = setup.enter_context(nc.sbuf_tensor("meta_b1", [DIM, 1], F32))
                meta_w2 = setup.enter_context(nc.sbuf_tensor("meta_w2", [DIM, heads], F32))
                meta_b2 = setup.enter_context(nc.sbuf_tensor("meta_b2", [128, heads], F32))
                mask = setup.enter_context(nc.sbuf_tensor("mask", [128, 2, 2, WIN], F32))
                b_v = setup.enter_context(nc.sbuf_tensor("b_v", [DIM, 1], F32))
            b_proj = setup.enter_context(nc.sbuf_tensor(f"{cfg.name}_b_proj", [128, DIM], F32))
            s_zero = did["setup_zeroed"]
            s_par = did["setup_loaded"]
            s_vec = did["setup_vector"]
            s_mul = did["setup_products"]
            s_act = did["setup_scalar"]
            loads = []

            def column(a):
                return a.rearrange("(c o) -> c o", o=1)

            def every_row(a, n):
                return a.rearrange("(o c) -> o c", o=1).broadcast_to([128, n])

            loads += [(ident[:, :], const["ident"]), (w_fc1[:, :], par["fc1_w"]),
                      (w_fc2[:, :, :], par["fc2_w"].rearrange("(c p) n -> p c n", p=128)),
                      (w_qkv[0:DIM, :], par["qkv_w"]), (w_proj[0:DIM, :], par["proj_w"]),
                      (b_qk[:, :], par["qkv_b"][0:2 * DIM].rearrange("(t c) -> c t", t=2)),
                      (b_v[:, :], column(par["qkv_b"][2 * DIM:3 * DIM])),
                      (b_fc1[:, :], par["fc1_b"].rearrange("(c p) -> p c", p=128)),
                      (row_fc2[:, :], every_row(par["fc2_b"], DIM)),
                      (head_mask[:, :], const[f"{cfg.name}_head_mask"])]
            if cosine:
                loads += [(same_head[:, :], const["same_head"]), (pick[:, :], const["pick"]),
                          (tau[:, :], column(par["tau"])),
                          (gain1[:, :], every_row(par["norm1_g"], DIM)),
                          (res_row1[:, :], every_row(par["norm1_b"], DIM)),
                          (gain2[:, :], every_row(par["norm2_g"], DIM)),
                          (res_row2[:, :], every_row(par["norm2_b"], DIM)),
                          (b_proj[DIM:DIM + 1, :], par["proj_b"].rearrange("(o c) -> o c", o=1)),
                          (rel[:, :, :], const["rel"]), (meta_w1[:, :], par["meta_w1"]),
                          (meta_b1[:, :], column(par["meta_b1"])), (meta_w2[:, :], par["meta_w2"]),
                          (meta_b2[:, :], every_row(par["meta_b2"], heads)),
                          (mask[:, :, :, :], const["mask"])]
            else:
                loads += [(norm_par[:, n:n + 1], column(par[k])) for n, k in enumerate(["g1", "b1", "g2", "b2"])]
                loads += [(b_proj[:, :], every_row(par["proj_b"], DIM))]

            with nc.Block() as block:
                @block.sync
                def _(sp):
                    sp.wait_ge(s_zero, 1)
                    for to, frm in loads:
                        sp.dma_start(to, frm, allow_slow_non_contiguous=True).then_inc(s_par, 16)

                @block.gpsimd
                def _(pool):
                    nc.gpsimd.memset(w_qkv[:, :], 0.0).then_inc(s_zero, 1)
                    for buf in (xT, hid, q_band, k_heads, v_heads, prob, probT, x_in, mixedT):
                        nc.gpsimd.memset(buf[:], 0.0)
                    if cosine:
                        nc.gpsimd.memset(bias_tab[:], 0.0)
                    nc.gpsimd.memset(epsilon[:], cfg.eps)
                    nc.gpsimd.memset(half_power[:], -0.5).then_inc(s_zero, 1)

                @block.vector
                def _(dve):
                    steps = [0]

                    def step(ins):
                        steps[0] += 1
                        ins.then_inc(s_vec, 1)
                        dve.wait_ge(s_vec, steps[0])

                    def centre(w, rows, slot):
                        step(nc.vector.reduce_sum(mean_row[0:rows, slot:slot + 1], w, axis=AX.X))
                        step(nc.vector.tensor_scalar(mean_row[0:rows, slot:slot + 1],
                                                     mean_row[0:rows, slot:slot + 1], 1.0 / DIM, None, ALU.mult))
                        step(nc.vector.tensor_scalar(w, w, mean_row[0:rows, slot:slot + 1], None, ALU.subtract))

                    dve.wait_ge(s_par, 16 * len(loads))
                    dve.wait_ge(s_zero, 2)
                    if cosine:
                        step(nc.vector.memset(mixedT[DIM:DIM + 1, :], 1.0))
                        dve.wait_ge(s_mul, 1)
                        step(nc.vector.tensor_tensor(w_proj[DIM:DIM + 1, :], psT[DIM:DIM + 1, 0:DIM],
                                                     b_proj[DIM:DIM + 1, :], ALU.add))
                        centre(w_proj[:, :], DIM + 1, 0)
                        for c in range(CHUNKS):
                            centre(w_fc2[:, c, :], 128, 1 + c)
                        centre(row_fc2[:, :], 128, 4)
                        dve.wait_ge(s_mul, 2)
                        step(nc.vector.tensor_scalar(scr[0:DIM, 0:1], psM[0:DIM, 0, 0:1], 0.01, None, ALU.max))
                        step(nc.vector.reciprocal(scr[0:DIM, 0:1], scr[0:DIM, 0:1]))
                        step(nc.vector.tensor_scalar(head_mask[:, :], head_mask[:, :], scr[0:DIM, 0:1], None, ALU.mult))
                        for order in range(2):
                            dve.wait_ge(s_mul, 2 + 2 * order + 2)
                            for part, (k0, k1) in enumerate([(0, 42), (42, WIN)]):
                                for r in (0, HALF):
                                    rows = slice(r, r + WIN)
                                    out = bias_tab[rows, order, 0, :].rearrange("p (h k) -> p h k", k=WIN)[:, :, k0:k1]
                                    got = psS[rows, part, 0:(k1 - k0) * heads].rearrange("p (k h) -> p h k", h=heads)
                                    step(nc.vector.tensor_tensor(out, got, bcast(meta_b2[rows, :], 2, k1 - k0), ALU.add))
                            for edge in (1, 0):
                                out = bias_tab[:, order, edge, :].rearrange("p (h k) -> p h k", k=WIN)
                                base = bias_tab[:, order, 0, :].rearrange("p (h k) -> p h k", k=WIN)
                                step(nc.vector.tensor_tensor(out, base, bcast(mask[:, order, edge, :], 1, heads), ALU.add))
                    else:
                        dve.wait_ge(s_mul, 1)
                        step(nc.vector.tensor_tensor(b_qk[:, :], b_qk[:, :], psT[0:DIM, 0:2], ALU.add))
                        step(nc.vector.tensor_scalar(b_qk[:, 0:1], b_qk[:, 0:1], D ** -0.5, None, ALU.mult))
                        step(nc.vector.tensor_tensor(b_v[:, :], b_v[:, :], psT[0:DIM, 2:3], ALU.add))
                        step(nc.vector.tensor_tensor(b_fc1[:, :], b_fc1[:, :], psT[:, 3:3 + CHUNKS], ALU.add))
                        step(nc.vector.tensor_scalar(w_qkv[0:DIM, :], w_qkv[0:DIM, :], norm_par[:, 0:1], None, ALU.mult))
                        step(nc.vector.tensor_scalar(w_qkv[0:DIM, 0:DIM], w_qkv[0:DIM, 0:DIM], D ** -0.5, None, ALU.mult))
                        step(nc.vector.tensor_scalar(w_fc1[:, :], w_fc1[:, :], norm_par[:, 2:3], None, ALU.mult))
                        step(nc.vector.tensor_copy(scr[0:DIM, 0:128], bcast(b_v[:, 0:1], 1, 128)[:, :, 0]))
                        dve.wait_ge(s_mul, 2)
                        step(nc.vector.tensor_tensor(res_row1[:, :], psM[:, 0, 0:DIM], b_proj[:, :], ALU.add))

                @block.tensor
                def _(pe):
                    pe.wait_ge(s_par, 16 * len(loads))
                    if cosine:
                        nc.tensor.matmul(psT[DIM:DIM + 1, 0:DIM], b_v[:, :], w_proj[0:DIM, :],
                                         start=True, stop=True).then_inc(s_mul, 1)
                        nc.tensor.matmul(psM[0:DIM, 0, 0:1], pick[:, :], tau[:, :],
                                         start=True, stop=True).then_inc(s_mul, 1)
                        for order in range(2):
                            cols = WIN * WIN
                            starts = list(range(0, cols, 480))
                            for n, a in enumerate(starts):
                                b = min(a + 480, cols)
                                if n or order:
                                    pe.wait_ge(s_act, n + order * len(starts))
                                last = nc.tensor.matmul(psM[0:DIM, 1, 0:b - a], meta_w1[:, :], rel[:, order, a:b],
                                                        start=True, stop=True)
                                last.then_inc(did["setup_hidden"], 1)
                            pe.wait_ge(s_act, (order + 1) * len(starts))
                            if order:
                                pe.wait_ge(s_vec, 1 + 1 + 3 * 5 + 3 + 6)
                            for half in (0, HALF):
                                for k in range(WIN):
                                    part, col = (0, k) if k < 42 else (1, k - 42)
                                    keyed = hidden[:, order, :].rearrange("c (q k) -> c q k", k=WIN)[:, :, k]
                                    last = nc.tensor.matmul(psS[half:half + WIN, part, col * heads:(col + 1) * heads],
                                                            keyed, meta_w2[:, :], start=True, stop=True)
                                last.then_inc(s_mul, 1)
                    else:
                        pe.wait_ge(s_zero, 1)
                        for n in range(3):
                            nc.tensor.matmul(psT[0:DIM, n:n + 1], w_qkv[0:DIM, n * DIM:(n + 1) * DIM], norm_par[:, 1:2],
                                             start=True, stop=True)
                        for c in range(CHUNKS):
                            last = nc.tensor.matmul(psT[:, 3 + c:4 + c], w_fc1[:, c * 128:(c + 1) * 128],
                                                    norm_par[:, 3:4], start=True, stop=True)
                        last.then_inc(s_mul, 1)
                        pe.wait_ge(s_vec, 8)
                        nc.tensor.matmul(psM[:, 0, 0:DIM], scr[0:DIM, 0:128], w_proj[0:DIM, :],
                                         start=True, stop=True).then_inc(s_mul, 1)

                if cosine:
                    @block.scalar
                    def _(act):
                        act.wait_ge(s_par, 16 * len(loads))
                        done = 0
                        for order in range(2):
                            cols = WIN * WIN
                            for a in range(0, cols, 480):
                                b = min(a + 480, cols)
                                done += 1
                                act.wait_ge(did["setup_hidden"], done)
                                nc.scalar.activation(hidden[:, order, a:b], psM[0:DIM, 1, 0:b - a], ACT.Relu,
                                                     bias=meta_b1[:, :]).then_inc(s_act, 1)

        def dma_total(parity, upto):
            per = 16 * (WINDOWS + 1 if cosine else PAIRS)
            if not cosine:
                return upto * per
            if parity == 0:
                return upto * per
            return upto * per + (upto // 4) * 16 * 19

        def swin_windows(image, wy, tile, move):
            rows = bass.ds(image * SIDE + cfg.shift + win * wy, win) if wy < 7 else None
            for p in range(PAIRS):
                for half in range(2):
                    at = half * HALF
                    col = cfg.shift + win * (2 * p + half)
                    spans = [(col, 0, win)] if col + win <= SIDE else [(col, 0, SIDE - col), (0, SIDE - col, win)]
                    if wy < 7:
                        for c0, a, b in spans:
                            move(tile[at + a * win:at + b * win, p, :],
                                 rows, slice(c0, c0 + b - a), "y x c -> x y c")
                    else:
                        low = cfg.shift + win * 7
                        for r0, ya, yb in [(low, 0, SIDE - low), (0, SIDE - low, win)]:
                            if len(spans) == 1:
                                move(tile[at + ya * win:at + yb * win, p, :],
                                     bass.ds(image * SIDE + r0, yb - ya), slice(col, col + win), "y x c -> y x c")
                            else:
                                for y in range(ya, yb):
                                    for c0, a, b in spans:
                                        move(tile[at + y * win + a:at + y * win + b, p, :],
                                             bass.ds(image * SIDE + r0 + y - ya, 1), slice(c0, c0 + b - a),
                                             "y x c -> (y x) c")

        with nc.Block() as block:
            s_load = [did["x_loaded_even"], did["x_loaded_odd"]]
            s_store = [did["x2_stored_even"], did["x2_stored_odd"]]

            @block.sync
            def _(sp):
                src_rows = src.rearrange("b h w c -> (b h) w c")
                dst_rows = dst.rearrange("b h w c -> (b h) w c")

                def may_load(n):
                    sp.wait_ge(did["x_res"], upto(n - 2))
                    sp.wait_ge(did["x_turned" if cosine else "x_norm"], upto(n - 2))

                if cosine:
                    def load(image, wy):
                        may_load(image * 8 + wy)
                        swin_windows(image, wy, x_in[:, wy % 2], lambda tile, rows, cols, order:
                                     sp.dma_start(tile, src_rows[rows, cols, :].rearrange(order))
                                     .then_inc(s_load[wy % 2], 16))

                    def store(image, wy):
                        sp.wait_ge(did["x2"], upto(image * 8 + wy))
                        swin_windows(image, wy, x2[:, wy % 2], lambda tile, rows, cols, order:
                                     sp.dma_start(dst_rows[rows, cols, :].rearrange(order), tile)
                                     .then_inc(s_store[wy % 2], 16))

                    for wy in range(8):
                        load(0, wy)
                    with sp.Fori(1, IMAGES) as image:
                        for wy in range(8):
                            load(image, wy)
                            store(image - 1, wy)
                    for wy in range(8):
                        store(IMAGES - 1, wy)
                else:
                    def place(n, p):
                        pair = n * PAIRS + p
                        return bass.ds((pair // 7) * 2 * win, 2 * win), bass.ds((pair % 7) * win, win)

                    def load(n, parity):
                        may_load(n)
                        for p in range(PAIRS):
                            rows, cols = place(n, p)
                            sp.dma_start(x_in[:, parity, p, :], src_rows[rows, cols, :]).then_inc(s_load[parity], 16)

                    def store(n, parity):
                        sp.wait_ge(did["x2"], upto(n))
                        for p in range(PAIRS):
                            rows, cols = place(n, p)
                            sp.dma_start(dst_rows[rows, cols, :], x2[:, parity, p, :]).then_inc(s_store[parity], 16)

                    for n in range(8):
                        load(n, n % 2)
                    with sp.Fori(4, groups // 2) as m:
                        for k in range(2):
                            load(2 * m + k, k)
                            store(2 * m + k - 8, k)
                    for n in range(groups - 8, groups):
                        store(n, n % 2)
                for parity in range(2):
                    sp.wait_ge(s_store[parity], dma_total(parity, groups // 2))

            def moved(g, parity):
                return 0 if isinstance(g, int) and g < 0 else dma_total(parity, g // 2 + 1)

            @block.tensor
            def _(pe):
                def body(g, r):
                    turn, make, out1, out2, mlp, fin = g + 2, g + 1, g - 1, g - 2, g - 3, g - 4
                    qk_of = turn if cosine else make

                    def use_after_norms(bank):
                        if cosine:
                            pe.wait_ge(did["sq_norm"], upto(make))
                        elif bank == 0:
                            pe.wait_ge(did["q_read"], upto(g))
                        else:
                            pe.wait_ge(did["k_read"], upto(g))

                    for slot in range(PAIRS):
                        if exists(g, groups):
                            pe.wait_ge(did["q_band"], upto(g))
                            pe.wait_ge(did["k_heads"], upto(g, slot, PAIRS))
                            ug, us = before(g, slot, 1 if SB == 2 else 2)
                            for bank in range(SB):
                                pe.wait_ge(did[f"score_read{bank}"], upto(ug, us, PAIRS))
                                for band, j0, nj, at_bank, col in cfg.score_parts:
                                    if at_bank != bank:
                                        continue
                                    for half in range(2):
                                        w = 2 * slot + half
                                        last = nc.tensor.matmul(
                                            psS[half * HALF:half * HALF + HALF, bank if SB == 2 else slot % 2,
                                                col:col + nj * WIN],
                                            q_band[:, r % 2, band, w * WIN:w * WIN + HALF],
                                            k_heads[:, r % 2, w, j0 * WIN:(j0 + nj) * WIN], start=True, stop=True)
                                last.then_inc(did[f"scored{bank}"], 1)
                        if slot == 0 and exists(out2, groups):
                            pe.wait_ge(did["mixedT"], upto(out2))
                            use_after_norms(0)
                            pe.wait_ge(did["hid"], upto(fin, 2, CHUNKS))
                            rows = DIM + 1 if cosine else DIM
                            for w in range(WINDOWS):
                                at, p = w % 2 * HALF, w // 2
                                last = nc.tensor.matmul(psM[at:at + HALF, 0, p * DIM:(p + 1) * DIM],
                                                        mixedT[0:rows, w * WIN:w * WIN + HALF],
                                                        w_proj[0:rows, :], start=True, stop=True)
                            last.then_inc(did["proj_made"], 1)
                        if slot == 0 and exists(fin, groups):
                            pe.wait_ge(did["hid"], upto(fin, 2, CHUNKS))
                            use_after_norms(1)
                            for p in range(PAIRS):
                                for c in range(CHUNKS):
                                    for half in range(2):
                                        first = (2 * p + half) * WIN
                                        last = nc.tensor.matmul(
                                            psM[half * HALF:(half + 1) * HALF, 1, p * DIM:(p + 1) * DIM],
                                            hid[:, c, first:first + HALF],
                                            w_fc2[:, c, :], start=(c == 0), stop=(c == CHUNKS - 1))
                            last.then_inc(did["fc2_made"], 1)
                        if slot == 1 and exists(mlp, groups):
                            pe.wait_ge(did["x1T"], upto(mlp))
                            pe.wait_ge(did["fc2_read"], upto(fin))
                            use_after_norms(1)
                            nc.tensor.matmul(psM[:, 1, 0:NT], w_fc1[:, 0:128], x1T[:, :],
                                             start=True, stop=True).then_inc(did["fc1_made"], 1)
                        if slot == 1 and exists(turn, groups):
                            if cosine:
                                pe.wait_ge(s_load[r % 2], moved(turn, r % 2))
                            else:
                                pe.wait_ge(did["x_norm"], upto(turn))
                            pe.wait_ge(did["x1T"], upto(mlp))
                            pe.wait_ge(did["mixedT"], upto(out2))
                            pe.wait_ge(did["xT"], upto(make))
                            for p in range(PAIRS):
                                rows = x_in[:, r % 2, p, :] if cosine else x_norm[:, p, :]
                                last = nc.tensor.transpose(psT[0:DIM, p * 128:(p + 1) * 128], rows, ident[:, :])
                            last.then_inc(did["x_turned"], 1)
                        if slot == 2 and exists(out1, groups):
                            pe.wait_ge(did["mixed"], upto(out1, 1, 2))
                            pe.wait_ge(did["x1T"], upto(mlp))
                            pe.wait_ge(did["xT"], upto(turn))
                            for p in range(PAIRS):
                                last = nc.tensor.transpose(psT[0:DIM, p * 128:(p + 1) * 128], mixed[:, p, :], ident[:, :])
                            last.then_inc(did["mixed_turned"], 1)
                        if slot == 2 and exists(qk_of, groups):
                            at = (r + (0 if cosine else 1)) % 2
                            pe.wait_ge(did["xT"], upto(qk_of))
                            pe.wait_ge(did["hid"], upto(mlp, 1, CHUNKS))
                            pe.wait_ge(did["fc2_read"], upto(fin))
                            use_after_norms(1)
                            nc.tensor.matmul(psM[0:DIM, 1, 0:NT], w_qkv[0:DIM, DIM:2 * DIM], xT[0:DIM, at, 0:NT],
                                             start=True, stop=True).then_inc(did["k_made"], 1)
                            pe.wait_ge(did["hid"], upto(mlp, 2, CHUNKS))
                            pe.wait_ge(did["v_heads"], upto(make))
                            pe.wait_ge(did["proj_read"], upto(out2))
                            nc.tensor.matmul(psM[0:DIM, 0, 0:NT], w_qkv[0:DIM, 0:DIM], xT[0:DIM, at, 0:NT],
                                             start=True, stop=True).then_inc(did["q_made"], 1)
                        ag, as_ = before(g, slot, 2)
                        if exists(ag, groups):
                            pe.wait_ge(did["v_heads"], upto(ag))
                            pe.wait_ge(did["probT"], upto(ag, as_, PAIRS))
                            if as_ % 2 == 0:
                                mg, ms = before(ag, as_, 2)
                                pe.wait_ge(did["mixed"], upto(mg, ms // 2, 2))
                            at = (r + (0 if slot >= 2 else 1)) % 2
                            for hp in range(HP):
                                last = nc.tensor.matmul(
                                    psO[:, (as_ % 2) * 2 * DIM:(as_ % 2 + 1) * 2 * DIM]
                                    .rearrange("r (h n) -> r h n", h=HP)[:, hp, :],
                                    probT[:, as_ % 2, hp * 128:(hp + 1) * 128],
                                    v_heads[:, at, as_, hp].rearrange("r v o d -> r (v o d)"), start=True, stop=True)
                            last.then_inc(did["mixed_made"], 1)
                        if slot == 3 and exists(out2, groups):
                            pe.wait_ge(did["x1" if cosine else "x1_norm"], upto(out2))
                            pe.wait_ge(did["mixedT"], upto(out1))
                            pe.wait_ge(did["xT"], upto(turn))
                            for p in range(PAIRS):
                                rows = x1[:, p, :] if cosine else x1_norm[:, p, :]
                                last = nc.tensor.transpose(psT[0:DIM, p * 128:(p + 1) * 128], rows, ident[:, :])
                            last.then_inc(did["x1_turned"], 1)
                        if slot == 3 and cosine and exists(turn, groups):
                            pe.wait_ge(did["qk_sq"], upto(turn))
                            pe.wait_ge(did["q_read"], upto(turn))
                            pe.wait_ge(did["k_read"], upto(turn))
                            for n in range(2):
                                last = nc.tensor.matmul(psM[0:DIM, n, 0:NT], same_head[:, :], qk_sq[:, n, :],
                                                        start=True, stop=True)
                            last.then_inc(did["norms_made"], 1)
                        if slot == 1 and exists(make, groups):
                            pe.wait_ge(did["xT"], upto(make))
                            pe.wait_ge(did["proj_read"], upto(out2))
                            use_after_norms(0)
                            for w in range(WINDOWS):
                                for odd in range(2):
                                    cols = w_qkv[:, 2 * DIM:3 * DIM].rearrange("c (h o d) -> c h o d", o=2, d=D)[:, :, odd, :]
                                    out = psM[odd * HALF:(odd + 1) * HALF, 0, 0:WINDOWS * HP * D]\
                                        .rearrange("r (p h v d) -> r p h v d", p=PAIRS, h=HP, v=2)[:, w // 2, :, w % 2, :]
                                    last = nc.tensor.matmul(out, xT[:, (r + 1) % 2, w * WIN:w * WIN + HALF], cols,
                                                            start=True, stop=True)
                            last.then_inc(did["v_made"], 1)
                        if slot == 1 and exists(mlp, groups):
                            pe.wait_ge(did["hid"], upto(mlp, 0, CHUNKS))
                            nc.tensor.matmul(psM[:, 1, 0:NT], w_fc1[:, 128:256], x1T[:, :],
                                             start=True, stop=True).then_inc(did["fc1_made"], 1)
                        tg, ts = before(g, slot, 1)
                        if exists(tg, groups):
                            pe.wait_ge(did["prob"], upto(tg, ts, PAIRS))
                            rg, rs = before(tg, ts, 1 if HP > 3 else 2)
                            pe.wait_ge(did["probT"], upto(rg, rs, PAIRS))
                            for hp in range(HP):
                                bank = hp // 3 if HP > 3 else ts % 2
                                last = nc.tensor.transpose(psP[:, bank, hp % 3 * 128:hp % 3 * 128 + 128],
                                                           prob[:, ts % 2, 2 * hp:2 * hp + 2, :].rearrange("p h k -> p (h k)"),
                                                           ident[:, :])
                            last.then_inc(did["prob_turned"], 1)
                        if slot == 1 and exists(mlp, groups):
                            pe.wait_ge(did["v_heads"], upto(make))
                            pe.wait_ge(did["proj_read"], upto(out2))
                            nc.tensor.matmul(psM[:, 0, 0:NT], w_fc1[:, 256:384], x1T[:, :],
                                             start=True, stop=True).then_inc(did["fc1_made"], 1)

                run_groups(pe, groups, body)

            @block.scalar
            def _(act):
                def body(g, r):
                    turn, make, out1, out2, mlp, fin = g + 2, g + 1, g - 1, g - 2, g - 3, g - 4

                    def gelu(c):
                        if exists(mlp, groups):
                            act.wait_ge(did["fc1_made"], upto(mlp, c, CHUNKS))
                            act.wait_ge(did["fc2_made"], upto(fin))
                            nc.scalar.activation(hid[:, c, 0:NT], psM[:, 1 if c < 2 else 0, 0:NT], ACT.Gelu,
                                                 bias=b_fc1[:, c:c + 1]).then_inc(did["hid"], 1)

                    for slot in range(PAIRS):
                        tg, ts = before(g, slot, 2)
                        if exists(tg, groups):
                            act.wait_ge(did["prob_turned"], upto(tg, ts, PAIRS))
                            fg, fs = before(tg, ts, 2)
                            act.wait_ge(did["mixed_made"], upto(fg, fs, PAIRS))
                            if HP > 3:
                                frm = psP[:, :, 0:384]
                                to = probT[:, ts % 2, :].rearrange("p (b q) -> p b q", b=2)
                            else:
                                frm = psP[:, ts % 2, 0:384]
                                to = probT[:, ts % 2, :]
                            nc.scalar.activation(to, frm, ACT.Copy).then_inc(did["probT"], 1)
                        if slot == 2:
                            gelu(2)
                            act.preload_act_table_set(EXP_SET)
                        eg, es = before(g, slot, 1)
                        if exists(eg, groups):
                            act.wait_ge(did["shifted"], upto(eg, es, PAIRS))
                            fg, fs = before(eg, es, 2)
                            act.wait_ge(did["prob_turned"], upto(fg, fs, PAIRS))
                            act.wait_ge(did["total"], upto(fg, fs, PAIRS))
                            nc.scalar.activation(prob[:, es % 2, :, 0:WIN],
                                                 score[:, es % 2, :].rearrange("p (h k) -> p h k", k=WIN),
                                                 ACT.Exp).then_inc(did["prob"], 1)
                        if slot == 0 and cosine:
                            if exists(make, groups):
                                act.wait_ge(did["sq_norm"], upto(make))
                                nc.scalar.activation(sq_norm[:, :, :], sq_norm[:, :, :], ACT.Ln).then_inc(did["log_norm"], 1)
                                act.wait_ge(did["log_norm"], upto(make))
                                nc.scalar.activation(sq_norm[:, :, :], sq_norm[:, :, :], ACT.Exp,
                                                     scale=-0.5).then_inc(did["inv_norm"], 1)
                            if exists(out2, groups):
                                act.wait_ge(did["proj_made"], upto(out2))
                                act.wait_ge(did["y_ln"], upto(mlp))
                                act.wait_ge(did["y_var"], upto(mlp))
                                made = psM[:, 0, 0:PAIRS * DIM]
                                nc.scalar.activation(y[:, :, :].rearrange("p n c -> p (n c)"), made, ACT.Copy)
                                nc.scalar.activation(y_sq[:, :, :].rearrange("p n c -> p (n c)"), made, ACT.Square,
                                                     scale=DIM ** -0.5).then_inc(did["proj_read"], 1)
                        if slot == 1:
                            act.preload_act_table_set(GELU_SET)
                            if exists(turn, groups):
                                act.wait_ge(did["x_turned"], upto(turn))
                                act.wait_ge(did["v_made"], upto(g))
                                act.wait_ge(did["k_made"], upto(g))
                                nc.scalar.activation(xT[0:DIM, r % 2, 0:NT].rearrange("p (w t) -> p w t", t=WIN),
                                                     windows_of(psT[0:DIM, :], WIN), ACT.Copy).then_inc(did["xT"], 1)
                            if cosine and exists(fin, groups):
                                act.wait_ge(did["fc2_read"], upto(fin))
                                act.wait_ge(did["z_var"], upto(g - 5))
                                nc.scalar.activation(z_sq[:, :, :], z[:, :, :], ACT.Square,
                                                     scale=DIM ** -0.5).then_inc(did["z_sq"], 1)
                            gelu(0)
                            if exists(make, groups):
                                act.wait_ge(did["v_made"], upto(make))
                                act.wait_ge(did["mixed_made"], upto(g - 1, PAIRS - 1, PAIRS))
                                for odd in range(2):
                                    rows = slice(odd * HALF, (odd + 1) * HALF)
                                    last = nc.scalar.activation(
                                        v_heads[rows, (r + 1) % 2].rearrange("r p h v o d -> r (p h v) o d")[:, :, odd, :],
                                        psM[rows, 0, 0:WINDOWS * HP * D].rearrange("r (n d) -> r n d", d=D), ACT.Copy)
                                last.then_inc(did["v_heads"], 1)
                            gelu(1)
                        if slot == 2:
                            if exists(out1, groups):
                                act.wait_ge(did["mixed_turned"], upto(out1))
                                act.wait_ge(did["proj_made"], upto(out2))
                                nc.scalar.activation(mixedT[0:DIM, 0:NT].rearrange("p (w t) -> p w t", t=WIN),
                                                     windows_of(psT[0:DIM, :], WIN), ACT.Copy).then_inc(did["mixedT"], 1)
                            if not cosine and exists(make, groups):
                                act.wait_ge(did["k_made"], upto(make))
                                act.wait_ge(did["k_heads"], upto(g, PAIRS - 1, PAIRS))
                                nc.scalar.activation(k_hat[:, :], psM[0:DIM, 1, 0:NT], ACT.Identity,
                                                     bias=b_qk[:, 1:2]).then_inc(did["k_hat"], 1)
                        if slot == 3:
                            if cosine and exists(turn, groups):
                                act.wait_ge(did["q_read"], upto(turn))
                                act.wait_ge(did["norms_made"], upto(make))
                                nc.scalar.activation(qk_sq[:, :, :], qk[:, :, :], ACT.Square).then_inc(did["qk_sq"], 1)
                            if exists(out2, groups):
                                act.wait_ge(did["x1_turned"], upto(out2))
                                act.wait_ge(did["fc1_made"], upto(mlp, 2, CHUNKS))
                                nc.scalar.activation(x1T[:, :].rearrange("p (w t) -> p w t", t=WIN),
                                                     windows_of(psT[0:DIM, :], WIN), ACT.Copy).then_inc(did["x1T"], 1)

                run_groups(act, groups, body)

            @block.vector
            def _(dve):
                def body(g, r):
                    turn, make, out1, out2, mlp, fin = g + 2, g + 1, g - 1, g - 2, g - 3, g - 4
                    for slot in range(PAIRS):
                        if slot == 1 and not cosine and exists(out2, groups):
                            dve.wait_ge(did["moments2"], upto(mlp))
                            dve.wait_ge(did["x1"], upto(out2))
                            for p in range(PAIRS):
                                last = nc.vector.bn_stats(stats2[:, p, :], x1[:, p, :])
                            last.then_inc(did["stats2"], 1)
                            dve.wait_ge(did["stats2"], upto(out2))
                            dve.wait_ge(did["var_eps2"], upto(mlp))
                        if slot == 3 and not cosine and exists(g + 3, groups):
                            dve.wait_ge(s_load[(r + 1) % 2], moved(g + 3, (r + 1) % 2))
                            for p in range(PAIRS):
                                last = nc.vector.bn_stats(stats[:, p, :], x_in[:, (r + 1) % 2, p, :])
                            last.then_inc(did["stats"], 1)
                            dve.wait_ge(did["stats"], upto(g + 3))
                            dve.wait_ge(did["x_norm"], upto(turn))
                        if exists(g, groups):
                            half = slot % 2
                            hg, hs = before(g, slot, 2)
                            dve.wait_ge(did["prob"], upto(hg, hs, PAIRS))
                            heads_view = score[:, half, :].rearrange("p (h k) -> p h k", k=WIN)
                            if cosine:
                                for bank in range(SB):
                                    dve.wait_ge(did[f"scored{bank}"], upto(g, slot, PAIRS))
                                    cols = slice(bank * SBC, (bank + 1) * SBC)
                                    kind = bias_tab[:, bass.ds((g % 8) // 7, 1), slot // 3, cols]
                                    nc.vector.tensor_tensor(score[:, half, cols], psS[:, bank, 0:SBC],
                                                            kind.rearrange("p o n -> p (o n)"), ALU.add)\
                                        .then_inc(did[f"score_read{bank}"], 1)
                                dve.wait_ge(did["score_read1"], upto(g, slot, PAIRS))
                                nc.vector.tensor_reduce(top[:, half, :], heads_view, AX.X, ALU.max).then_inc(did["top"], 1)
                            else:
                                dve.wait_ge(did["scored0"], upto(g, slot, PAIRS))
                                from_psum = psS[:, half, 0:SC].rearrange("p (h k) -> p h k", k=WIN)
                                nc.vector.tensor_reduce(top[:, half, :], from_psum, AX.X, ALU.max).then_inc(did["top"], 1)
                                dve.wait_ge(did["top"], upto(g, slot, PAIRS))
                                nc.vector.tensor_tensor(heads_view, from_psum, bcast(top[:, half, :], 2, WIN),
                                                        ALU.subtract).then_inc(did["shifted"], 1)
                        if slot == 1 and not cosine and exists(out2, groups):
                            for p in range(PAIRS):
                                last = nc.vector.bn_aggr(moments2[:, p, :], stats2[:, p, :])
                            last.then_inc(did["moments2"], 1)
                        if slot == 3 and not cosine and exists(g + 3, groups):
                            for p in range(PAIRS):
                                last = nc.vector.bn_aggr(moments[:, p, :], stats[:, p, :])
                            last.then_inc(did["moments"], 1)
                        tg, ts = before(g, slot, 1)
                        if exists(tg, groups):
                            dve.wait_ge(did["prob"], upto(tg, ts, PAIRS))
                            nc.vector.tensor_reduce(total[:, ts, :], prob[:, ts % 2, :, 0:WIN], AX.X, ALU.add)\
                                .then_inc(did["total"], 1)
                        if slot == 0 and not cosine and exists(turn, groups):
                            dve.wait_ge(did["rstd"], upto(turn))
                            dve.wait_ge(did["x_turned"], upto(make))
                            for p in range(PAIRS):
                                last = nc.vector.tensor_scalar(x_norm[:, p, :], x_in[:, r % 2, p, :], moments[:, p, 0:1],
                                                               rstd[:, p:p + 1], ALU.subtract, ALU.mult)
                            last.then_inc(did["x_norm"], 1)
                        if slot == 0 and exists(fin, groups):
                            dve.wait_ge(did["fc2_made"], upto(fin))
                            out_of = psM[:, 1, 0:PAIRS * DIM].rearrange("p (n c) -> p n c", c=DIM)
                            if cosine:
                                dve.wait_ge(did["z_ln"], upto(g - 5))
                                dve.wait_ge(did["z_sq"], upto(g - 5))
                                nc.vector.tensor_tensor(z[:, :, :], out_of, bcast(row_fc2[:, :], 1, PAIRS),
                                                        ALU.add).then_inc(did["fc2_read"], 1)
                            else:
                                dve.wait_ge(did["x1_res"], upto(fin))
                                dve.wait_ge(s_store[r % 2], moved(fin - 2, r % 2))
                                nc.vector.tensor_tensor(x2[:, r % 2], out_of, x1_res[:, r % 4],
                                                        ALU.add).then_inc(did["x2"], 1)
                        if slot == 0 and not cosine and exists(out2, groups):
                            dve.wait_ge(did["proj_made"], upto(out2))
                            dve.wait_ge(did["x_res"], upto(out2))
                            dve.wait_ge(did["x1_norm"], upto(mlp))
                            dve.wait_ge(did["x1_res"], upto(mlp))
                            nc.vector.tensor_tensor(x1[:, :, :], psM[:, 0, 0:PAIRS * DIM]
                                                    .rearrange("p (n c) -> p n c", c=DIM), x_res[:, (r + 2) % 4],
                                                    ALU.add).then_inc(did["x1"], 1)
                        if slot == 1 and cosine:
                            if exists(make, groups):
                                dve.wait_ge(did["inv_norm"], upto(make))
                                dve.wait_ge(did["scored1"], upto(g - 1, PAIRS - 1, PAIRS))
                                dve.wait_ge(did["k_heads"], upto(g, PAIRS - 1, PAIRS))
                                nc.vector.tensor_tensor(k_hat[:, :], qk[:, 1, :], sq_norm[:, 1, :], ALU.mult)\
                                    .then_inc(did["k_hat"], 1)
                                for band in range(BANDS):
                                    rows = slice(32 * band, 32 * band + 32)
                                    last = nc.vector.tensor_tensor(q_band[rows, (r + 1) % 2, band, 0:NT], qk[rows, 0, :],
                                                                   sq_norm[rows, 0, :], ALU.mult)
                                last.then_inc(did["q_band"], 1)
                            if exists(out2, groups):
                                dve.wait_ge(did["proj_read"], upto(out2))
                                dve.wait_ge(did["y_eps"], upto(mlp))
                                nc.vector.tensor_reduce(y_var[:, :], y_sq[:, :, :], AX.X, ALU.add).then_inc(did["y_var"], 1)
                            if exists(fin, groups):
                                dve.wait_ge(did["z_sq"], upto(fin))
                                dve.wait_ge(did["z_eps"], upto(g - 5))
                                nc.vector.tensor_reduce(z_var[:, :], z_sq[:, :, :], AX.X, ALU.add).then_inc(did["z_var"], 1)
                        if slot == 2 and cosine:
                            if exists(out2, groups):
                                dve.wait_ge(did["y_rstd"], upto(out2))
                                dve.wait_ge(did["x1"], upto(mlp))
                                for p in range(PAIRS):
                                    last = nc.vector.scalar_tensor_tensor(y_ln[:, p, :], y[:, p, :], y_rstd[:, p:p + 1],
                                                                          gain1[:, :], ALU.mult, ALU.mult)
                                last.then_inc(did["y_ln"], 1)
                            if exists(turn, groups):
                                dve.wait_ge(did["q_band"], upto(make))
                                dve.wait_ge(did["qk_sq"], upto(make))
                                for n, name in ((1, "k"), (0, "q")):
                                    dve.wait_ge(did[f"{name}_made"], upto(turn))
                                    nc.vector.tensor_scalar(qk[:, n, :], psM[0:DIM, n, 0:NT], b_qk[:, n:n + 1],
                                                            None, ALU.add).then_inc(did[f"{name}_read"], 1)
                        if slot == 2 and not cosine:
                            if exists(out2, groups):
                                dve.wait_ge(did["rstd2"], upto(out2))
                                dve.wait_ge(did["x1_turned"], upto(mlp))
                                for p in range(PAIRS):
                                    last = nc.vector.tensor_scalar(x1_norm[:, p, :], x1[:, p, :], moments2[:, p, 0:1],
                                                                   rstd2[:, p:p + 1], ALU.subtract, ALU.mult)
                                last.then_inc(did["x1_norm"], 1)
                            if exists(make, groups):
                                dve.wait_ge(did["q_made"], upto(make))
                                dve.wait_ge(did["scored0"], upto(g - 1, PAIRS - 1, PAIRS))
                                for band in range(BANDS):
                                    rows = slice(32 * band, 32 * band + 32)
                                    last = nc.vector.tensor_scalar(q_band[rows, (r + 1) % 2, band, 0:NT],
                                                                   psM[rows, 0, 0:NT], b_qk[rows, 0:1], None, ALU.add)
                                last.then_inc(did["q_band"], 1)
                        if slot == 3 and cosine:
                            if exists(turn, groups):
                                dve.wait_ge(did["norms_made"], upto(turn))
                                dve.wait_ge(did["q_band"], upto(make))
                                nc.vector.tensor_scalar(sq_norm[:, :, :], psM[0:DIM, :, 0:NT], 1e-6, None,
                                                        ALU.max).then_inc(did["sq_norm"], 1)
                            if exists(fin, groups):
                                dve.wait_ge(did["z_rstd"], upto(fin))
                                dve.wait_ge(did["x2"], upto(g - 5))
                                for p in range(PAIRS):
                                    last = nc.vector.scalar_tensor_tensor(z_ln[:, p, :], z[:, p, :], z_rstd[:, p:p + 1],
                                                                          gain2[:, :], ALU.mult, ALU.mult)
                                last.then_inc(did["z_ln"], 1)
                        mg, ms = before(g, slot, 2)
                        if ms % 2 == 1 and exists(mg, groups):
                            dve.wait_ge(did["total"], upto(mg, ms, PAIRS))
                            dve.wait_ge(did["mixed"], upto(mg - 1, ms // 2, 2))
                            nc.vector.reciprocal(inv_total[:, ms - 1:ms + 1, :], total[:, ms - 1:ms + 1, :])\
                                .then_inc(did["inv_total"], 1)
                            dve.wait_ge(did["inv_total"], upto(mg, ms // 2, 2))
                            dve.wait_ge(did["mixed_made"], upto(mg, ms, PAIRS))
                            dve.wait_ge(did["mixed_turned"], upto(mg - 1))
                            for half in range(2):
                                rows = slice(half * HALF, (half + 1) * HALF)
                                made = psO[rows, 0:4 * DIM].rearrange("r (n v o d) -> r n v o d", v=2, o=2, d=D)[:, :, half]
                                inv = inv_total[rows, ms - 1:ms + 1, :].rearrange("r p (h o) -> r (p h) o", o=2)
                                out = mixed[rows, ms - 1:ms + 1, :].rearrange("r p (h o d) -> r (p h) o d", o=2, d=D)
                                last = nc.vector.tensor_tensor(out, made, bcast(inv, 3, D), ALU.mult)
                            last.then_inc(did["mixed"], 1)

                run_groups(dve, groups, body)

            @block.gpsimd
            def _(pool):
                def body(g, r):
                    turn, make, out1, out2, mlp, fin = g + 2, g + 1, g - 1, g - 2, g - 3, g - 4
                    for slot in range(PAIRS):
                        if cosine and exists(g, groups):
                            half = slot % 2
                            pool.wait_ge(did["top"], upto(g, slot, PAIRS))
                            view = score[:, half, :].rearrange("p (h k) -> p h k", k=WIN)
                            nc.gpsimd.tensor_tensor(view, view, bcast(top[:, half, :], 2, WIN), ALU.subtract)\
                                .then_inc(did["shifted"], 1)
                        if slot == 0 and exists(make, groups):
                            pool.wait_ge(s_load[(r + 1) % 2], moved(make, (r + 1) % 2))
                            pool.wait_ge(did["x1"], upto(mlp))
                            nc.gpsimd.tensor_tensor(x_res[:, (r + 1) % 4], x_in[:, (r + 1) % 2],
                                                    bcast(res_row1[:, :], 1, PAIRS), ALU.add).then_inc(did["x_res"], 1)
                        if slot == 0 and cosine and exists(g - 5, groups):
                            pool.wait_ge(did["z_ln"], upto(g - 5))
                            pool.wait_ge(did["x1_res"], upto(g - 5))
                            pool.wait_ge(s_store[(r + 1) % 2], moved(g - 7, (r + 1) % 2))
                            nc.gpsimd.tensor_tensor(x2[:, (r + 1) % 2], z_ln[:, :, :], x1_res[:, (r + 3) % 4], ALU.add)\
                                .then_inc(did["x2"], 1)
                        if slot == 1 and exists(out2, groups):
                            if cosine:
                                pool.wait_ge(did["y_var"], upto(out2))
                                pool.wait_ge(did["y_rstd"], upto(mlp))
                                nc.gpsimd.tensor_tensor(y_eps[:, :], y_var[:, :], epsilon[:, :], ALU.add)\
                                    .then_inc(did["y_eps"], 1)
                                pool.wait_ge(did["y_eps"], upto(out2))
                                pool.wait_ge(did["y_ln"], upto(mlp))
                                nc.gpsimd.tensor_tensor(y_rstd[:, :], y_eps[:, :], half_power[:, :], ALU.pow)\
                                    .then_inc(did["y_rstd"], 1)
                            else:
                                pool.wait_ge(did["moments2"], upto(out2))
                                pool.wait_ge(did["rstd2"], upto(mlp))
                                nc.gpsimd.tensor_tensor(var_eps2[:, :], moments2[:, :, 1], epsilon[:, :], ALU.add)\
                                    .then_inc(did["var_eps2"], 1)
                                pool.wait_ge(did["var_eps2"], upto(out2))
                                pool.wait_ge(did["x1_norm"], upto(mlp))
                                nc.gpsimd.tensor_tensor(rstd2[:, :], var_eps2[:, :], half_power[:, :], ALU.pow)\
                                    .then_inc(did["rstd2"], 1)
                                pool.wait_ge(did["x2"], upto(g - 6))
                                pool.wait_ge(did["x1"], upto(out2))
                                nc.gpsimd.tensor_tensor(x1_res[:, (r + 2) % 4], x1[:, :, :],
                                                        bcast(row_fc2[:, :], 1, PAIRS), ALU.add).then_inc(did["x1_res"], 1)
                        if slot == 2 and cosine:
                            if exists(fin, groups):
                                pool.wait_ge(did["z_var"], upto(fin))
                                pool.wait_ge(did["z_rstd"], upto(g - 5))
                                nc.gpsimd.tensor_tensor(z_eps[:, :], z_var[:, :], epsilon[:, :], ALU.add)\
                                    .then_inc(did["z_eps"], 1)
                                pool.wait_ge(did["z_eps"], upto(fin))
                                pool.wait_ge(did["z_ln"], upto(g - 5))
                                nc.gpsimd.tensor_tensor(z_rstd[:, :], z_eps[:, :], half_power[:, :], ALU.pow)\
                                    .then_inc(did["z_rstd"], 1)
                        if slot == 2 and cosine and exists(out2, groups):
                            pool.wait_ge(did["y_ln"], upto(out2))
                            pool.wait_ge(did["x1_turned"], upto(mlp))
                            pool.wait_ge(did["x1_res"], upto(mlp))
                            pool.wait_ge(did["x_res"], upto(out2))
                            nc.gpsimd.tensor_tensor(x1[:, :, :], y_ln[:, :, :], x_res[:, (r + 2) % 4], ALU.add)\
                                .then_inc(did["x1"], 1)
                        if exists(make, groups) and slot in ((2, 3) if cosine else (3,)):
                            if slot == (2 if cosine else 3):
                                pool.wait_ge(did["k_hat"], upto(make))
                                pool.wait_ge(did[f"scored{SB - 1}"], upto(g - 1, PAIRS - 1, PAIRS))
                            for p in ((0, 1, 2, 3) if not cosine else (0, 1) if slot == 2 else (2, 3)):
                                for half in range(2):
                                    w = 2 * p + half
                                    last = nc.gpsimd.tensor_tensor(
                                        k_heads[0:DIM, (r + 1) % 2, w, :].rearrange("c (j k) -> c j k", j=J),
                                        bcast(k_hat[:, w * WIN:(w + 1) * WIN], 1, J),
                                        bcast(head_mask[:, :], 2, WIN), ALU.mult)
                                last.then_inc(did["k_heads"], 1)
                        if slot == 3 and cosine and exists(out2, groups):
                            pool.wait_ge(did["x2"], upto(g - 6))
                            pool.wait_ge(did["x1"], upto(out2))
                            nc.gpsimd.tensor_tensor(x1_res[:, (r + 2) % 4], x1[:, :, :],
                                                    bcast(res_row2[:, :], 1, PAIRS), ALU.add).then_inc(did["x1_res"], 1)
                        if slot == 3 and not cosine and exists(g + 3, groups):
                            pool.wait_ge(did["moments"], upto(g + 3))
                            pool.wait_ge(did["rstd"], upto(turn))
                            nc.gpsimd.tensor_tensor(var_eps[:, :], moments[:, :, 1], epsilon[:, :], ALU.add)\
                                .then_inc(did["var_eps"], 1)
                            pool.wait_ge(did["var_eps"], upto(g + 3))
                            pool.wait_ge(did["x_norm"], upto(turn))
                            nc.gpsimd.tensor_tensor(rstd[:, :], var_eps[:, :], half_power[:, :], ALU.pow)\
                                .then_inc(did["rstd"], 1)

                run_groups(pool, groups, body)


def two_blocks(nc, x, out, params, const):
    scratch = nc.dram_tensor("between_blocks", [IMAGES, SIDE, SIDE, DIM], F32, kind="Internal").ap()
    with ExitStack() as ctx:
        def pb(name, shape):
            return ctx.enter_context(nc.psum_tensor(name, shape, F32))

        psum = {"scores": pb("ps_scores", [128, 2, BANK]), "probs": pb("ps_probs", [128, 2, BANK]),
                "turn": pb("ps_turn", [128, BANK]), "dense": pb("ps_dense", [128, 2, BANK]),
                "mixed": pb("ps_mixed", [128, BANK])}
        block_program(nc, Swin, x, scratch, params["L0"], const, psum)
        block_program(nc, Plain, scratch, out, params["L1"], const, psum)


def shape_constants():
    def token(order, n):
        return (n % 7, n // 7) if order == 0 else (n // 7, n % 7)

    c = {"ident": np.eye(128, dtype=np.float32)}
    f = np.arange(DIM)
    c["same_head"] = (f[:, None] // 8 == f[None, :] // 8).astype(np.float32)
    c["pick"] = (np.arange(12)[:, None] == f[None, :] // 8).astype(np.float32)
    c["swin_head_mask"] = (f[:, None] % 32 // 8 == np.arange(4)[None, :]).astype(np.float32)
    c["plain_head_mask"] = (f[:, None] % 32 // 16 == np.arange(2)[None, :]).astype(np.float32)
    rel = np.zeros((2, 2, 49, 49), np.float32)
    mask = np.zeros((128, 2, 2, 49), np.float32)
    region = np.zeros((SIDE, SIDE))
    n = 0
    for hs in (slice(0, -7), slice(-7, -3), slice(-3, None)):
        for ws in (slice(0, -7), slice(-7, -3), slice(-3, None)):
            region[hs, ws] = n
            n += 1
    for order in range(2):
        at = np.array([token(order, n) for n in range(49)])
        d = (at[:, None, :] - at[None, :, :]).astype(np.float32)
        rel[:, order] = np.moveaxis(np.sign(d) * np.log1p(np.abs(d)), 2, 0)
        wy = 7 if order else 0
        for edge in range(2):
            for half in range(2):
                wx = 6 * edge + half
                r = region[wy * 7 + at[:, 0], wx * 7 + at[:, 1]]
                mask[half * HALF:half * HALF + 49, order, edge] = np.where(r[:, None] != r[None, :], -100.0, 0.0)
    c["rel"] = rel.reshape(2, 2, 49 * 49)
    c["mask"] = mask
    return c


_L0 = ["qkv_w", "qkv_b", "proj_w", "proj_b", "tau", "meta_w1", "meta_b1", "meta_w2", "meta_b2", "norm1_g", "norm1_b",
       "fc1_w", "fc1_b", "fc2_w", "fc2_b", "norm2_g", "norm2_b"]
_L1 = {"g1": "g1", "b1": "b1", "w_qkv": "qkv_w", "b_qkv": "qkv_b", "w_proj": "proj_w", "b_proj": "proj_b", "g2": "g2",
       "b2": "b2", "w_fc1": "fc1_w", "b_fc1": "fc1_b", "w_fc2": "fc2_w", "b_fc2": "fc2_b"}


def kernel(**inputs):
    import numpy as _np
    import concourse.bacc as _bacc
    from concourse import mybir as _mybir
    from concourse.bass_utils import run_bass_kernel_spmd as _run

    nc = _bacc.Bacc("TRN2", target_bir_lowering=False, num_devices=1)
    arrays = {}

    def give(name, a):
        a = _np.ascontiguousarray(a)
        arrays[f"in_{name}"] = a
        return nc.dram_tensor(f"in_{name}", a.shape, _mybir.dt.from_np(a.dtype), kind="ExternalInput").ap()

    x = give("x", inputs["x"])
    params = {"L0": {k: give(f"L0_{k}", inputs[f"L0_conv_{k}"]) for k in _L0},
              "L1": {v: give(f"L1_{k}", inputs[f"L1_conv_{k}"]) for k, v in _L1.items()}}
    const = {k: give(f"const_{k}", v) for k, v in shape_constants().items()}
    out = nc.dram_tensor("out_0_dram", (IMAGES, SIDE, SIDE, DIM), _mybir.dt.float32, kind="ExternalOutput").ap()
    two_blocks(nc, x, out, params, const)
    r = _run(nc, [arrays], core_ids=[0])
    return r.results[0]["out_0_dram"]
```

```python
from contextlib import ExitStack

import numpy as np
import concourse.bass as bass
from concourse import mybir

F32 = mybir.dt.float32
F32R = mybir.dt.float32r
ALU = mybir.AluOpType
ACT = mybir.ActivationFunctionType
AX = mybir.AxisListType

IMAGES, SIDE, DIM, HIDDEN = 32, 56, 96, 384
PAIRS = 4
WINDOWS = 2 * PAIRS
HALF = 64
CHUNKS = HIDDEN // 128
BANDS = 3
BANK = 512
EXP_SET = "natural_log_exp_and_others"
GELU_SET = "gelu_and_others"


class Swin:
    name, win, heads, shift, eps = "swin", 7, 12, 3, 1e-5
    groups = IMAGES * (SIDE // 7) * (SIDE // 7) // WINDOWS
    cosine = True
    score_banks = 2
    score_parts = [(0, 0, 4, 0, 0), (1, 0, 2, 0, 196), (1, 2, 2, 1, 0), (2, 0, 4, 1, 98)]


class Plain:
    name, win, heads, shift, eps = "plain", 8, 6, 0, 1e-6
    groups = IMAGES * (SIDE // 8) * (SIDE // 8) // WINDOWS
    cosine = False
    score_banks = 1
    score_parts = [(0, 0, 2, 0, 0), (1, 0, 2, 0, 128), (2, 0, 2, 0, 256)]


STEPS = {
    "setup_zeroed": "buffers cleared", "setup_loaded": "weights in SBUF", "setup_vector": "vector engine's set-up steps",
    "setup_products": "tensor engine's set-up steps", "setup_scalar": "scalar engine's set-up steps",
    "setup_hidden": "a part of the bias network's hidden layer is in PSUM",
    "x_loaded_even": "windows of an even group are in x_in", "x_loaded_odd": "windows of an odd group are in x_in",
    "x2_stored_even": "an even group's result is in DRAM", "x2_stored_odd": "an odd group's result is in DRAM",
    "stats": "partial moments of x_in", "moments": "mean and variance of x_in", "var_eps": "variance + epsilon",
    "rstd": "its power -1/2", "x_centred": "input less its mean", "x_norm": "normalised input", "x_res": "input + constant row",
    "x_turned": "input is feature-major in psT", "xT": "... and in SBUF, with its high part", "xT_low": "its low part",
    "q_made": "queries in dense bank 0", "k_made": "keys in dense bank 1",
    "q_read": "dense bank 0 read", "k_read": "dense bank 1 read",
    "qk_sq": "squares of queries and keys", "norms_made": "squared norms in the dense banks",
    "sq_norm": "squared norms with their floor in SBUF", "log_norm": "their logarithm", "inv_norm": "1 / norm",
    "q_band0": "first band of the plain block's queries", "q_band": "queries, one copy to a band, other bands zero", "k_hat": "keys ready to be spread over heads",
    "k_heads": "keys spread over heads, for one pair", "v_made": "values in dense bank 0", "v_heads": "... and in SBUF",
    "scored0": "scores in their first bank", "scored1": "scores in their second bank",
    "score_read0": "first score bank read", "score_read1": "second score bank read",
    "top": "greatest score of each query and head", "shifted": "scores less their top",
    "prob": "exponentials",
    "prob_turned": "exponentials turned in psP", "probT": "... and in SBUF",
    "mixed_made": "a pair's exponentials times values, and their sums, in psO",
    "inv_total": "1 / sum, for two pairs", "mixedT": "two pairs' attention output, feature-major in SBUF",
    "proj_made": "projection in dense bank 0", "proj_read": "... and read",
    "y_ln": "normalised projection", "y_var": "variance", "y_eps": "+ epsilon", "y_rstd": "power -1/2",
    "x1": "first residual", "x1_res": "x1 + constant row", "stats2": "partial moments of x1",
    "moments2": "mean and variance of x1", "var_eps2": "+ epsilon", "rstd2": "power -1/2", "x1_norm": "normalised x1",
    "x1_turned": "MLP input feature-major in psT", "x1T": "its high part in SBUF", "x1T_low": "its low part",
    "fc1_made": "a chunk of the hidden layer in a dense bank", "hid": "GELU of a chunk in SBUF",
    "fc2_made": "MLP output in dense bank 1", "fc2_read": "... and read",
    "z_sq": "squares of the MLP output", "z_var": "variance", "z_eps": "+ epsilon", "z_rstd": "power -1/2",
    "z_ln": "normalised MLP output", "x2": "the block's result",
}


def bcast(ap, axis, count):
    dims = [list(d) for d in ap.ap]
    dims.insert(axis, [0, count])
    return bass.AP(ap.tensor, ap.offset, dims)


def count_for(group, index, per_group, groups):
    if isinstance(group, int):
        if group < 0:
            return 0
        if group >= groups:
            group, index = groups - 1, per_group - 1
    return group * per_group + (index + 1)


def before(group, slot, lag):
    while slot < lag:
        group, slot = group - 1, slot + PAIRS
    return group, slot - lag


def exists(group, groups):
    return not isinstance(group, int) or 0 <= group < groups


def run_groups(engine, groups, body):
    for g in range(-3, 8):
        body(g, g % 4)
    with engine.Fori(2, groups // 4 - 1) as m:
        for r in range(4):
            body(4 * m + r, r)
    for g in range(groups - 4, groups + 5):
        body(g, g % 4)


def block_program(nc, cfg, src, dst, par, const, psum):
    win, heads, groups = cfg.win, cfg.heads, cfg.groups
    WIN = win * win
    NT = WINDOWS * WIN
    NTP = NT + 16
    D = DIM // heads
    J = 32 // D
    HP = heads // 2
    SC = heads * WIN
    cosine = cfg.cosine
    SB = cfg.score_banks
    SBC = SC // SB
    TT = 2 * WIN
    QT = HALF + WIN
    HB = J // 2
    SUMS = 2 * HALF * 2

    ctx = ExitStack()
    with ctx:
        def sb(name, shape, dtype=F32):
            return ctx.enter_context(nc.sbuf_tensor(f"{cfg.name}_{name}", shape, dtype))

        did = {name: ctx.enter_context(nc.semaphore(f"{cfg.name}_{name}")) for name in STEPS}
        if not cosine:
            did.update(q_read=did["q_band"], k_read=did["k_hat"], score_read0=did["shifted"],
                       proj_read=did["x1"], fc2_read=did["x2"])

        def upto(group, index=0, per=1):
            return count_for(group, index, per, groups)

        psS = psum["scores"]
        psP = psum["probs"]
        psT = psum["turn"]
        psM = psum["dense"]
        psO = psum["mixed"]

        ident = sb("ident", [128, 128])
        w_qkv = sb("w_qkv", [128, 3 * DIM])
        w_qk_high = sb("w_qk_high", [DIM, 2 * DIM], F32R)
        w_qk_low = sb("w_qk_low", [DIM, 2 * DIM], F32R)
        w_fc1_high = sb("w_fc1_high", [DIM, HIDDEN], F32R)
        w_fc1_low = sb("w_fc1_low", [DIM, HIDDEN], F32R)
        b_qk = sb("b_qk", [DIM, 2])
        w_proj = sb("w_proj", [DIM + 1, DIM])
        w_fc1 = sb("w_fc1", [DIM, HIDDEN])
        b_fc1 = sb("b_fc1", [128, CHUNKS])
        w_fc2 = sb("w_fc2", [128, CHUNKS, DIM])
        row_fc2 = sb("row_fc2", [128, DIM])
        head_mask = sb("head_mask", [DIM, J])
        mean_row = sb("mean_row", [128, 8])
        res_row1 = sb("res_row1", [128, DIM])
        scr = sb("scr", [128, 128])
        half_power = sb("half_power", [TT, PAIRS])
        epsilon = sb("epsilon", [TT, PAIRS])
        sum_heads = sb("sum_heads", [128, HB, 32])
        if cosine:
            same_head = sb("same_head", [DIM, DIM])
            gain1 = sb("gain1", [128, DIM])
            gain2 = sb("gain2", [128, DIM])
            res_row2 = sb("res_row2", [128, DIM])
            bias_tab = sb("bias_tab", [128, 2, 2, SC])
            pick = sb("pick", [heads, DIM])
            tau = sb("tau", [heads, 1])
        else:
            norm_par = sb("norm_par", [DIM, 4])
            b_v = sb("b_v", [DIM, 1])

        x_in = sb("x_in", [TT, 2, PAIRS, DIM])
        x_res = sb("x_res", [TT, 4, PAIRS, DIM])
        xT = sb("xT", [128, 2, NT])
        xT_high = sb("xT_high", [DIM, 2, NT], F32R)
        xT_low = sb("xT_low", [DIM, 2, NT], F32R)
        q_band = sb("q_band", [128, 2, BANDS, NTP])
        k_hat = sb("k_hat", [DIM, NT])
        k_heads = sb("k_heads", [128, 2, WINDOWS, J * WIN])
        v_heads = sb("v_heads", [128, 2, WINDOWS, BANDS, HB, 32])
        score = sb("score", [128, 2, SC])
        top = sb("top", [128, 2, heads])
        prob = sb("prob", [128, 2, heads, HALF])
        probT = sb("probT", [128, 2, HP, QT])
        inv_total = sb("inv_total", [DIM, 2 * TT])
        mixedT = sb("mixedT", [DIM + 1, 2, NT])
        x1 = sb("x1", [TT, PAIRS, DIM])
        x1_res = sb("x1_res", [TT, 4, PAIRS, DIM])
        x1T_high = sb("x1T_high", [DIM, NT], F32R)
        x1T_low = sb("x1T_low", [DIM, NT], F32R)
        hid = sb("hid", [128, CHUNKS, NT])
        x2 = sb("x2", [TT, 2, PAIRS, DIM])
        if cosine:
            qk = sb("qk", [DIM, 2, NT])
            qk_sq = sb("qk_sq", [DIM, 2, NT])
            sq_norm = sb("sq_norm", [DIM, 2, NT])
            y = sb("y", [TT, PAIRS, DIM])
            y_sq = sb("y_sq", [TT, PAIRS, DIM])
            y_var = sb("y_var", [TT, PAIRS])
            y_eps = sb("y_eps", [TT, PAIRS])
            y_rstd = sb("y_rstd", [TT, PAIRS])
            y_ln = sb("y_ln", [TT, PAIRS, DIM])
            z = sb("z", [TT, PAIRS, DIM])
            z_sq = sb("z_sq", [TT, PAIRS, DIM])
            z_var = sb("z_var", [TT, PAIRS])
            z_eps = sb("z_eps", [TT, PAIRS])
            z_rstd = sb("z_rstd", [TT, PAIRS])
            z_ln = sb("z_ln", [TT, PAIRS, DIM])
        else:
            stats = sb("stats", [TT, PAIRS, 6])
            moments = sb("moments", [TT, PAIRS, 2])
            var_eps = sb("var_eps", [TT, PAIRS])
            rstd = sb("rstd", [TT, PAIRS])
            x_norm = sb("x_norm", [TT, PAIRS, DIM])
            stats2 = sb("stats2", [TT, PAIRS, 6])
            moments2 = sb("moments2", [TT, PAIRS, 2])
            var_eps2 = sb("var_eps2", [TT, PAIRS])
            rstd2 = sb("rstd2", [TT, PAIRS])
            x1_norm = sb("x1_norm", [TT, PAIRS, DIM])

        def own_heads(buffer, odd):
            part = v_heads[odd * HALF:odd * HALF + WIN, buffer, 0, 0, 0, odd * D:(odd + 1) * D]
            return bass.AP(part.tensor, part.offset,
                           [list(part.ap[0]), [HB * 32, WINDOWS * BANDS], [32 + 2 * D, HB], [1, D]])

        setup = ExitStack()
        with setup:
            if cosine:
                hidden = setup.enter_context(nc.sbuf_tensor("meta_hidden", [DIM, 2, WIN * WIN], F32))
                rel = setup.enter_context(nc.sbuf_tensor("meta_rel", [2, 2, WIN * WIN], F32))
                meta_w1 = setup.enter_context(nc.sbuf_tensor("meta_w1", [2, DIM], F32))
                meta_b1 = setup.enter_context(nc.sbuf_tensor("meta_b1", [DIM, 1], F32))
                meta_w2 = setup.enter_context(nc.sbuf_tensor("meta_w2", [DIM, heads], F32))
                meta_b2 = setup.enter_context(nc.sbuf_tensor("meta_b2", [128, heads], F32))
                mask = setup.enter_context(nc.sbuf_tensor("mask", [128, 2, 2, WIN], F32))
                b_v = setup.enter_context(nc.sbuf_tensor("b_v", [DIM, 1], F32))
            b_proj = setup.enter_context(nc.sbuf_tensor(f"{cfg.name}_b_proj", [128, DIM], F32))
            s_zero = did["setup_zeroed"]
            s_par = did["setup_loaded"]
            s_vec = did["setup_vector"]
            s_mul = did["setup_products"]
            s_act = did["setup_scalar"]
            loads = []

            def column(a):
                return a.rearrange("(c o) -> c o", o=1)

            def every_row(a, n):
                return a.rearrange("(o c) -> o c", o=1).broadcast_to([128, n])

            loads += [(ident[:, :], const["ident"]), (w_fc1[:, :], par["fc1_w"]),
                      (w_fc2[:, :, :], par["fc2_w"].rearrange("(c p) n -> p c n", p=128)),
                      (w_qkv[0:DIM, :], par["qkv_w"]), (w_proj[0:DIM, :], par["proj_w"]),
                      (b_qk[:, :], par["qkv_b"][0:2 * DIM].rearrange("(t c) -> c t", t=2)),
                      (b_v[:, :], column(par["qkv_b"][2 * DIM:3 * DIM])),
                      (b_fc1[:, :], par["fc1_b"].rearrange("(c p) -> p c", p=128)),
                      (row_fc2[:, :], every_row(par["fc2_b"], DIM)),
                      (head_mask[:, :], const[f"{cfg.name}_head_mask"]),
                      (sum_heads[:, :, :], const[f"{cfg.name}_sum_heads"])]
            if cosine:
                loads += [(same_head[:, :], const["same_head"]), (pick[:, :], const["pick"]),
                          (tau[:, :], column(par["tau"])),
                          (gain1[:, :], every_row(par["norm1_g"], DIM)),
                          (res_row1[:, :], every_row(par["norm1_b"], DIM)),
                          (gain2[:, :], every_row(par["norm2_g"], DIM)),
                          (res_row2[:, :], every_row(par["norm2_b"], DIM)),
                          (b_proj[DIM:DIM + 1, :], par["proj_b"].rearrange("(o c) -> o c", o=1)),
                          (rel[:, :, :], const["rel"]), (meta_w1[:, :], par["meta_w1"]),
                          (meta_b1[:, :], column(par["meta_b1"])), (meta_w2[:, :], par["meta_w2"]),
                          (meta_b2[:, :], every_row(par["meta_b2"], heads)),
                          (mask[:, :, :, :], const["mask"])]
            else:
                loads += [(norm_par[:, n:n + 1], column(par[k])) for n, k in enumerate(["g1", "b1", "g2", "b2"])]
                loads += [(b_proj[:, :], every_row(par["proj_b"], DIM))]

            with nc.Block() as block:
                @block.sync
                def _(sp):
                    sp.wait_ge(s_zero, 1)
                    for to, frm in loads:
                        sp.dma_start(to, frm, allow_slow_non_contiguous=True).then_inc(s_par, 16)

                @block.gpsimd
                def _(pool):
                    nc.gpsimd.memset(w_qkv[:, :], 0.0).then_inc(s_zero, 1)
                    for buf in (xT, q_band, k_heads, v_heads, prob):
                        nc.gpsimd.memset(buf[:], 0.0)
                    if cosine:
                        nc.gpsimd.memset(bias_tab[:], 0.0)
                    nc.gpsimd.memset(epsilon[:], cfg.eps)
                    nc.gpsimd.memset(half_power[:], -0.5).then_inc(s_zero, 1)

                @block.vector
                def _(dve):
                    steps = [0]

                    def step(ins):
                        steps[0] += 1
                        ins.then_inc(s_vec, 1)
                        dve.wait_ge(s_vec, steps[0])

                    def centre(w, rows, slot):
                        step(nc.vector.reduce_sum(mean_row[0:rows, slot:slot + 1], w, axis=AX.X))
                        step(nc.vector.tensor_scalar(mean_row[0:rows, slot:slot + 1],
                                                     mean_row[0:rows, slot:slot + 1], 1.0 / DIM, None, ALU.mult))
                        step(nc.vector.tensor_scalar(w, w, mean_row[0:rows, slot:slot + 1], None, ALU.subtract))

                    dve.wait_ge(s_par, 16 * len(loads))
                    dve.wait_ge(s_zero, 2)
                    def split(high, low, whole):
                        step(nc.vector.tensor_copy(high, whole))
                        step(nc.vector.tensor_tensor(low, whole, high.bitcast(F32), ALU.subtract))

                    if cosine:
                        step(nc.vector.memset(mixedT[DIM:DIM + 1, :, :], 1.0))
                        dve.wait_ge(s_mul, 1)
                        step(nc.vector.tensor_tensor(w_proj[DIM:DIM + 1, :], psT[DIM:DIM + 1, 0:DIM],
                                                     b_proj[DIM:DIM + 1, :], ALU.add))
                        centre(w_proj[:, :], DIM + 1, 0)
                        for c in range(CHUNKS):
                            centre(w_fc2[:, c, :], 128, 1 + c)
                        centre(row_fc2[:, :], 128, 4)
                        dve.wait_ge(s_mul, 2)
                        step(nc.vector.tensor_scalar(scr[0:DIM, 0:1], psM[0:DIM, 0, 0:1], 0.01, None, ALU.max))
                        step(nc.vector.reciprocal(scr[0:DIM, 0:1], scr[0:DIM, 0:1]))
                        step(nc.vector.tensor_scalar(head_mask[:, :], head_mask[:, :], scr[0:DIM, 0:1], None, ALU.mult))
                        split(w_qk_high[:, :], w_qk_low[:, :], w_qkv[0:DIM, 0:2 * DIM])
                        split(w_fc1_high[:, :], w_fc1_low[:, :], w_fc1[:, :])
                        for order in range(2):
                            dve.wait_ge(s_mul, 2 + 2 * order + 2)
                            for part, (k0, k1) in enumerate([(0, 42), (42, WIN)]):
                                for r in (0, HALF):
                                    rows = slice(r, r + WIN)
                                    out = bias_tab[rows, order, 0, :].rearrange("p (h k) -> p h k", k=WIN)[:, :, k0:k1]
                                    got = psS[rows, part, 0:(k1 - k0) * heads].rearrange("p (k h) -> p h k", h=heads)
                                    step(nc.vector.tensor_tensor(out, got, bcast(meta_b2[rows, :], 2, k1 - k0), ALU.add))
                            for edge in (1, 0):
                                out = bias_tab[:, order, edge, :].rearrange("p (h k) -> p h k", k=WIN)
                                base = bias_tab[:, order, 0, :].rearrange("p (h k) -> p h k", k=WIN)
                                step(nc.vector.tensor_tensor(out, base, bcast(mask[:, order, edge, :], 1, heads), ALU.add))
                    else:
                        dve.wait_ge(s_mul, 1)
                        step(nc.vector.tensor_tensor(b_qk[:, :], b_qk[:, :], psT[0:DIM, 0:2], ALU.add))
                        step(nc.vector.tensor_scalar(b_qk[:, 0:1], b_qk[:, 0:1], D ** -0.5, None, ALU.mult))
                        step(nc.vector.tensor_tensor(b_v[:, :], b_v[:, :], psT[0:DIM, 2:3], ALU.add))
                        step(nc.vector.tensor_tensor(b_fc1[:, :], b_fc1[:, :], psT[:, 3:3 + CHUNKS], ALU.add))
                        step(nc.vector.tensor_scalar(w_qkv[0:DIM, :], w_qkv[0:DIM, :], norm_par[:, 0:1], None, ALU.mult))
                        step(nc.vector.tensor_scalar(w_qkv[0:DIM, 0:DIM], w_qkv[0:DIM, 0:DIM], D ** -0.5, None, ALU.mult))
                        step(nc.vector.tensor_scalar(w_fc1[:, :], w_fc1[:, :], norm_par[:, 2:3], None, ALU.mult))
                        split(w_qk_high[:, :], w_qk_low[:, :], w_qkv[0:DIM, 0:2 * DIM])
                        split(w_fc1_high[:, :], w_fc1_low[:, :], w_fc1[:, :])
                        step(nc.vector.tensor_copy(scr[0:DIM, 0:128], bcast(b_v[:, 0:1], 1, 128)[:, :, 0]))
                        dve.wait_ge(s_mul, 2)
                        step(nc.vector.tensor_tensor(res_row1[:, :], psM[:, 0, 0:DIM], b_proj[:, :], ALU.add))

                @block.tensor
                def _(pe):
                    pe.wait_ge(s_par, 16 * len(loads))
                    if cosine:
                        nc.tensor.matmul(psT[DIM:DIM + 1, 0:DIM], b_v[:, :], w_proj[0:DIM, :],
                                         start=True, stop=True).then_inc(s_mul, 1)
                        nc.tensor.matmul(psM[0:DIM, 0, 0:1], pick[:, :], tau[:, :],
                                         start=True, stop=True).then_inc(s_mul, 1)
                        for order in range(2):
                            cols = WIN * WIN
                            starts = list(range(0, cols, 480))
                            for n, a in enumerate(starts):
                                b = min(a + 480, cols)
                                if n or order:
                                    pe.wait_ge(s_act, n + order * len(starts))
                                last = nc.tensor.matmul(psM[0:DIM, 1, 0:b - a], meta_w1[:, :], rel[:, order, a:b],
                                                        start=True, stop=True)
                                last.then_inc(did["setup_hidden"], 1)
                            pe.wait_ge(s_act, (order + 1) * len(starts))
                            if order:
                                pe.wait_ge(s_vec, 1 + 1 + 3 * 5 + 3 + 4 + 6)
                            for half in (0, HALF):
                                for k in range(WIN):
                                    part, col = (0, k) if k < 42 else (1, k - 42)
                                    keyed = hidden[:, order, :].rearrange("c (q k) -> c q k", k=WIN)[:, :, k]
                                    last = nc.tensor.matmul(psS[half:half + WIN, part, col * heads:(col + 1) * heads],
                                                            keyed, meta_w2[:, :], start=True, stop=True)
                                last.then_inc(s_mul, 1)
                    else:
                        pe.wait_ge(s_zero, 1)
                        for n in range(3):
                            nc.tensor.matmul(psT[0:DIM, n:n + 1], w_qkv[0:DIM, n * DIM:(n + 1) * DIM], norm_par[:, 1:2],
                                             start=True, stop=True)
                        for c in range(CHUNKS):
                            last = nc.tensor.matmul(psT[:, 3 + c:4 + c], w_fc1[:, c * 128:(c + 1) * 128],
                                                    norm_par[:, 3:4], start=True, stop=True)
                        last.then_inc(s_mul, 1)
                        pe.wait_ge(s_vec, 12)
                        nc.tensor.matmul(psM[:, 0, 0:DIM], scr[0:DIM, 0:128], w_proj[0:DIM, :],
                                         start=True, stop=True).then_inc(s_mul, 1)

                if cosine:
                    @block.scalar
                    def _(act):
                        act.wait_ge(s_par, 16 * len(loads))
                        done = 0
                        for order in range(2):
                            cols = WIN * WIN
                            for a in range(0, cols, 480):
                                b = min(a + 480, cols)
                                done += 1
                                act.wait_ge(did["setup_hidden"], done)
                                nc.scalar.activation(hidden[:, order, a:b], psM[0:DIM, 1, 0:b - a], ACT.Relu,
                                                     bias=meta_b1[:, :]).then_inc(s_act, 1)

        def wrapped(first, count):
            inside = min(count, SIDE - first)
            return [(first, 0, inside)] if inside == count else [(first, 0, inside), (0, inside, count)]

        PLAIN_ROW, LAST_ROW = 5, 18

        def dma_total(parity, upto):
            if not cosine:
                return upto * 16 * PAIRS
            last_rows = upto // 4 if parity else 0
            return upto * 16 * PLAIN_ROW + last_rows * 16 * (LAST_ROW - PLAIN_ROW)

        def swin_windows(image, wy, tile, move):
            low = cfg.shift + win * wy
            for p in range(PAIRS):
                left = cfg.shift + 2 * win * p
                if wy < 7:
                    for col, a, b in wrapped(left, 2 * win):
                        move(tile[a * win:b * win, p, :], bass.ds(image * SIDE + low, win), slice(col, col + b - a))
                else:
                    for half in range(2):
                        for row, ya, yb in wrapped(low, win):
                            for col, a, b in wrapped(left + half * win, win):
                                at = half * WIN + ya * win
                                move(tile[at + a * (yb - ya):at + b * (yb - ya), p, :],
                                     bass.ds(image * SIDE + row, yb - ya), slice(col, col + b - a))

        with nc.Block() as block:
            s_load = [did["x_loaded_even"], did["x_loaded_odd"]]
            s_store = [did["x2_stored_even"], did["x2_stored_odd"]]

            @block.sync
            def _(sp):
                src_rows = src.rearrange("b h w c -> (b h) w c")
                dst_rows = dst.rearrange("b h w c -> (b h) w c")

                def may_load(n):
                    sp.wait_ge(did["x_res"], upto(n - 2))
                    sp.wait_ge(did["x_turned" if cosine else "x_norm"], upto(n - 2))

                if cosine:
                    def load(image, wy):
                        may_load(image * 8 + wy)
                        swin_windows(image, wy, x_in[:, wy % 2], lambda tile, rows, cols:
                                     sp.dma_start(tile, src_rows[rows, cols, :].rearrange("y x c -> x y c"))
                                     .then_inc(s_load[wy % 2], 16))

                    def store(image, wy):
                        sp.wait_ge(did["x2"], upto(image * 8 + wy))
                        swin_windows(image, wy, x2[:, wy % 2], lambda tile, rows, cols:
                                     sp.dma_start(dst_rows[rows, cols, :].rearrange("y x c -> x y c"), tile)
                                     .then_inc(s_store[wy % 2], 16))

                    for wy in range(8):
                        load(0, wy)
                    with sp.Fori(1, IMAGES) as image:
                        for wy in range(8):
                            load(image, wy)
                            store(image - 1, wy)
                    for wy in range(8):
                        store(IMAGES - 1, wy)
                else:
                    def place(n, p):
                        pair = n * PAIRS + p
                        return bass.ds((pair // 7) * 2 * win, 2 * win), bass.ds((pair % 7) * win, win)

                    def load(n, parity):
                        may_load(n)
                        for p in range(PAIRS):
                            rows, cols = place(n, p)
                            sp.dma_start(x_in[:, parity, p, :], src_rows[rows, cols, :]).then_inc(s_load[parity], 16)

                    def store(n, parity):
                        sp.wait_ge(did["x2"], upto(n))
                        for p in range(PAIRS):
                            rows, cols = place(n, p)
                            sp.dma_start(dst_rows[rows, cols, :], x2[:, parity, p, :]).then_inc(s_store[parity], 16)

                    for n in range(8):
                        load(n, n % 2)
                    with sp.Fori(4, groups // 2) as m:
                        for k in range(2):
                            load(2 * m + k, k)
                            store(2 * m + k - 8, k)
                    for n in range(groups - 8, groups):
                        store(n, n % 2)
                for parity in range(2):
                    sp.wait_ge(s_store[parity], dma_total(parity, groups // 2))

            def moved(g, parity):
                return 0 if isinstance(g, int) and g < 0 else dma_total(parity, g // 2 + 1)

            @block.tensor
            def _(pe):
                def body(g, r):
                    turn, make, out1, out2, mlp, fin = g + 2, g + 1, g - 1, g - 2, g - 3, g - 4
                    qk_of = turn if cosine else make

                    def product(out, high, low, moving_high, moving_low):
                        nc.tensor.matmul(out, high, moving_high, start=True, stop=False)
                        nc.tensor.matmul(out, high, moving_low, start=False, stop=False)
                        return nc.tensor.matmul(out, low, moving_high, start=False, stop=True)

                    def all_windows(first):
                        part, pair, column = [list(d) for d in first.ap]
                        return bass.AP(first.tensor, first.offset, [part, pair, [HALF, 2], column])

                    def use_after_norms(bank):
                        if cosine:
                            pe.wait_ge(did["sq_norm"], upto(make))
                        elif bank == 0:
                            pe.wait_ge(did["q_read"], upto(g))
                            pe.wait_ge(did["q_band0"], upto(g))
                        else:
                            pe.wait_ge(did["k_read"], upto(g))

                    for slot in range(PAIRS):
                        if exists(g, groups):
                            pe.wait_ge(did["q_band"], upto(g))
                            if not cosine:
                                pe.wait_ge(did["q_band0"], upto(g))
                            pe.wait_ge(did["k_heads"], upto(g, slot, PAIRS))
                            ug, us = before(g, slot, 1 if SB == 2 else 2)
                            for bank in range(SB):
                                pe.wait_ge(did[f"score_read{bank}"], upto(ug, us, PAIRS))
                                for band, j0, nj, at_bank, col in cfg.score_parts:
                                    if at_bank != bank:
                                        continue
                                    for half in range(2):
                                        w = 2 * slot + half
                                        rows = HALF if half == 0 else WIN
                                        last = nc.tensor.matmul(
                                            psS[half * HALF:half * HALF + rows, bank if SB == 2 else slot % 2,
                                                col:col + nj * WIN],
                                            q_band[:, r % 2, band, w * WIN:w * WIN + rows],
                                            k_heads[:, r % 2, w, j0 * WIN:(j0 + nj) * WIN], start=True, stop=True)
                                last.then_inc(did[f"scored{bank}"], 1)
                        if slot == 0 and exists(out2, groups):
                            pe.wait_ge(did["mixedT"], upto(out2, 1, 2))
                            use_after_norms(0)
                            pe.wait_ge(did["hid"], upto(fin, 2, CHUNKS))
                            rows = DIM + 1 if cosine else DIM
                            for p in range(PAIRS):
                                last = nc.tensor.matmul(psM[0:TT, 0, p * DIM:(p + 1) * DIM],
                                                        mixedT[0:rows, r % 2, p * TT:(p + 1) * TT],
                                                        w_proj[0:rows, :], start=True, stop=True)
                            last.then_inc(did["proj_made"], 1)
                        if slot == 0 and exists(fin, groups):
                            pe.wait_ge(did["hid"], upto(fin, 2, CHUNKS))
                            use_after_norms(1)
                            for p in range(PAIRS):
                                for c in range(CHUNKS):
                                    last = nc.tensor.matmul(psM[0:TT, 1, p * DIM:(p + 1) * DIM],
                                                            hid[:, c, p * TT:(p + 1) * TT],
                                                            w_fc2[:, c, :], start=(c == 0), stop=(c == CHUNKS - 1))
                            last.then_inc(did["fc2_made"], 1)
                        if slot == 1 and exists(mlp, groups):
                            pe.wait_ge(did["x1T_low"], upto(mlp))
                            pe.wait_ge(did["fc2_read"], upto(fin))
                            use_after_norms(1)
                            product(psM[:, 1, 0:NT], w_fc1_high[:, 0:128], w_fc1_low[:, 0:128],
                                    x1T_high[:, :], x1T_low[:, :]).then_inc(did["fc1_made"], 1)
                        if slot == 1 and exists(turn, groups):
                            if cosine:
                                pe.wait_ge(s_load[r % 2], moved(turn, r % 2))
                            else:
                                pe.wait_ge(did["x_norm"], upto(turn))
                            pe.wait_ge(did["x1T_low"], upto(mlp))
                            pe.wait_ge(did["xT"], upto(make))
                            for p in range(PAIRS):
                                rows = x_in[:, r % 2, p, :] if cosine else x_norm[:, p, :]
                                last = nc.tensor.transpose(psT[0:DIM, p * TT:(p + 1) * TT], rows, ident[0:TT, 0:TT])
                            last.then_inc(did["x_turned"], 1)
                        if slot == 2 and exists(qk_of, groups):
                            at = (r + (0 if cosine else 1)) % 2
                            pe.wait_ge(did["xT_low"], upto(qk_of))
                            pe.wait_ge(did["hid"], upto(mlp, 1, CHUNKS))
                            pe.wait_ge(did["fc2_read"], upto(fin))
                            use_after_norms(1)
                            product(psM[0:DIM, 1, 0:NT], w_qk_high[:, DIM:2 * DIM], w_qk_low[:, DIM:2 * DIM],
                                    xT_high[:, at, :], xT_low[:, at, :]).then_inc(did["k_made"], 1)
                            pe.wait_ge(did["hid"], upto(mlp, 2, CHUNKS))
                            pe.wait_ge(did["v_heads"], upto(make))
                            pe.wait_ge(did["proj_read"], upto(out2))
                            product(psM[0:DIM, 0, 0:NT], w_qk_high[:, 0:DIM], w_qk_low[:, 0:DIM],
                                    xT_high[:, at, :], xT_low[:, at, :]).then_inc(did["q_made"], 1)
                        ag, as_ = before(g, slot, 2)
                        if exists(ag, groups):
                            pe.wait_ge(did["v_heads"], upto(ag))
                            pe.wait_ge(did["probT"], upto(ag, as_, PAIRS))
                            if as_ % 2 == 0:
                                mg, ms = before(ag, as_, 2)
                                pe.wait_ge(did["mixedT"], upto(mg, ms // 2, 2))
                            at = (r + (0 if slot >= 2 else 1)) % 2
                            turned = probT[:, as_ % 2]
                            for half in range(2):
                                first = (as_ % 2) * TT + half * WIN
                                for n in range(HB):
                                    for band in range(BANDS):
                                        last = nc.tensor.matmul(psO[32 * band:32 * band + 32, first:first + WIN],
                                                                v_heads[:, at, 2 * as_ + half, band, n, :],
                                                                turned[:, band * HB + n, half * HALF:half * HALF + WIN],
                                                                start=(n == 0), stop=(n == HB - 1))
                            if as_ % 2 == 1:
                                for n in range(HB):
                                    for band in range(BANDS):
                                        last = nc.tensor.matmul(
                                            psO[32 * band:32 * band + 32, SUMS:SUMS + 2 * TT], sum_heads[:, n, :],
                                            all_windows(probT[:, :, band * HB + n, 0:WIN]),
                                            start=(n == 0), stop=(n == HB - 1))
                            last.then_inc(did["mixed_made"], 1)
                        if slot == 3 and exists(out2, groups):
                            pe.wait_ge(did["x1" if cosine else "x1_norm"], upto(out2))
                            pe.wait_ge(did["xT"], upto(turn))
                            pe.wait_ge(did["x1T_low"], upto(mlp))
                            for p in range(PAIRS):
                                rows = x1[:, p, :] if cosine else x1_norm[:, p, :]
                                last = nc.tensor.transpose(psT[0:DIM, p * TT:(p + 1) * TT], rows, ident[0:TT, 0:TT])
                            last.then_inc(did["x1_turned"], 1)
                        if slot == 3 and cosine and exists(turn, groups):
                            pe.wait_ge(did["qk_sq"], upto(turn))
                            pe.wait_ge(did["q_read"], upto(turn))
                            pe.wait_ge(did["k_read"], upto(turn))
                            for n in range(2):
                                last = nc.tensor.matmul(psM[0:DIM, n, 0:NT], same_head[:, :], qk_sq[:, n, :],
                                                        start=True, stop=True)
                            last.then_inc(did["norms_made"], 1)
                        if slot == 1 and exists(make, groups):
                            pe.wait_ge(did["xT"], upto(make))
                            pe.wait_ge(did["proj_read"], upto(out2))
                            use_after_norms(0)
                            for w in range(WINDOWS):
                                for odd in range(2):
                                    cols = w_qkv[:, 2 * DIM:3 * DIM].rearrange("c (h o d) -> c h o d", o=2, d=D)[:, :, odd, :]
                                    out = psM[odd * HALF:odd * HALF + WIN, 0, w * HP * D:(w + 1) * HP * D]
                                    last = nc.tensor.matmul(out, xT[:, (r + 1) % 2, w * WIN:(w + 1) * WIN], cols,
                                                            start=True, stop=True)
                            last.then_inc(did["v_made"], 1)
                        if slot == 1 and exists(mlp, groups):
                            pe.wait_ge(did["hid"], upto(mlp, 0, CHUNKS))
                            product(psM[:, 1, 0:NT], w_fc1_high[:, 128:256], w_fc1_low[:, 128:256],
                                    x1T_high[:, :], x1T_low[:, :]).then_inc(did["fc1_made"], 1)
                        tg, ts = before(g, slot, 1)
                        if exists(tg, groups):
                            pe.wait_ge(did["prob"], upto(tg, ts, PAIRS))
                            rg, rs = before(tg, ts, 1 if HP > 3 else 2)
                            pe.wait_ge(did["probT"], upto(rg, rs, PAIRS))
                            for hp in range(HP):
                                bank = hp // 3 if HP > 3 else ts % 2
                                last = nc.tensor.transpose(psP[:, bank, hp % 3 * QT:(hp % 3 + 1) * QT],
                                                           prob[0:QT, ts % 2, 2 * hp:2 * hp + 2, :].rearrange("p h k -> p (h k)"),
                                                           ident[0:QT, 0:QT])
                            last.then_inc(did["prob_turned"], 1)
                        if slot == 1 and exists(mlp, groups):
                            pe.wait_ge(did["v_heads"], upto(make))
                            pe.wait_ge(did["proj_read"], upto(out2))
                            product(psM[:, 0, 0:NT], w_fc1_high[:, 256:384], w_fc1_low[:, 256:384],
                                    x1T_high[:, :], x1T_low[:, :]).then_inc(did["fc1_made"], 1)

                run_groups(pe, groups, body)

            @block.scalar
            def _(act):
                def body(g, r):
                    turn, make, out1, out2, mlp, fin = g + 2, g + 1, g - 1, g - 2, g - 3, g - 4

                    def gelu(c):
                        if exists(mlp, groups):
                            act.wait_ge(did["fc1_made"], upto(mlp, c, CHUNKS))
                            act.wait_ge(did["fc2_made"], upto(fin))
                            nc.scalar.activation(hid[:, c, 0:NT], psM[:, 1 if c < 2 else 0, 0:NT], ACT.Gelu,
                                                 bias=b_fc1[:, c:c + 1]).then_inc(did["hid"], 1)

                    for slot in range(PAIRS):
                        tg, ts = before(g, slot, 2)
                        if exists(tg, groups):
                            act.wait_ge(did["prob_turned"], upto(tg, ts, PAIRS))
                            fg, fs = before(tg, ts, 2 if ts % 2 else 1)
                            act.wait_ge(did["mixed_made"], upto(fg, fs, PAIRS))
                            if HP > 3:
                                frm = psP[:, :, 0:3 * QT]
                                to = probT[:, ts % 2].rearrange("p (b n) q -> p b (n q)", b=2)
                            else:
                                frm = psP[:, ts % 2, 0:3 * QT]
                                to = probT[:, ts % 2].rearrange("p n q -> p (n q)")
                            nc.scalar.activation(to, frm, ACT.Copy).then_inc(did["probT"], 1)
                        if slot == 2:
                            gelu(2)
                            act.preload_act_table_set(EXP_SET)
                        eg, es = before(g, slot, 1)
                        if exists(eg, groups):
                            act.wait_ge(did["shifted"], upto(eg, es, PAIRS))
                            fg, fs = before(eg, es, 2)
                            act.wait_ge(did["prob_turned"], upto(fg, fs, PAIRS))
                            nc.scalar.activation(prob[0:QT, es % 2, :, 0:WIN],
                                                 score[0:QT, es % 2, :].rearrange("p (h k) -> p h k", k=WIN),
                                                 ACT.Exp).then_inc(did["prob"], 1)
                        if slot == 0 and cosine:
                            if exists(make, groups):
                                act.wait_ge(did["sq_norm"], upto(make))
                                nc.scalar.activation(sq_norm[:, :, :], sq_norm[:, :, :], ACT.Ln).then_inc(did["log_norm"], 1)
                                act.wait_ge(did["log_norm"], upto(make))
                                nc.scalar.activation(sq_norm[:, :, :], sq_norm[:, :, :], ACT.Exp,
                                                     scale=-0.5).then_inc(did["inv_norm"], 1)
                            if exists(out2, groups):
                                act.wait_ge(did["proj_made"], upto(out2))
                                act.wait_ge(did["y_ln"], upto(mlp))
                                act.wait_ge(did["y_var"], upto(mlp))
                                made = psM[0:TT, 0, 0:PAIRS * DIM]
                                nc.scalar.activation(y[:, :, :].rearrange("p n c -> p (n c)"), made, ACT.Copy)
                                nc.scalar.activation(y_sq[:, :, :].rearrange("p n c -> p (n c)"), made, ACT.Square,
                                                     scale=DIM ** -0.5).then_inc(did["proj_read"], 1)
                        if slot == 1:
                            act.preload_act_table_set(GELU_SET)
                            gelu(0)
                            if exists(turn, groups):
                                act.wait_ge(did["x_turned"], upto(turn))
                                act.wait_ge(did["v_made"], upto(g))
                                act.wait_ge(did["k_made"], upto(g))
                                nc.scalar.activation(xT[0:DIM, r % 2, 0:NT], psT[0:DIM, 0:NT], ACT.Copy)
                                nc.scalar.activation(xT_high[:, r % 2, :], psT[0:DIM, 0:NT],
                                                     ACT.Copy).then_inc(did["xT"], 1)
                            if cosine and exists(fin, groups):
                                act.wait_ge(did["fc2_read"], upto(fin))
                                act.wait_ge(did["z_var"], upto(g - 5))
                                nc.scalar.activation(z_sq[:, :, :], z[:, :, :], ACT.Square,
                                                     scale=DIM ** -0.5).then_inc(did["z_sq"], 1)
                            if exists(make, groups):
                                act.wait_ge(did["v_made"], upto(make))
                                act.wait_ge(did["mixed_made"], upto(g - 1, PAIRS - 1, PAIRS))
                                for odd in range(2):
                                    rows = slice(odd * HALF, odd * HALF + WIN)
                                    made = psM[rows, 0, 0:WINDOWS * HP * D].rearrange("r (w n d) -> r w n d", n=HB, d=D)
                                    last = nc.scalar.activation(own_heads((r + 1) % 2, odd), made, ACT.Copy)
                                last.then_inc(did["v_heads"], 1)
                            gelu(1)
                        if slot == 2:
                            if not cosine and exists(make, groups):
                                act.wait_ge(did["k_made"], upto(make))
                                act.wait_ge(did["k_heads"], upto(g, PAIRS - 1, PAIRS))
                                nc.scalar.activation(k_hat[:, :], psM[0:DIM, 1, 0:NT], ACT.Identity,
                                                     bias=b_qk[:, 1:2]).then_inc(did["k_hat"], 1)
                        if slot == 3:
                            if not cosine and exists(make, groups):
                                act.wait_ge(did["q_made"], upto(make))
                                act.wait_ge(did["scored0"], upto(g - 1, PAIRS - 1, PAIRS))
                                for band in (1, 2):
                                    rows = slice(32 * band, 32 * band + 32)
                                    last = nc.scalar.activation(q_band[rows, (r + 1) % 2, band, 0:NT], psM[rows, 0, 0:NT],
                                                                ACT.Identity, bias=b_qk[rows, 0:1])
                                last.then_inc(did["q_band"], 1)
                            if cosine and exists(turn, groups):
                                act.wait_ge(did["q_read"], upto(turn))
                                act.wait_ge(did["norms_made"], upto(make))
                                nc.scalar.activation(qk_sq[:, :, :], qk[:, :, :], ACT.Square).then_inc(did["qk_sq"], 1)
                            if exists(out2, groups):
                                act.wait_ge(did["x1_turned"], upto(out2))
                                act.wait_ge(did["fc1_made"], upto(mlp, 2, CHUNKS))
                                nc.scalar.activation(x1T_high[:, :], psT[0:DIM, 0:NT], ACT.Copy).then_inc(did["x1T"], 1)

                run_groups(act, groups, body)

            @block.vector
            def _(dve):
                def body(g, r):
                    turn, make, out1, out2, mlp, fin = g + 2, g + 1, g - 1, g - 2, g - 3, g - 4
                    for slot in range(PAIRS):
                        if slot == 1 and not cosine and exists(out2, groups):
                            dve.wait_ge(did["moments2"], upto(mlp))
                            dve.wait_ge(did["x1"], upto(out2))
                            for p in range(PAIRS):
                                last = nc.vector.bn_stats(stats2[:, p, :], x1[:, p, :])
                            last.then_inc(did["stats2"], 1)
                            dve.wait_ge(did["stats2"], upto(out2))
                            dve.wait_ge(did["var_eps2"], upto(mlp))
                        if slot == 3 and not cosine and exists(g + 3, groups):
                            dve.wait_ge(s_load[(r + 1) % 2], moved(g + 3, (r + 1) % 2))
                            dve.wait_ge(did["moments"], upto(turn))
                            for p in range(PAIRS):
                                last = nc.vector.bn_stats(stats[:, p, :], x_in[:, (r + 1) % 2, p, :])
                            last.then_inc(did["stats"], 1)
                            dve.wait_ge(did["stats"], upto(g + 3))
                            dve.wait_ge(did["x_norm"], upto(turn))
                        if exists(g, groups):
                            half = slot % 2
                            hg, hs = before(g, slot, 2)
                            dve.wait_ge(did["prob"], upto(hg, hs, PAIRS))
                            heads_view = score[0:QT, half, :].rearrange("p (h k) -> p h k", k=WIN)
                            if cosine:
                                for bank in range(SB):
                                    dve.wait_ge(did[f"scored{bank}"], upto(g, slot, PAIRS))
                                    cols = slice(bank * SBC, (bank + 1) * SBC)
                                    kind = bias_tab[0:QT, bass.ds((g % 8) // 7, 1), slot // 3, cols]
                                    nc.vector.tensor_tensor(score[0:QT, half, cols], psS[0:QT, bank, 0:SBC],
                                                            kind.rearrange("p o n -> p (o n)"), ALU.add)\
                                        .then_inc(did[f"score_read{bank}"], 1)
                                dve.wait_ge(did["score_read1"], upto(g, slot, PAIRS))
                                nc.vector.tensor_reduce(top[0:QT, half, :], heads_view, AX.X, ALU.max).then_inc(did["top"], 1)
                            else:
                                dve.wait_ge(did["scored0"], upto(g, slot, PAIRS))
                                from_psum = psS[0:QT, half, 0:SC].rearrange("p (h k) -> p h k", k=WIN)
                                nc.vector.tensor_reduce(top[0:QT, half, :], from_psum, AX.X, ALU.max).then_inc(did["top"], 1)
                                dve.wait_ge(did["top"], upto(g, slot, PAIRS))
                                nc.vector.tensor_tensor(heads_view, from_psum, bcast(top[0:QT, half, :], 2, WIN),
                                                        ALU.subtract).then_inc(did["shifted"], 1)
                        if slot == 1 and not cosine and exists(out2, groups):
                            for p in range(PAIRS):
                                last = nc.vector.bn_aggr(moments2[:, p, :], stats2[:, p, :])
                            last.then_inc(did["moments2"], 1)
                        if slot == 3 and not cosine and exists(g + 3, groups):
                            for p in range(PAIRS):
                                last = nc.vector.bn_aggr(moments[:, p, :], stats[:, p, :])
                            last.then_inc(did["moments"], 1)
                        if slot == 0 and exists(mlp, groups):
                            dve.wait_ge(did["x1T"], upto(mlp))
                            nc.vector.tensor_tensor(x1T_low[:, :], psT[0:DIM, 0:NT], x1T_high[:, :].bitcast(F32),
                                                    ALU.subtract).then_inc(did["x1T_low"], 1)
                        if slot == 0 and exists(fin, groups):
                            dve.wait_ge(did["fc2_made"], upto(fin))
                            out_of = psM[0:TT, 1, 0:PAIRS * DIM].rearrange("p (n c) -> p n c", c=DIM)
                            if cosine:
                                dve.wait_ge(did["z_ln"], upto(g - 5))
                                dve.wait_ge(did["z_sq"], upto(g - 5))
                                nc.vector.tensor_tensor(z[:, :, :], out_of, bcast(row_fc2[0:TT, :], 1, PAIRS),
                                                        ALU.add).then_inc(did["fc2_read"], 1)
                            else:
                                dve.wait_ge(did["x1_res"], upto(fin))
                                dve.wait_ge(s_store[r % 2], moved(fin - 2, r % 2))
                                nc.vector.tensor_tensor(x2[:, r % 2], out_of, x1_res[:, r % 4],
                                                        ALU.add).then_inc(did["x2"], 1)
                        if slot == 0 and not cosine and exists(out2, groups):
                            dve.wait_ge(did["proj_made"], upto(out2))
                            dve.wait_ge(did["x_res"], upto(out2))
                            dve.wait_ge(did["x1_norm"], upto(mlp))
                            dve.wait_ge(did["x1_res"], upto(mlp))
                            nc.vector.tensor_tensor(x1[:, :, :], psM[:, 0, 0:PAIRS * DIM]
                                                    .rearrange("p (n c) -> p n c", c=DIM), x_res[:, (r + 2) % 4],
                                                    ALU.add).then_inc(did["x1"], 1)
                        if slot == 1 and not cosine:
                            if exists(turn, groups):
                                dve.wait_ge(did["xT"], upto(turn))
                                nc.vector.tensor_tensor(xT_low[:, r % 2, :], xT[0:DIM, r % 2, 0:NT],
                                                        xT_high[:, r % 2, :].bitcast(F32),
                                                        ALU.subtract).then_inc(did["xT_low"], 1)
                        if slot == 1 and cosine:
                            if exists(make, groups):
                                dve.wait_ge(did["inv_norm"], upto(make))
                                dve.wait_ge(did["scored1"], upto(g - 1, PAIRS - 1, PAIRS))
                                dve.wait_ge(did["k_heads"], upto(g, PAIRS - 1, PAIRS))
                                nc.vector.tensor_tensor(k_hat[:, :], qk[:, 1, :], sq_norm[:, 1, :], ALU.mult)\
                                    .then_inc(did["k_hat"], 1)
                                for band in range(BANDS):
                                    rows = slice(32 * band, 32 * band + 32)
                                    last = nc.vector.tensor_tensor(q_band[rows, (r + 1) % 2, band, 0:NT], qk[rows, 0, :],
                                                                   sq_norm[rows, 0, :], ALU.mult)
                                last.then_inc(did["q_band"], 1)
                            if exists(turn, groups):
                                dve.wait_ge(did["xT"], upto(turn))
                                nc.vector.tensor_tensor(xT_low[:, r % 2, :], xT[0:DIM, r % 2, 0:NT],
                                                        xT_high[:, r % 2, :].bitcast(F32),
                                                        ALU.subtract).then_inc(did["xT_low"], 1)
                            if exists(out2, groups):
                                dve.wait_ge(did["proj_read"], upto(out2))
                                dve.wait_ge(did["y_eps"], upto(mlp))
                                nc.vector.tensor_reduce(y_var[:, :], y_sq[:, :, :], AX.X, ALU.add).then_inc(did["y_var"], 1)
                            if exists(fin, groups):
                                dve.wait_ge(did["z_sq"], upto(fin))
                                dve.wait_ge(did["z_eps"], upto(g - 5))
                                nc.vector.tensor_reduce(z_var[:, :], z_sq[:, :, :], AX.X, ALU.add).then_inc(did["z_var"], 1)
                        if slot == 2 and cosine:
                            if exists(out2, groups):
                                dve.wait_ge(did["y_rstd"], upto(out2))
                                dve.wait_ge(did["x1"], upto(mlp))
                                for p in range(PAIRS):
                                    last = nc.vector.scalar_tensor_tensor(y_ln[:, p, :], y[:, p, :], y_rstd[:, p:p + 1],
                                                                          gain1[0:TT, :], ALU.mult, ALU.mult)
                                last.then_inc(did["y_ln"], 1)
                            if exists(turn, groups):
                                dve.wait_ge(did["q_band"], upto(make))
                                dve.wait_ge(did["qk_sq"], upto(make))
                                for n, name in ((1, "k"), (0, "q")):
                                    dve.wait_ge(did[f"{name}_made"], upto(turn))
                                    nc.vector.tensor_scalar(qk[:, n, :], psM[0:DIM, n, 0:NT], b_qk[:, n:n + 1],
                                                            None, ALU.add).then_inc(did[f"{name}_read"], 1)
                        if slot == 2 and not cosine:
                            if exists(make, groups):
                                dve.wait_ge(did["q_made"], upto(make))
                                dve.wait_ge(did["scored0"], upto(g - 1, PAIRS - 1, PAIRS))
                                nc.vector.tensor_scalar(q_band[0:32, (r + 1) % 2, 0, 0:NT], psM[0:32, 0, 0:NT],
                                                        b_qk[0:32, 0:1], None, ALU.add).then_inc(did["q_band0"], 1)
                            if exists(out2, groups):
                                dve.wait_ge(did["rstd2"], upto(out2))
                                dve.wait_ge(did["x1_turned"], upto(mlp))
                                for p in range(PAIRS):
                                    last = nc.vector.tensor_scalar(x1_norm[:, p, :], x1[:, p, :], moments2[:, p, 0:1],
                                                                   rstd2[:, p:p + 1], ALU.subtract, ALU.mult)
                                last.then_inc(did["x1_norm"], 1)
                        if slot == 3 and cosine:
                            if exists(turn, groups):
                                dve.wait_ge(did["norms_made"], upto(turn))
                                dve.wait_ge(did["q_band"], upto(make))
                                nc.vector.tensor_scalar(sq_norm[:, :, :], psM[0:DIM, :, 0:NT], 1e-6, None,
                                                        ALU.max).then_inc(did["sq_norm"], 1)
                            if exists(fin, groups):
                                dve.wait_ge(did["z_rstd"], upto(fin))
                                dve.wait_ge(did["x2"], upto(g - 5))
                                for p in range(PAIRS):
                                    last = nc.vector.scalar_tensor_tensor(z_ln[:, p, :], z[:, p, :], z_rstd[:, p:p + 1],
                                                                          gain2[0:TT, :], ALU.mult, ALU.mult)
                                last.then_inc(did["z_ln"], 1)
                        mg, ms = before(g, slot, 2)
                        if ms % 2 == 1 and exists(mg, groups):
                            dve.wait_ge(did["mixed_made"], upto(mg, ms, PAIRS))
                            dve.wait_ge(did["mixedT"], upto(mg, ms // 2 - 1, 2) if ms > 1 else upto(mg - 1, 1, 2))
                            nc.vector.reciprocal(inv_total[:, :], psO[0:DIM, SUMS:SUMS + 2 * TT])\
                                .then_inc(did["inv_total"], 1)
                            dve.wait_ge(did["inv_total"], upto(mg, ms // 2, 2))
                            dve.wait_ge(did["proj_made"], upto(mg - 2))
                            at = (r + (0 if slot >= 2 else 1)) % 2
                            nc.vector.tensor_tensor(mixedT[0:DIM, at, (ms - 1) * TT:(ms + 1) * TT], psO[0:DIM, 0:2 * TT],
                                                    inv_total[:, :], ALU.mult).then_inc(did["mixedT"], 1)

                run_groups(dve, groups, body)

            @block.gpsimd
            def _(pool):
                def body(g, r):
                    turn, make, out1, out2, mlp, fin = g + 2, g + 1, g - 1, g - 2, g - 3, g - 4

                    def spread_keys(*pairs):
                        if exists(make, groups):
                            pool.wait_ge(did["k_hat"], upto(make))
                            pool.wait_ge(did[f"scored{SB - 1}"], upto(g - 1, PAIRS - 1, PAIRS))
                            for p in pairs:
                                for w in (2 * p, 2 * p + 1):
                                    last = nc.gpsimd.tensor_tensor(
                                        k_heads[0:DIM, (r + 1) % 2, w, :].rearrange("c (j k) -> c j k", j=J),
                                        bcast(k_hat[:, w * WIN:(w + 1) * WIN], 1, J),
                                        bcast(head_mask[:, :], 2, WIN), ALU.mult)
                                last.then_inc(did["k_heads"], 1)

                    for slot in range(PAIRS):
                        if cosine and exists(g, groups):
                            half = slot % 2
                            pool.wait_ge(did["top"], upto(g, slot, PAIRS))
                            view = score[0:QT, half, :].rearrange("p (h k) -> p h k", k=WIN)
                            nc.gpsimd.tensor_tensor(view, view, bcast(top[0:QT, half, :], 2, WIN), ALU.subtract)\
                                .then_inc(did["shifted"], 1)
                        if slot == 0 and not cosine and exists(turn, groups):
                            pool.wait_ge(did["moments"], upto(turn))
                            pool.wait_ge(did["x_turned"], upto(make))
                            nc.gpsimd.tensor_tensor(x_norm[:, :, :], x_in[:, r % 2], bcast(moments[:, :, 0], 2, DIM),
                                                    ALU.subtract).then_inc(did["x_centred"], 1)
                            pool.wait_ge(did["x_centred"], upto(turn))
                            pool.wait_ge(did["rstd"], upto(turn))
                            nc.gpsimd.tensor_tensor(x_norm[:, :, :], x_norm[:, :, :], bcast(rstd[:, :], 2, DIM),
                                                    ALU.mult).then_inc(did["x_norm"], 1)
                        if slot == 0 and exists(make, groups):
                            pool.wait_ge(s_load[(r + 1) % 2], moved(make, (r + 1) % 2))
                            pool.wait_ge(did["x1"], upto(mlp))
                            nc.gpsimd.tensor_tensor(x_res[:, (r + 1) % 4], x_in[:, (r + 1) % 2],
                                                    bcast(res_row1[0:TT, :], 1, PAIRS), ALU.add).then_inc(did["x_res"], 1)
                        if slot == 0 and cosine and exists(g - 5, groups):
                            pool.wait_ge(did["z_ln"], upto(g - 5))
                            pool.wait_ge(did["x1_res"], upto(g - 5))
                            pool.wait_ge(s_store[(r + 1) % 2], moved(g - 7, (r + 1) % 2))
                            nc.gpsimd.tensor_tensor(x2[:, (r + 1) % 2], z_ln[:, :, :], x1_res[:, (r + 3) % 4], ALU.add)\
                                .then_inc(did["x2"], 1)
                        if slot == 1 and cosine:
                            spread_keys(0, 1)
                        if slot == 1 and exists(out2, groups):
                            if cosine:
                                pool.wait_ge(did["y_var"], upto(out2))
                                pool.wait_ge(did["y_rstd"], upto(mlp))
                                nc.gpsimd.tensor_tensor(y_eps[:, :], y_var[:, :], epsilon[:, :], ALU.add)\
                                    .then_inc(did["y_eps"], 1)
                                pool.wait_ge(did["y_eps"], upto(out2))
                                pool.wait_ge(did["y_ln"], upto(mlp))
                                nc.gpsimd.tensor_tensor(y_rstd[:, :], y_eps[:, :], half_power[:, :], ALU.pow)\
                                    .then_inc(did["y_rstd"], 1)
                            else:
                                pool.wait_ge(did["moments2"], upto(out2))
                                pool.wait_ge(did["rstd2"], upto(mlp))
                                nc.gpsimd.tensor_tensor(var_eps2[:, :], moments2[:, :, 1], epsilon[:, :], ALU.add)\
                                    .then_inc(did["var_eps2"], 1)
                                pool.wait_ge(did["var_eps2"], upto(out2))
                                pool.wait_ge(did["x1_norm"], upto(mlp))
                                nc.gpsimd.tensor_tensor(rstd2[:, :], var_eps2[:, :], half_power[:, :], ALU.pow)\
                                    .then_inc(did["rstd2"], 1)
                                pool.wait_ge(did["x2"], upto(g - 6))
                                pool.wait_ge(did["x1"], upto(out2))
                                nc.gpsimd.tensor_tensor(x1_res[:, (r + 2) % 4], x1[:, :, :],
                                                        bcast(row_fc2[0:TT, :], 1, PAIRS), ALU.add).then_inc(did["x1_res"], 1)
                        if slot == 1 and cosine:
                            spread_keys(2, 3)
                        if slot == 2 and cosine and exists(out2, groups):
                            pool.wait_ge(did["y_ln"], upto(out2))
                            pool.wait_ge(did["x1_turned"], upto(mlp))
                            pool.wait_ge(did["x1_res"], upto(mlp))
                            pool.wait_ge(did["x_res"], upto(out2))
                            nc.gpsimd.tensor_tensor(x1[:, :, :], y_ln[:, :, :], x_res[:, (r + 2) % 4], ALU.add)\
                                .then_inc(did["x1"], 1)
                        if slot == 2 and cosine:
                            if exists(fin, groups):
                                pool.wait_ge(did["z_var"], upto(fin))
                                pool.wait_ge(did["z_rstd"], upto(g - 5))
                                nc.gpsimd.tensor_tensor(z_eps[:, :], z_var[:, :], epsilon[:, :], ALU.add)\
                                    .then_inc(did["z_eps"], 1)
                                pool.wait_ge(did["z_eps"], upto(fin))
                                pool.wait_ge(did["z_ln"], upto(g - 5))
                                nc.gpsimd.tensor_tensor(z_rstd[:, :], z_eps[:, :], half_power[:, :], ALU.pow)\
                                    .then_inc(did["z_rstd"], 1)
                        if slot == 3 and not cosine:
                            spread_keys(0, 1, 2, 3)
                        if slot == 3 and cosine and exists(out2, groups):
                            pool.wait_ge(did["x2"], upto(g - 6))
                            pool.wait_ge(did["x1"], upto(out2))
                            nc.gpsimd.tensor_tensor(x1_res[:, (r + 2) % 4], x1[:, :, :],
                                                    bcast(res_row2[0:TT, :], 1, PAIRS), ALU.add).then_inc(did["x1_res"], 1)
                        if slot == 3 and not cosine and exists(g + 3, groups):
                            pool.wait_ge(did["moments"], upto(g + 3))
                            pool.wait_ge(did["rstd"], upto(turn))
                            nc.gpsimd.tensor_tensor(var_eps[:, :], moments[:, :, 1], epsilon[:, :], ALU.add)\
                                .then_inc(did["var_eps"], 1)
                            pool.wait_ge(did["var_eps"], upto(g + 3))
                            pool.wait_ge(did["x_norm"], upto(turn))
                            nc.gpsimd.tensor_tensor(rstd[:, :], var_eps[:, :], half_power[:, :], ALU.pow)\
                                .then_inc(did["rstd"], 1)

                run_groups(pool, groups, body)


def two_blocks(nc, x, out, params, const):
    scratch = nc.dram_tensor("between_blocks", [IMAGES, SIDE, SIDE, DIM], F32, kind="Internal").ap()
    with ExitStack() as ctx:
        def pb(name, shape):
            return ctx.enter_context(nc.psum_tensor(name, shape, F32))

        psum = {"scores": pb("ps_scores", [128, 2, BANK]), "probs": pb("ps_probs", [128, 2, BANK]),
                "turn": pb("ps_turn", [128, BANK]), "dense": pb("ps_dense", [128, 2, BANK]),
                "mixed": pb("ps_mixed", [128, BANK])}
        block_program(nc, Swin, x, scratch, params["L0"], const, psum)
        block_program(nc, Plain, scratch, out, params["L1"], const, psum)


def shape_constants():
    def token(order, n):
        if order == 0:
            return n % 7, n // 7
        return (n % 4, n // 4) if n < 28 else (4 + (n - 28) % 3, (n - 28) // 3)

    c = {"ident": np.eye(128, dtype=np.float32)}
    f = np.arange(DIM)
    c["same_head"] = (f[:, None] // 8 == f[None, :] // 8).astype(np.float32)
    c["pick"] = (np.arange(12)[:, None] == f[None, :] // 8).astype(np.float32)
    c["swin_head_mask"] = (f[:, None] % 32 // 8 == np.arange(4)[None, :]).astype(np.float32)
    c["plain_head_mask"] = (f[:, None] % 32 // 16 == np.arange(2)[None, :]).astype(np.float32)
    key_head = np.arange(128)[:, None, None] // HALF
    for name, size in (("swin", 8), ("plain", 16)):
        n_in_band = 16 // size
        col = np.arange(32)[None, None, :] // size
        c[f"{name}_sum_heads"] = (col == 2 * np.arange(n_in_band)[None, :, None] + key_head).astype(np.float32)
    rel = np.zeros((2, 2, 49, 49), np.float32)
    mask = np.zeros((128, 2, 2, 49), np.float32)
    region = np.zeros((SIDE, SIDE))
    n = 0
    for hs in (slice(0, -7), slice(-7, -3), slice(-3, None)):
        for ws in (slice(0, -7), slice(-7, -3), slice(-3, None)):
            region[hs, ws] = n
            n += 1
    for order in range(2):
        at = np.array([token(order, n) for n in range(49)])
        d = (at[:, None, :] - at[None, :, :]).astype(np.float32)
        rel[:, order] = np.moveaxis(np.sign(d) * np.log1p(np.abs(d)), 2, 0)
        wy = 7 if order else 0
        for edge in range(2):
            for half in range(2):
                wx = 6 * edge + half
                r = region[wy * 7 + at[:, 0], wx * 7 + at[:, 1]]
                mask[half * HALF:half * HALF + 49, order, edge] = np.where(r[:, None] != r[None, :], -100.0, 0.0)
    c["rel"] = rel.reshape(2, 2, 49 * 49)
    c["mask"] = mask
    return c


_L0 = ["qkv_w", "qkv_b", "proj_w", "proj_b", "tau", "meta_w1", "meta_b1", "meta_w2", "meta_b2", "norm1_g", "norm1_b",
       "fc1_w", "fc1_b", "fc2_w", "fc2_b", "norm2_g", "norm2_b"]
_L1 = {"g1": "g1", "b1": "b1", "w_qkv": "qkv_w", "b_qkv": "qkv_b", "w_proj": "proj_w", "b_proj": "proj_b", "g2": "g2",
       "b2": "b2", "w_fc1": "fc1_w", "b_fc1": "fc1_b", "w_fc2": "fc2_w", "b_fc2": "fc2_b"}


def kernel(**inputs):
    import numpy as _np
    import concourse.bacc as _bacc
    from concourse import mybir as _mybir
    from concourse.bass_utils import run_bass_kernel_spmd as _run

    nc = _bacc.Bacc("TRN2", target_bir_lowering=False, num_devices=1)
    arrays = {}

    def give(name, a):
        a = _np.ascontiguousarray(a)
        arrays[f"in_{name}"] = a
        return nc.dram_tensor(f"in_{name}", a.shape, _mybir.dt.from_np(a.dtype), kind="ExternalInput").ap()

    x = give("x", inputs["x"])
    params = {"L0": {k: give(f"L0_{k}", inputs[f"L0_conv_{k}"]) for k in _L0},
              "L1": {v: give(f"L1_{k}", inputs[f"L1_conv_{k}"]) for k, v in _L1.items()}}
    const = {k: give(f"const_{k}", v) for k, v in shape_constants().items()}
    out = nc.dram_tensor("out_0_dram", (IMAGES, SIDE, SIDE, DIM), _mybir.dt.float32, kind="ExternalOutput").ap()
    two_blocks(nc, x, out, params, const)
    r = _run(nc, [arrays], core_ids=[0])
    return r.results[0]["out_0_dram"]
```
